# Optimizing a Trainium2 kernel written in Bass

```python
import numpy as np
import jax
import jax.numpy as jnp

def _softmax(x, axis=-1):
    return jax.nn.softmax(x, axis=axis)

def _gelu(x):
    return jax.nn.gelu(x, approximate=True)

def _silu(x):
    return jax.nn.silu(x)

def _sigmoid(x):
    return jax.nn.sigmoid(x)

def _layernorm(x, axis=-1, eps=1e-05):
    m = jnp.mean(x, axis=axis, keepdims=True)
    v = jnp.var(x, axis=axis, keepdims=True)
    return (x - m) / jnp.sqrt(v + eps)

def _scatter_add(tgt, idx, src, axis=0):
    return tgt.at[idx].add(src)

def _segment_sum(src, seg, n):
    return jax.ops.segment_sum(src, seg, n)
kernel_name = 'mk_cond_seq_d2_seqx_r4_9466c5'

def setup_inputs(seed: int=0):
    np.random.seed(seed)
    _w = jnp.asarray

    def _rec_inputs():
        import jax
        import jax.numpy as jnp
        _rk = jax.random.key(seed)
        x = -0.0002928 + 1 * jax.random.normal(jax.random.fold_in(_rk, 1), (128, 64, 256), jnp.float32)
        _lenS = 64 - jax.random.randint(jax.random.fold_in(_rk, 7), (128,), 0, max(1, 64 // 4) + 1, jnp.int32)
        _lenS2 = 64 - jax.random.randint(jax.random.fold_in(_rk, 8), (128,), 0, max(1, 64 // 4) + 1, jnp.int32)
        cond_1024 = 0.000887014 + 1.03683 * jax.random.normal(jax.random.fold_in(_rk, 11), (128, 256), jnp.float32)
        pos_S = jnp.arange(64, dtype=jnp.int32)
        _validS = jnp.arange(64)[None, :] < _lenS[:, None]
        _validS2 = jnp.arange(64)[None, :] < _lenS2[:, None]
        _causal = jnp.tril(jnp.ones((64, 64), dtype=bool))
        mask_BxSxSx11_ik0 = jnp.where(jnp.ones((128, 64, 64, 11), dtype=bool), 0, 1).astype(jnp.int32)
        return (x, cond_1024, pos_S, mask_BxSxSx11_ik0)
    x, cond_1024, pos_S, mask_BxSxSx11_ik0 = _rec_inputs()

    def _L0_cond_setup():
        import jax, jax.numpy as jnp
        import numpy as np
        EPS = 1e-06
        NUM_HEADS = 16

        def _rms(x, w=None):
            y = x * jax.lax.rsqrt(jnp.mean(x * x, axis=-1, keepdims=True) + EPS)
            return y if w is None else y * w

        def _rope(q, k, pos):
            dh = q.shape[-1]
            half = dh // 2
            freqs = 1.0 / 10000.0 ** (jnp.arange(half, dtype=jnp.float32) / half)
            ang = pos.astype(jnp.float32)[:, None] * freqs[None, :]
            cos = jnp.concatenate([jnp.cos(ang), jnp.cos(ang)], -1)
            sin = jnp.concatenate([jnp.sin(ang), jnp.sin(ang)], -1)

            def rot(v):
                v1, v2 = jnp.split(v, 2, axis=-1)
                return jnp.concatenate([-v2, v1], -1)
            return (q * cos + rot(q) * sin, k * cos + rot(k) * sin)
        key = jax.random.key(seed)
        ks = jax.random.split(key, 12)
        B, T, D, H = (2, 512, 256, NUM_HEADS)
        Dh = D // H
        Hm = 704
        s = lambda fan_in: 1.0 / np.sqrt(fan_in)
        return {'x': jax.random.normal(ks[0], (B, T, D), jnp.float32), 'c': jax.random.normal(ks[1], (B, D), jnp.float32), 'pos': jnp.arange(T, dtype=jnp.int32), 'adaln_w': jax.random.normal(ks[2], (D, 6 * D), jnp.float32) * s(D) * 0.1, 'adaln_b': jax.random.normal(ks[3], (6 * D,), jnp.float32) * 0.02, 'qkv_w': jax.random.normal(ks[4], (D, 3 * D), jnp.float32) * s(D), 'lnq_w': jnp.ones((Dh,), jnp.float32), 'lnk_w': jnp.ones((Dh,), jnp.float32), 'proj_w': jax.random.normal(ks[5], (D, D), jnp.float32) * s(D), 'proj_b': jnp.zeros((D,), jnp.float32), 'w1_w': jax.random.normal(ks[6], (D, Hm), jnp.float32) * s(D), 'w3_w': jax.random.normal(ks[7], (D, Hm), jnp.float32) * s(D), 'w2_w': jax.random.normal(ks[8], (Hm, D), jnp.float32) * s(Hm)}
    _L0_cond_all = _L0_cond_setup()
    _L0_cond_in = {k: v for k, v in _L0_cond_all.items() if k in ('adaln_w', 'adaln_b', 'qkv_w', 'lnq_w', 'lnk_w', 'proj_w', 'proj_b', 'w1_w', 'w3_w', 'w2_w')}
    del _L0_cond_all

    def _L1_cond_setup():
        import jax, jax.numpy as jnp
        import numpy as np
        NONGT = 20
        H = 16
        NEG = -9000000000000000.0

        def _gat_attention(self_feat, cond_adj, label_bias, Wq, bq, Wk, bk, Wout, bout):
            B, N, F = self_feat.shape
            ng = min(NONGT, N)
            dh = F // H
            kv = self_feat[:, :ng]
            qh = (self_feat @ Wq.T + bq).reshape(B, N, H, dh)
            kh = (kv @ Wk.T + bk).reshape(B, ng, H, dh)
            aff = jnp.einsum('bnhd,bmhd->bnhm', qh, kh) * (1.0 / np.sqrt(dh))
            mask = cond_adj[:, :, None, :] > 0
            aff = jnp.where(mask, aff, NEG) + label_bias[:, :, None, :]
            w = jax.nn.softmax(aff, axis=-1)
            out_t = jnp.einsum('bnhm,bmf->bnhf', w, kv)
            out = jnp.einsum('bnhf,hgf->bnhg', out_t, Wout) + bout.reshape(H, F // H)
            return out.reshape(B, N, F)

        def _forward(v, q, adj, W_self, b_self, w_bias, b_bias, Wq, bq, Wk, bk, Wout, bout):
            adj_f = adj.astype(jnp.float32)
            exp_v = v
            row_zero = exp_v.sum(-1) == 0
            q_exp = jnp.where(row_zero[..., None], 0.0, q[:, None, :])
            vcq = jnp.concatenate([exp_v, q_exp], axis=-1)
            self_feat = vcq @ W_self.T + b_self
            output = self_feat
            for d in range(2):
                A = adj_f if d == 0 else jnp.swapaxes(adj_f, 1, 2)
                A = A[:, :, :NONGT, :]
                cond = A.sum(-1)
                vb = A @ w_bias + b_bias
                output = output + _gat_attention(self_feat, cond, vb, Wq[d], bq[d], Wk[d], bk[d], Wout[d], bout[d])
            rel = jax.nn.relu(output)
            return exp_v + rel
        key = jax.random.key(seed)
        ks = jax.random.split(key, 8)
        B, N, L, F, Q = (64, 36, 11, 256, 256)
        IN = F + Q
        s = 0.02
        return {'v': jax.random.normal(ks[0], (B, N, F), jnp.float32), 'q': jax.random.normal(ks[1], (B, Q), jnp.float32), 'adj': jax.random.randint(ks[2], (B, N, N, L), 0, 2, jnp.int32), 'W_self': jax.random.normal(ks[3], (F, IN), jnp.float32) * s, 'b_self': jnp.zeros((F,), jnp.float32), 'w_bias': jax.random.normal(ks[4], (L,), jnp.float32) * s, 'b_bias': jnp.zeros((), jnp.float32), 'Wq': jax.random.normal(ks[5], (2, F, F), jnp.float32) * s, 'bq': jnp.zeros((2, F), jnp.float32), 'Wk': jax.random.normal(ks[6], (2, F, F), jnp.float32) * s, 'bk': jnp.zeros((2, F), jnp.float32), 'Wout': jax.random.normal(ks[7], (2, H, F // H, F), jnp.float32) * s, 'bout': jnp.zeros((2, F), jnp.float32)}
    _L1_cond_all = _L1_cond_setup()
    _L1_cond_in = {k: v for k, v in _L1_cond_all.items() if k in ('W_self', 'b_self', 'w_bias', 'b_bias', 'Wq', 'bq', 'Wk', 'bk', 'Wout', 'bout')}
    del _L1_cond_all
    return {'x': x, 'cond_1024': cond_1024, 'pos_S': pos_S, 'mask_BxSxSx11_ik0': mask_BxSxSx11_ik0, 'L0_cond_adaln_w': _L0_cond_in['adaln_w'], 'L0_cond_adaln_b': _L0_cond_in['adaln_b'], 'L0_cond_qkv_w': _L0_cond_in['qkv_w'], 'L0_cond_lnq_w': _L0_cond_in['lnq_w'], 'L0_cond_lnk_w': _L0_cond_in['lnk_w'], 'L0_cond_proj_w': _L0_cond_in['proj_w'], 'L0_cond_proj_b': _L0_cond_in['proj_b'], 'L0_cond_w1_w': _L0_cond_in['w1_w'], 'L0_cond_w3_w': _L0_cond_in['w3_w'], 'L0_cond_w2_w': _L0_cond_in['w2_w'], 'L1_cond_W_self': _L1_cond_in['W_self'], 'L1_cond_b_self': _L1_cond_in['b_self'], 'L1_cond_w_bias': _L1_cond_in['w_bias'], 'L1_cond_b_bias': _L1_cond_in['b_bias'], 'L1_cond_Wq': _L1_cond_in['Wq'], 'L1_cond_bq': _L1_cond_in['bq'], 'L1_cond_Wk': _L1_cond_in['Wk'], 'L1_cond_bk': _L1_cond_in['bk'], 'L1_cond_Wout': _L1_cond_in['Wout'], 'L1_cond_bout': _L1_cond_in['bout']}

def reference(x, cond_1024, pos_S, mask_BxSxSx11_ik0, L0_cond_adaln_w, L0_cond_adaln_b, L0_cond_qkv_w, L0_cond_lnq_w, L0_cond_lnk_w, L0_cond_proj_w, L0_cond_proj_b, L0_cond_w1_w, L0_cond_w3_w, L0_cond_w2_w, L1_cond_W_self, L1_cond_b_self, L1_cond_w_bias, L1_cond_b_bias, L1_cond_Wq, L1_cond_bq, L1_cond_Wk, L1_cond_bk, L1_cond_Wout, L1_cond_bout):
    import jax
    import jax.numpy as jnp

    def _L0_cond_ref(x, c, pos, adaln_w, adaln_b, qkv_w, lnq_w, lnk_w, proj_w, proj_b, w1_w, w3_w, w2_w):
        import jax, jax.numpy as jnp
        import numpy as np
        EPS = 1e-06
        NUM_HEADS = 16

        def _rms(x, w=None):
            y = x * jax.lax.rsqrt(jnp.mean(x * x, axis=-1, keepdims=True) + EPS)
            return y if w is None else y * w

        def _rope(q, k, pos):
            dh = q.shape[-1]
            half = dh // 2
            freqs = 1.0 / 10000.0 ** (jnp.arange(half, dtype=jnp.float32) / half)
            ang = pos.astype(jnp.float32)[:, None] * freqs[None, :]
            cos = jnp.concatenate([jnp.cos(ang), jnp.cos(ang)], -1)
            sin = jnp.concatenate([jnp.sin(ang), jnp.sin(ang)], -1)

            def rot(v):
                v1, v2 = jnp.split(v, 2, axis=-1)
                return jnp.concatenate([-v2, v1], -1)
            return (q * cos + rot(q) * sin, k * cos + rot(k) * sin)
        B, T, D = x.shape
        H = NUM_HEADS
        Dh = D // H
        mods = jax.nn.silu(c) @ adaln_w + adaln_b
        shift_msa, scale_msa, gate_msa, shift_mlp, scale_mlp, gate_mlp = jnp.split(mods, 6, axis=-1)
        x_mod = _rms(x) * (1.0 + scale_msa[:, None, :]) + shift_msa[:, None, :]
        qkv = x_mod @ qkv_w
        q, k, v = jnp.split(qkv, 3, axis=-1)
        q = q.reshape(B, T, H, Dh).transpose(0, 2, 1, 3)
        k = k.reshape(B, T, H, Dh).transpose(0, 2, 1, 3)
        v = v.reshape(B, T, H, Dh).transpose(0, 2, 1, 3)
        q = _rms(q, lnq_w)
        k = _rms(k, lnk_w)
        q, k = _rope(q, k, pos)
        scores = jnp.einsum('bhqd,bhkd->bhqk', q, k) / jnp.sqrt(jnp.float32(Dh))
        attn = jax.nn.softmax(scores, axis=-1)
        attn_out = jnp.einsum('bhqk,bhkd->bhqd', attn, v)
        attn_out = attn_out.transpose(0, 2, 1, 3).reshape(B, T, D)
        x = x + gate_msa[:, None, :] * (attn_out @ proj_w + proj_b)
        h = _rms(x) * (1.0 + scale_mlp[:, None, :]) + shift_mlp[:, None, :]
        mlp = jax.nn.silu(h @ w1_w) * (h @ w3_w) @ w2_w
        x = x + gate_mlp[:, None, :] * mlp
        return x

    def _L1_cond_ref(v, q, adj, W_self, b_self, w_bias, b_bias, Wq, bq, Wk, bk, Wout, bout):
        import jax, jax.numpy as jnp
        import numpy as np
        NONGT = 20
        H = 16
        NEG = -9000000000000000.0

        def _gat_attention(self_feat, cond_adj, label_bias, Wq, bq, Wk, bk, Wout, bout):
            B, N, F = self_feat.shape
            ng = min(NONGT, N)
            dh = F // H
            kv = self_feat[:, :ng]
            qh = (self_feat @ Wq.T + bq).reshape(B, N, H, dh)
            kh = (kv @ Wk.T + bk).reshape(B, ng, H, dh)
            aff = jnp.einsum('bnhd,bmhd->bnhm', qh, kh) * (1.0 / np.sqrt(dh))
            mask = cond_adj[:, :, None, :] > 0
            aff = jnp.where(mask, aff, NEG) + label_bias[:, :, None, :]
            w = jax.nn.softmax(aff, axis=-1)
            out_t = jnp.einsum('bnhm,bmf->bnhf', w, kv)
            out = jnp.einsum('bnhf,hgf->bnhg', out_t, Wout) + bout.reshape(H, F // H)
            return out.reshape(B, N, F)

        def _forward(v, q, adj, W_self, b_self, w_bias, b_bias, Wq, bq, Wk, bk, Wout, bout):
            adj_f = adj.astype(jnp.float32)
            exp_v = v
            row_zero = exp_v.sum(-1) == 0
            q_exp = jnp.where(row_zero[..., None], 0.0, q[:, None, :])
            vcq = jnp.concatenate([exp_v, q_exp], axis=-1)
            self_feat = vcq @ W_self.T + b_self
            output = self_feat
            for d in range(2):
                A = adj_f if d == 0 else jnp.swapaxes(adj_f, 1, 2)
                A = A[:, :, :NONGT, :]
                cond = A.sum(-1)
                vb = A @ w_bias + b_bias
                output = output + _gat_attention(self_feat, cond, vb, Wq[d], bq[d], Wk[d], bk[d], Wout[d], bout[d])
            rel = jax.nn.relu(output)
            return exp_v + rel
        return _forward(v, q, adj, W_self, b_self, w_bias, b_bias, Wq, bq, Wk, bk, Wout, bout)
    x = _L0_cond_ref(x, cond_1024, pos_S, L0_cond_adaln_w, L0_cond_adaln_b, L0_cond_qkv_w, L0_cond_lnq_w, L0_cond_lnk_w, L0_cond_proj_w, L0_cond_proj_b, L0_cond_w1_w, L0_cond_w3_w, L0_cond_w2_w)
    x = _L1_cond_ref(x, cond_1024, mask_BxSxSx11_ik0, L1_cond_W_self, L1_cond_b_self, L1_cond_w_bias, L1_cond_b_bias, L1_cond_Wq, L1_cond_bq, L1_cond_Wk, L1_cond_bk, L1_cond_Wout, L1_cond_bout)
    return x

_drawn_inputs = setup_inputs


def setup_inputs(seed=0):
    import zlib

    import numpy as np

    out = dict(_drawn_inputs(seed))
    spreads = {'L0_cond_lnq_w': (1.0, 0.6),
     'L0_cond_lnk_w': (1.0, 0.6),
     'L0_cond_proj_b': (0.0, 0.8),
     'L1_cond_b_self': (0.0, 0.1),
     'L1_cond_bq': (0.0, 0.1),
     'L1_cond_bk': (0.0, 0.1),
     'L1_cond_bout': (0.0, 0.1)}
    factors = {'L0_cond_adaln_b': 4.671, 'L0_cond_qkv_w': 4.12, 'L0_cond_proj_w': 4.15}
    for name, (base, spread) in spreads.items():
        noise = np.random.default_rng([zlib.crc32(name.encode()), seed]).standard_normal(out[name].shape)
        drawn = base * np.exp(spread * noise) if base else spread * noise
        out[name] = jnp.asarray(drawn.astype(out[name].dtype))
    for name, factor in factors.items():
        out[name] = (out[name] * factor).astype(out[name].dtype)
    return out
```

```python
from contextlib import ExitStack

import concourse.bass as bass
from concourse import mybir

F32 = mybir.dt.float32
F32R = mybir.dt.float32r
I32 = mybir.dt.int32
ALU = mybir.AluOpType
ACT = mybir.ActivationFunctionType
AX = mybir.AxisListType

P = 128
B, S, D = 128, 64, 256
H, DH = 16, 16
HM = 704
NKV = 20
NKP = 32
NL = 11
EPS = 1e-6
NEG = -9000000000000000.0
DC = D // P
MC = -(-HM // P)
MB = 4
MT = MB * S
TILES = MT // P
NM = B // MB
NJ = H // 2
NG = H // 4
ND = 2
NE = ND * NKV
NMOD = 6 * DC
SHIFT_A, SCALE_A, GATE_A, SHIFT_M, SCALE_M, GATE_M = range(0, NMOD, DC)
COND = NMOD
TWO_PI_PARTS = (6.28125, 0.0019350051879882812, 3.019916e-7)
WEIGHTS = {"qkv": (DC, 3 * D), "proj": (DC, D), "w1": (DC, MC * P), "w3": (DC, MC * P), "w2": (MC, D),
           "self": (DC, D), "q1": (DC, ND * D)}
WEIGHT_SCALE = {"w2": 0.5}

ORDER = [
    (1, "norm", 0), (0, "norm", 0), (1, "mlp_up", 0), (0, "qkv", 0), (0, "qkv", 1), (0, "rope_scale", 0),
    (0, "rope", 0), (1, "mlp_up", 1), (0, "heads", 0), (0, "rope", 1), (0, "score", 0), (1, "mlp_up", 2),
    (0, "heads", 1), (1, "edges", 0), (0, "score", 1), (1, "mlp_down", 0), (0, "probsT", 0), (0, "mix", 0),
    (1, "self", 0), (0, "probsT", 1), (0, "mix", 1), (1, "k1", 0), (1, "q1", 0), (0, "proj", 0),
    (1, "score1", 0), (1, "v1", 0), (1, "probsT1", 0), (1, "mix1", 0), (1, "score1", 1),
    (1, "probsT1", 1), (1, "mix1", 1), (1, "out", 0),
]
L0_ORDER = [step for step in ORDER if step[0] == 0]
L1_ORDER = [step for step in ORDER if step[0] == 1]


class Signal:

    def __init__(self, sem, per):
        self.sem, self.per = sem, per


def wait(engine, signal, m, n):
    value = m * signal.per + n
    if not isinstance(value, int) or value > 0:
        engine.wait_ge(signal.sem, value)


def wait_last(engine, signal, m):
    wait(engine, signal, m, 0)


def run_streams(engine, steps):
    def take(order, m0, m1):
        for stream, name, n in order:
            if (stream, name) in steps:
                steps[stream, name](m0 if stream == 0 else m1, n)

    take(L0_ORDER, 0, None)
    take(ORDER, 1, 0)
    with engine.Fori(1, NM - 1) as m:
        take(ORDER, m + 1, m)
    take(L1_ORDER, None, NM - 1)


def build_program(nc, d):
    with ExitStack() as ctx:
        def sb(name, shape, dt=F32):
            return ctx.enter_context(nc.sbuf_tensor(name, shape, dt))

        def signal(name, per=1):
            return Signal(ctx.enter_context(nc.semaphore(name)), per)

        ident = sb("ident", [P, P])
        mean_col = sb("mean_col", [P, 1])
        ones_r = sb("ones_r", [P, P], F32R)
        ones_f = sb("ones_f", [P, 56])
        hmask4 = sb("hmask4", [P, 4])
        hmask8 = sb("hmask8", [P, 8])
        seq_ind = sb("seq_ind", [P, 2])
        eps = sb("eps", [P, 1])
        wh = {k: sb(f"{k}_hi", [P, *s], F32R) for k, s in WEIGHTS.items()}
        wl = {k: sb(f"{k}_lo", [P, *s], F32R) for k, s in WEIGHTS.items()}
        wk1 = sb("wk1", [P, DC, ND * D])
        wo1 = sb("wo1", [P, DC, ND * D])
        mods = sb("mods", [P, NMOD + DC, B])
        colb = sb("colb", [P, NMOD + 2 * DC + 3 * ND * DC])
        adaln_b, proj_b = colb[:, 0:NMOD], colb[:, NMOD:NMOD + DC]
        self_b = colb[:, NMOD + DC:NMOD + 2 * DC]
        bq, bk, bo = (colb[:, NMOD + 2 * DC + i * ND * DC:NMOD + 2 * DC + (i + 1) * ND * DC] for i in range(3))
        bq4 = sb("bq4", [P, ND * DC])
        bout = sb("bout", [P, DC])
        lnw = sb("lnw", [P, 2, DH])
        edge_w = sb("edge_w", [P, NL])
        edge_b = sb("edge_b", [P, 1])
        pos_i = sb("pos_i", [P, 1], I32)
        pos_f = sb("pos_f", [P, 1])
        freq = sb("freq", [P, DH // 2])
        ang = sb("ang", [P, 2, DH // 2])
        turns_i = sb("turns_i", [P, 2, DH // 2], I32)
        turns = sb("turns", [P, 2, DH // 2])
        cosw = sb("cosw", [P, 2, DH])
        sinw = sb("sinw", [P, 2, DH])

        xn = [sb(f"xn{i}", [P, DC, MT]) for i in range(2)]
        rms_root = [sb(f"rms_root{i}", [P, TILES]) for i in range(2)]
        rms_inv = [sb(f"rms_inv{i}", [P, TILES]) for i in range(2)]
        mod = [sb(f"mod{i}", [P, NMOD + DC, MB]) for i in range(2)]
        nh = [sb(f"nh{i}", [P, DC, MT], F32R) for i in range(2)]
        nl = [sb(f"nl{i}", [P, DC, MT], F32R) for i in range(2)]

        x_in = sb("x_in", [P, DC, MT])
        x_res = sb("x_res", [P, DC, MT])
        x1 = sb("x1", [P, DC, MT])
        qk = sb("qk", [P, TILES, 2, H, DH])
        qk_sq = sb("qk_sq", [P, 2, H, DH])
        qk_ss = sb("qk_ss", [P, TILES, 2 * H])
        qk_root = sb("qk_root", [P, TILES, 2 * H])
        qk_inv = sb("qk_inv", [P, TILES, 2 * H])
        q_inv = sb("q_inv", [P, 2, TILES, H])
        qc = sb("qc", [P, 2, H, DH])
        qs = sb("qs", [P, 2, H, DH])
        qr = qk_sq
        qd = sb("qd", [P, NG, 2, 4 * DH])
        kd = sb("kd", [P, NG, 2, 4 * DH])
        vb = sb("vb", [P, TILES, NJ, 2, 2, DH])
        qT = [sb(f"qT{i}", [P, NG, P]) for i in range(TILES)]
        kT = sb("kT", [P, NG, S])
        kbd = sb("kbd", [P, TILES, NG, 4, S])
        mx0 = sb("mx0", [P, H])
        e0 = [sb(f"e0_{i}", [P, H, S]) for i in range(TILES)]
        sum0 = sb("sum0", [P, H])
        inv0 = [sb(f"inv0_{i}", [P, H]) for i in range(TILES)]
        pT0 = sb("pT0", [P, NJ, P])
        aoh = sb("aoh", [P, DC, MT], F32R)
        aol = sb("aol", [P, DC, MT], F32R)

        th = sb("th", [P, 2, MT])
        gf = sb("gf", [P, 2, MT])
        gh = sb("gh", [P, MC, MT], F32R)
        gl = sb("gl", [P, MC, MT], F32R)
        x2 = sb("x2", [P, DC, MT])
        sf = sb("sf", [P, DC, MT])
        gate = sb("gate", [P, MT])
        kv = sb("kv", [P, DC, MB, NKP])
        q1T = sb("q1T", [P, ND, DC, MT])
        k1T = sb("k1T", [P, ND, DC, MB, NKP])
        kbd1 = sb("kbd1", [P, ND * DC, MB, 8, NKV])
        vb1 = sb("vb1", [P, MB, NJ, 2, DH])
        adj = sb("adj", [P, TILES, NE, NL], I32)
        adw = q1T[:, :, :, :].rearrange("p a c t -> p (a c t)")[:, 0:TILES * NE * NL].rearrange("p (e l) -> p e l", l=NL)
        edge_n = sb("edge_n", [P, TILES, NE])
        edge_v = sb("edge_v", [P, TILES, NE])
        edge_bias = sb("edge_bias", [P, TILES, NE])
        e1 = sb("e1", [P, ND, H, NKV])
        mx1 = sb("mx1", [P, ND, H])
        sum1 = sb("sum1", [P, ND, H])
        inv1 = sb("inv1", [P, ND, H])
        p1 = sb("p1", [P, NJ, ND, 2, NKP])
        pT1 = sb("pT1", [P, NJ, P])
        stage = [kbd1[:, :, :, :, :].rearrange("p a b c d -> p (a b c d)")[:, 0:DC * 3 * D],
                 kbd[:, :, :, :, :].rearrange("p a b c d -> p (a b c d)")[:, 0:DC * 3 * D]]

        cond, cond_t = (v.rearrange("p (c b) -> p c b", b=B) for v in (th[:, 0, :], th[:, 1, :]))
        cond_s = gf[:, 0, :].rearrange("p (c b) -> p c b", b=B)

        lin = [ctx.enter_context(nc.psum_tensor(f"lin{i}", [P, 2, MT], F32)) for i in range(2)]
        s0_ps = ctx.enter_context(nc.psum_tensor("s0_ps", [P, 2, 2 * MT], F32))
        tr = [ctx.enter_context(nc.psum_tensor(f"tr{i}", [P, 4, P], F32)) for i in range(2)]
        ao_ps = ctx.enter_context(nc.psum_tensor("ao_ps", [P, 2, MT], F32))
        ao1_ps = ctx.enter_context(nc.psum_tensor("ao1_ps", [P, 2, MT], F32))
        s1_ps = [lin[i][:, :, :].rearrange("p a b -> p (a b)") for i in range(2)]
        tr1 = [s.rearrange("p (a b) -> p a b", b=P) for s in s1_ps]
        qkv_ps = [(s0_ps[:, 0, :], s0_ps[:, 1, 0:D]),
                  (tr[0][:, :, :].rearrange("p a b -> p (a b)"),
                   tr[1][:, :, :].rearrange("p a b -> p (a b)")[:, 0:D])]
        ms_ps = [ao_ps[:, 1, 0:TILES], ao1_ps[:, 1, 0:TILES]]
        spread_ps = [tr[1][:, 0:TILES, :].rearrange("p a b -> p (a b)"), lin[1][:, 0, :]]

        consts_in = signal("consts_in")
        stage_in = [signal("stage0_in"), signal("stage1_in")]
        zeros_set = signal("zeros_set")
        weight_hi = signal("weight_hi")
        weight_lo = signal("weight_lo")
        table_step = signal("table_step")
        sines = signal("sines")
        cond_tanh = signal("cond_tanh")
        cond_ready = signal("cond_ready")
        mods_ps = signal("mods_ps")
        mods_set = signal("mods_set")
        biases_set = signal("biases_set")

        x_in_s, x_res_s, adj_s = signal("x_in_s", 16), signal("x_res_s", 16), signal("adj_s", 16)
        out_s = signal("out_s", 16)
        mod_set = [signal("mod_set_L0"), signal("mod_set_L1")]
        squares = [signal("squares_L0"), signal("squares_L1")]
        means = [signal("means_L0"), signal("means_L1")]
        roots = [signal("roots_L0"), signal("roots_L1")]
        inverses = [signal("inverses_L0"), signal("inverses_L1")]
        spread = [signal("spread_L0"), signal("spread_L1")]
        normed = [signal("normed_L0"), signal("normed_L1")]
        scaled = [signal("scaled_L0"), signal("scaled_L1")]
        shifted = [signal("shifted_L0"), signal("shifted_L1")]
        normed_hi = [signal("normed_hi_L0"), signal("normed_hi_L1")]
        normed_lo = [signal("normed_lo_L0"), signal("normed_lo_L1")]
        qkv_done = signal("qkv_done", TILES)
        qk_squares, qk_kept, v_kept = signal("qk_squares", TILES), signal("qk_kept", TILES), signal("v_kept", TILES)
        qk_sums, qk_roots, qk_inverses = signal("qk_sums", TILES), signal("qk_roots"), signal("qk_inverses")
        q_inverses = signal("q_inverses", 2)
        cos_part, sin_part = signal("cos_part", TILES), signal("sin_part", TILES)
        rotated = signal("rotated", 2 * TILES)
        heads_split = signal("heads_split", TILES)
        qT_ps, kT_ps = signal("qT_ps", TILES), signal("kT_ps", TILES)
        qT_kept, kT_kept = signal("qT_kept", TILES), signal("kT_kept", TILES)
        k_spread = signal("k_spread", TILES)
        scores, maxima, shifted_s = signal("scores", TILES), signal("maxima", TILES), signal("shifted_s", TILES)
        exps, exp_sums, inv_sums = signal("exps", TILES), signal("exp_sums", TILES), signal("inv_sums", TILES)
        probs = signal("probs", TILES)
        pT_ps = signal("pT_ps", 2 * TILES)
        pT_a, pT_b = signal("pT_a", TILES), signal("pT_b", TILES)
        mixed, mixed_hi, mixed_lo = signal("mixed", TILES), signal("mixed_hi", TILES), signal("mixed_lo", TILES)
        proj_done, proj_gated, x1_done = signal("proj_done"), signal("proj_gated", DC), signal("x1_done")

        z_done, z_tanh, z_silu = signal("z_done", MC), signal("z_tanh", MC // 2), signal("z_silu", MC // 2)
        g_done, g_hi, g_lo = signal("g_done", MC // 2), signal("g_hi", MC // 2), signal("g_lo", MC // 2)
        down_done, down_gated = signal("down_done"), signal("down_gated")
        x2_done, x2_hi, x2_lo = signal("x2_done"), signal("x2_hi"), signal("x2_lo")
        rowsum, row_gate, cond_part = signal("rowsum"), signal("row_gate"), signal("cond_part")
        self_ps, self_done = signal("self_ps"), signal("self_done", DC)
        self_hi, self_lo = signal("self_hi"), signal("self_lo")
        q1_ps, q1_kept = signal("q1_ps", ND), signal("q1_kept", ND)
        kv_kept = signal("kv_kept")
        k1_ps, k1_kept, k1_spread = signal("k1_ps"), signal("k1_kept"), signal("k1_spread", ND * DC)
        v1_ps, v1_kept = signal("v1_ps"), signal("v1_kept")
        edge_count, edge_weighted, edge_value = signal("edge_count"), signal("edge_weighted"), signal("edge_value")
        edge_masked, edge_ready = signal("edge_masked"), signal("edge_ready")
        scores1, biased1 = signal("scores1", TILES), signal("biased1", TILES)
        maxima1, shifted1, exps1 = signal("maxima1", TILES), signal("shifted1", TILES), signal("exps1", TILES)
        sums1, inverses1, probs1 = signal("sums1", TILES), signal("inverses1", TILES), signal("probs1", TILES)
        pT1_ps, pT1_a, pT1_b = signal("pT1_ps", 2 * TILES), signal("pT1_a", TILES), signal("pT1_b", TILES)
        mixed1, summed1 = signal("mixed1", TILES), signal("summed1", TILES)
        relu_done = signal("relu_done")

        small = [(ident[:, :], d["ident"]), (mean_col[:, :], d["mean_col"]), (hmask4[:, :], d["hmask4"]),
                 (hmask8[:, :], d["hmask8"]), (seq_ind[:, :], d["seq_ind"]), (colb[:, :], d["colb"]),
                 (lnw[:, :, :], d["lnw"]), (edge_w[:, :], d["edge_w"]), (edge_b[:, :], d["edge_b"]),
                 (pos_i[:, :], d["pos"]), (freq[:, :], d["freq"]),
                 (cond[:, :, :], d["condT"].rearrange("(c p) b -> p c b", p=P)),
                 (wk1[:, :, :], d["k1"].rearrange("(c p) n -> p c n", p=P)),
                 (wo1[:, :, :], d["out1"].rearrange("(c p) n -> p c n", p=P))]
        staged = [(d[k].rearrange("(c p) n -> p c n", p=P), c * n) for k, (c, n) in WEIGHTS.items()]
        staged += [(d["adaln"][c * P:(c + 1) * P, :], NMOD * P) for c in range(DC)]
        NW = len(WEIGHTS)
        x_v = d["xT"].rearrange("(c p) t -> p c t", p=P)
        out_v = d["outT"].rearrange("(c p) t -> p c t", p=P)
        adj_v = d["adj"].rearrange("(n p) e -> p n e", p=P)
        names = list(WEIGHTS)

        def stage_view(k):
            shape = WEIGHTS[names[k]]
            return stage[k % 2][:, 0:shape[0] * shape[1]].rearrange("p (c n) -> p c n", n=shape[1])

        block = ctx.enter_context(nc.Block())

        @block.sync
        def _(sp):
            for dst, src in small:
                sp.dma_start(dst, src).then_inc(consts_in.sem, 16)
            for k, (src, n) in enumerate(staged):
                if k >= 2:
                    sp.wait_ge(weight_lo.sem, k - 1)
                if k < NW:
                    sp.dma_start(stage_view(k), src).then_inc(stage_in[k % 2].sem, 16)
                else:
                    sp.dma_start(stage[k % 2][:, 0:n], src).then_inc(stage_in[k % 2].sem, 16)
            sp.wait_ge(mods_ps.sem, NMOD)
            sp.dma_start(stage[0][:, 0:DC * D].rearrange("p (c n) -> p c n", n=D),
                         d["self_cond"].rearrange("(c p) n -> p c n", p=P)).then_inc(stage_in[0].sem, 16)

            def load_x(m, n):
                wait_last(sp, normed[0], m)
                sp.dma_start(x_in[:, :, :], x_v[:, :, bass.ds(m * MT, MT)]).then_inc(x_in_s.sem, 16)

            def load_residual(m, n):
                wait_last(sp, x1_done, m)
                sp.dma_start(x_res[:, :, :], x_v[:, :, bass.ds(m * MT, MT)]).then_inc(x_res_s.sem, 16)

            def load_edges(m, n):
                wait_last(sp, edge_weighted, m)
                sp.dma_start(adj[:, :, :, :].rearrange("p n e l -> p n (e l)"),
                             adj_v[:, bass.ds(m * TILES, TILES), :]).then_inc(adj_s.sem, 16)

            def store(m, n):
                wait(sp, relu_done, m, 1)
                sp.dma_start(out_v[:, :, bass.ds(m * MT, MT)], sf[:, :, :]).then_inc(out_s.sem, 16)

            run_streams(sp, {(0, "norm"): load_x, (0, "qkv"): lambda m, n: load_residual(m, n) if n == 0 else None,
                             (1, "norm"): load_edges, (1, "out"): store})
            wait(sp, out_s, NM, 0)

        @block.tensor
        def _(pe):
            def linear(out, terms):
                for i, (lhsT, rhs) in enumerate(terms):
                    last = nc.tensor.matmul(out, lhsT, rhs, start=i == 0, stop=i == len(terms) - 1)
                return last

            def fm_terms(k, cols, hi, lo, chunks):
                return [(w[:, c, cols], a[:, c, :]) for c in range(chunks)
                        for w, a in ((wl[k], hi), (wh[k], lo), (wh[k], hi))]

            pe.wait_ge(consts_in.sem, 16 * len(small))
            pe.wait_ge(cond_ready.sem, 1)
            for c in range(DC):
                pe.wait_ge(stage_in[(NW + c) % 2].sem, 16 * ((NW + c) // 2 + 1))
            ps = [lin[0][:, :, :], lin[1][:, :, :], tr[0][:, :, :]]
            for j in range(NMOD):
                out = ps[j // 4].rearrange("p a b -> p (a b)")[:, (j % 4) * P:(j % 4 + 1) * P]
                for c in range(DC):
                    last = nc.tensor.matmul(out, stage[(NW + c) % 2][:, j * P:(j + 1) * P], cond_s[:, c, :],
                                            start=c == 0, stop=c == DC - 1)
                last.then_inc(mods_ps.sem, 1)
            pe.wait_ge(stage_in[0].sem, 16 * ((NW + DC + 1) // 2 + 1))
            w_cond = stage[0][:, 0:DC * D].rearrange("p (c n) -> p c n", n=D)
            for o in range(DC):
                for c in range(DC):
                    last = nc.tensor.matmul(ao_ps[:, 0, o * P:(o + 1) * P], w_cond[:, c, o * P:(o + 1) * P],
                                            cond[:, c, :], start=c == 0, stop=c == DC - 1)
                last.then_inc(mods_ps.sem, 1)
            pe.wait_ge(weight_hi.sem, NW)
            pe.wait_ge(weight_lo.sem, NW)
            pe.wait_ge(zeros_set.sem, 5)
            pe.wait_ge(mods_set.sem, NMOD + DC)

            def norm(stream):
                def step(m, n):
                    wait(pe, squares[stream], m, 1)
                    if stream == 1:
                        wait_last(pe, pT1_b, m)
                        wait_last(pe, summed1, m)
                    else:
                        wait_last(pe, pT_b, m)
                        wait_last(pe, mixed_lo, m)
                    for t in range(TILES):
                        for c in range(DC):
                            last = nc.tensor.matmul(ms_ps[stream][:, t:t + 1], xn[stream][:, c, t * P:(t + 1) * P],
                                                    mean_col[:, :], start=c == 0, stop=c == DC - 1)
                    last.then_inc(means[stream].sem, 1)
                    wait(pe, inverses[stream], m, 1)
                    for t in range(TILES):
                        last = nc.tensor.matmul(spread_ps[stream][:, t * P:(t + 1) * P],
                                                rms_inv[stream][:, t:t + 1].to_broadcast([P, P]), ident[:, :],
                                                start=True, stop=True)
                    last.then_inc(spread[stream].sem, 1)
                return step

            def qkv(m, t):
                if t == 0:
                    wait(pe, normed_hi[0], m, 1)
                    wait(pe, normed_lo[0], m, 1)
                    wait_last(pe, proj_gated, m)
                qk_ps, v_ps = qkv_ps[t]
                rows = slice(t * P, (t + 1) * P)
                terms = [(a[:, c, rows], w[:, c, :]) for c in range(DC)
                         for a, w in ((nh[0], wl["qkv"]), (nl[0], wh["qkv"]), (nh[0], wh["qkv"]))]
                linear(qk_ps, [(a, w[:, 0:2 * D]) for a, w in terms])
                linear(v_ps, [(a, w[:, 2 * D:3 * D]) for a, w in terms]).then_inc(qkv_done.sem, 1)

            def heads(m, t):
                wait(pe, heads_split, m, t + 1)
                if t == 0:
                    wait(pe, v_kept, m, TILES)
                    wait(pe, qk_kept, m, TILES)
                else:
                    wait(pe, kT_kept, m, t)
                    wait(pe, qT_kept, m, t)
                for g in range(NG):
                    last = nc.tensor.transpose(tr[0][:, g, :], qd[:, g, :, :].rearrange("p s f -> p (s f)"), ident[:, :])
                last.then_inc(qT_ps.sem, 1)
                for g in range(NG):
                    last = nc.tensor.transpose(tr[1][:, g, :], kd[:, g, :, :].rearrange("p s f -> p (s f)"), ident[:, :])
                last.then_inc(kT_ps.sem, 1)

            def score(m, t):
                wait(pe, qT_kept, m, t + 1)
                wait(pe, k_spread, m, t + 1)
                if t == 0:
                    wait(pe, qk_kept, m, 1)
                    wait(pe, v_kept, m, 1)
                else:
                    wait(pe, shifted_s, m, t)
                for g in range(NG):
                    last = nc.tensor.matmul(s0_ps[:, g // 2, (g % 2) * 4 * S:(g % 2 + 1) * 4 * S], qT[t][:, g, :],
                                            kbd[:, t, g, :, :].rearrange("p h s -> p (h s)"), start=True, stop=True)
                last.then_inc(scores.sem, 1)

            def probs_t(m, t):
                wait(pe, probs, m, t + 1)
                wait(pe, qT_kept, m, TILES)
                wait(pe, kT_kept, m, TILES)
                if t > 0:
                    wait(pe, pT_a, m, t)
                    wait(pe, pT_b, m, t)
                for j in range(NJ):
                    last = nc.tensor.transpose(tr[j // 4][:, j % 4, :],
                                               e0[t][:, 2 * j:2 * j + 2, :].rearrange("p h s -> p (h s)"), ident[:, :])
                    if j % 4 == 3:
                        last.then_inc(pT_ps.sem, 1)

            def mix(m, t):
                wait(pe, pT_a, m, t + 1)
                wait(pe, pT_b, m, t + 1)
                wait(pe, v_kept, m, t + 1)
                if t > 0:
                    wait(pe, mixed_lo, m, t)
                for j in range(NJ):
                    for s in range(2):
                        f = 32 * (j % 4)
                        last = nc.tensor.matmul(ao_ps[f:f + 32, 0, (j // 4) * P + s * S:(j // 4) * P + (s + 1) * S],
                                                vb[:, t, j, s, :, :].rearrange("p h f -> p (h f)"),
                                                pT0[:, j, s * S:(s + 1) * S], start=True, stop=True,
                                                tile_position=(0, f))
                last.then_inc(mixed.sem, 1)

            def proj(m, n):
                wait(pe, mixed_hi, m, TILES)
                wait(pe, mixed_lo, m, TILES)
                wait(pe, shifted_s, m, TILES)
                for o in range(DC):
                    last = linear(s0_ps[:, 0, o * MT:(o + 1) * MT],
                                  fm_terms("proj", slice(o * P, (o + 1) * P), aoh, aol, DC))
                last.then_inc(proj_done.sem, 1)

            def mlp_up(m, n):
                if n == 0:
                    wait(pe, normed_hi[1], m, 1)
                    wait(pe, normed_lo[1], m, 1)
                    wait_last(pe, pT1_a, m)
                else:
                    wait(pe, z_silu, m, n)
                for k, name in enumerate(("w1", "w3")):
                    if k == 1 and n > 0:
                        wait(pe, g_done, m, n)
                    for c in range(2):
                        j = 2 * n + c
                        last = linear(lin[k][:, c, :], fm_terms(name, slice(j * P, (j + 1) * P), nh[1], nl[1], DC))
                    last.then_inc(z_done.sem, 1)

            def mlp_down(m, n):
                wait(pe, g_hi, m, MC // 2)
                wait(pe, g_lo, m, MC // 2)
                for o in range(DC):
                    last = linear(lin[0][:, o, :], fm_terms("w2", slice(o * P, (o + 1) * P), gh, gl, MC))
                last.then_inc(down_done.sem, 1)

            def self_feat(m, n):
                wait(pe, x2_hi, m, 1)
                wait(pe, x2_lo, m, 1)
                linear(lin[1][:, 0, :], [(ones_r[:, :], a[:, c, :]) for c in range(DC) for a in (nl[1], nh[1])])\
                    .then_inc(rowsum.sem, 1)
                for o in range(DC):
                    last = linear(lin[0][:, o, :], fm_terms("self", slice(o * P, (o + 1) * P), nh[1], nl[1], DC))
                last.then_inc(self_ps.sem, 1)

            def k1(m, n):
                wait(pe, kv_kept, m, 1)
                wait(pe, row_gate, m, 1)
                for k in range(ND * DC):
                    for c in range(DC):
                        last = nc.tensor.matmul(lin[1][:, k // 2, (k % 2) * P:(k % 2 + 1) * P],
                                                wk1[:, c, k * P:(k + 1) * P],
                                                kv[:, c, :, :].rearrange("p b k -> p (b k)"),
                                                start=c == 0, stop=c == DC - 1)
                last.then_inc(k1_ps.sem, 1)

            def q1(m, n):
                wait(pe, self_hi, m, 1)
                wait(pe, self_lo, m, 1)
                for direction in range(ND):
                    if direction == 1:
                        wait(pe, k1_kept, m, 1)
                    for o in range(DC):
                        k = direction * DC + o
                        last = linear(lin[direction][:, o, :],
                                      fm_terms("q1", slice(k * P, (k + 1) * P), nh[1], nl[1], DC))
                    last.then_inc(q1_ps.sem, 1)

            def v1(m, n):
                wait_last(pe, summed1, m)
                wait(pe, kv_kept, m, 1)
                linear(ao1_ps[:, :, :].rearrange("p a b -> p (a b)"),
                       [(kv[:, c, :, :].rearrange("p b k -> p (b k)"), wo1[:, c, :]) for c in range(DC)])\
                    .then_inc(v1_ps.sem, 1)

            def score1(m, t):
                if t == 0:
                    wait(pe, q1_kept, m, ND)
                    wait(pe, k1_spread, m, ND * DC)
                else:
                    wait(pe, pT1_a, m, t)
                    wait(pe, pT1_b, m, t)
                for direction in range(ND):
                    for c in range(DC):
                        for s in range(2):
                            b = 2 * t + s
                            last = nc.tensor.matmul(
                                s1_ps[direction][s * S:(s + 1) * S, c * 8 * NKV:(c + 1) * 8 * NKV],
                                q1T[:, direction, c, b * S:(b + 1) * S],
                                kbd1[:, direction * DC + c, b, :, :].rearrange("p h k -> p (h k)"),
                                start=True, stop=True)
                last.then_inc(scores1.sem, 1)

            def probs_t1(m, t):
                wait(pe, probs1, m, t + 1)
                for j in range(NJ):
                    last = nc.tensor.transpose(tr1[j // 4][:, j % 4, :],
                                               p1[:, j, :, :, :].rearrange("p a h k -> p (a h k)"), ident[:, :])
                    if j % 4 == 3:
                        last.then_inc(pT1_ps.sem, 1)

            def mix1(m, t):
                wait(pe, pT1_a, m, t + 1)
                wait(pe, pT1_b, m, t + 1)
                wait(pe, v1_kept, m, 1)
                if t > 0:
                    wait(pe, summed1, m, t)
                for j in range(NJ):
                    for s in range(2):
                        f = 32 * (j % 4)
                        last = nc.tensor.matmul(ao1_ps[f:f + 32, 0, (j // 4) * P + s * S:(j // 4) * P + (s + 1) * S],
                                                vb1[:, 2 * t + s, j, :, :].rearrange("p h f -> p (h f)"),
                                                pT1[:, j, s * S:(s + 1) * S], start=True, stop=True,
                                                tile_position=(0, f))
                last.then_inc(mixed1.sem, 1)

            run_streams(pe, {
                (0, "norm"): norm(0), (1, "norm"): norm(1), (0, "qkv"): qkv, (0, "heads"): heads,
                (0, "score"): score, (0, "probsT"): probs_t, (0, "mix"): mix, (0, "proj"): proj,
                (1, "mlp_up"): mlp_up, (1, "mlp_down"): mlp_down, (1, "self"): self_feat, (1, "k1"): k1,
                (1, "q1"): q1, (1, "v1"): v1, (1, "score1"): score1, (1, "probsT1"): probs_t1, (1, "mix1"): mix1,
            })

        @block.scalar
        def _(act):
            act.wait_ge(consts_in.sem, 16 * len(small))
            nc.scalar.activation(cond_t[:, :, :], cond[:, :, :], ACT.Tanh, scale=0.5).then_inc(cond_tanh.sem, 1)
            for k, name in enumerate(names):
                act.wait_ge(stage_in[k % 2].sem, 16 * (k // 2 + 1))
                nc.scalar.activation(wh[name][:, :, :], stage_view(k), ACT.Copy,
                                     scale=WEIGHT_SCALE.get(name, 1.0)).then_inc(weight_hi.sem, 1)
            act.wait_ge(table_step.sem, 8)
            nc.scalar.activation(ang[:, :, :], ang[:, :, :], ACT.Sin).then_inc(sines.sem, 1)
            act.wait_ge(biases_set.sem, 2)
            act.wait_ge(zeros_set.sem, 5)

            def norm(stream):
                x = (x_in, x1)[stream]

                def step(m, n):
                    if stream == 0:
                        wait(act, x_in_s, m, 16)
                        wait_last(act, normed_lo[0], m)
                    else:
                        wait(act, x1_done, m, 1)
                        wait_last(act, normed_lo[1], m)
                    wait_last(act, normed_hi[stream], m)
                    nc.scalar.activation(xn[stream][:, :, :], x[:, :, :], ACT.Square).then_inc(squares[stream].sem, 1)
                    wait(act, means[stream], m, 1)
                    nc.scalar.activation(rms_root[stream][:, :], ms_ps[stream], ACT.Sqrt,
                                         bias=eps[:, :]).then_inc(roots[stream].sem, 1)
                    wait(act, shifted[stream], m, 1)
                    wait_last(act, (qkv_done, q1_ps)[stream], m)
                    nc.scalar.activation(nh[stream][:, :, :], xn[stream][:, :, :], ACT.Copy)\
                        .then_inc(normed_hi[stream].sem, 1)
                return step

            def qkv(m, t):
                wait(act, qkv_done, m, t + 1)
                qk_ps, v_ps = qkv_ps[t]
                wait(act, qk_sums, m, t)
                if t == 0:
                    wait_last(act, heads_split, m)
                nc.scalar.activation(qk_sq[:, :, :, :].rearrange("p a h f -> p (a h f)"), qk_ps, ACT.Square)\
                    .then_inc(qk_squares.sem, 1)
                if t == 0:
                    wait_last(act, cos_part, m)
                    wait_last(act, sin_part, m)
                    wait_last(act, mixed, m)
                nc.scalar.activation(qk[:, t, :, :, :].rearrange("p a h f -> p (a h f)"), qk_ps, ACT.Copy)\
                    .then_inc(qk_kept.sem, 1)
                v = v_ps.rearrange("p (j h f) -> p j h f", h=2, f=DH)
                for s in range(2):
                    for h in range(2):
                        last = nc.scalar.activation(vb[h * S:(h + 1) * S, t, :, s, h, :], v[s * S:(s + 1) * S, :, h, :],
                                                    ACT.Copy)
                last.then_inc(v_kept.sem, 1)

            def rope_scale(m, n):
                wait(act, qk_sums, m, TILES)
                wait_last(act, qk_inverses, m)
                nc.scalar.activation(qk_root[:, :, :], qk_ss[:, :, :], ACT.Sqrt, bias=eps[:, :], scale=1.0 / DH)\
                    .then_inc(qk_roots.sem, 1)

            def heads(m, t):
                wait(act, qT_ps, m, t + 1)
                wait(act, scores, m, t - TILES + 1)
                nc.scalar.activation(qT[t][:, :, :], tr[0][:, :, :], ACT.Copy).then_inc(qT_kept.sem, 1)
                wait(act, kT_ps, m, t + 1)
                wait(act, k_spread, m, t)
                for s in range(2):
                    last = nc.scalar.activation(kT[s * S:(s + 1) * S, :, :], tr[1][s * S:(s + 1) * S, :, s * S:(s + 1) * S],
                                                ACT.Copy)
                last.then_inc(kT_kept.sem, 1)

            def score(m, t):
                wait(act, shifted_s, m, t + 1)
                nc.scalar.activation(e0[t][:, :, :], e0[t][:, :, :], ACT.Exp, scale=DH ** -0.5).then_inc(exps.sem, 1)

            def probs_t(m, t):
                wait(act, pT_ps, m, 2 * t + 1)
                wait(act, mixed, m, t)
                nc.scalar.activation(pT0[:, 0:4, :], tr[0][:, :, :], ACT.Copy).then_inc(pT_a.sem, 1)

            def mix(m, t):
                wait(act, mixed, m, t + 1)
                wait_last(act, proj_done, m)
                nc.scalar.activation(aoh[:, :, t * P:(t + 1) * P],
                                     ao_ps[:, 0, :].rearrange("p (c t) -> p c t", c=DC), ACT.Copy)\
                    .then_inc(mixed_hi.sem, 1)

            def mlp_up(m, n):
                wait(act, z_done, m, 2 * n + 1)
                wait(act, z_silu, m, n)
                nc.scalar.activation(th[:, :, :], lin[0][:, :, :], ACT.Tanh, scale=0.5).then_inc(z_tanh.sem, 1)
                wait(act, g_done, m, n + 1)
                wait_last(act, down_done, m)
                nc.scalar.activation(gh[:, 2 * n:2 * n + 2, :], gf[:, :, :], ACT.Copy).then_inc(g_hi.sem, 1)

            def self_feat(m, n):
                wait(act, x2_done, m, 1)
                nc.scalar.activation(nh[1][:, :, :], x2[:, :, :], ACT.Copy).then_inc(x2_hi.sem, 1)
                wait(act, self_done, m, DC)
                wait_last(act, v1_ps, m)
                nc.scalar.activation(kv[:, :, :, :], sf[:, :, :].rearrange("p c (b s) -> p c b s", s=S)[:, :, :, 0:NKP],
                                     ACT.Copy).then_inc(kv_kept.sem, 1)
                wait(act, x2_lo, m, 1)
                wait(act, self_ps, m, 1)
                nc.scalar.activation(nh[1][:, :, :], sf[:, :, :], ACT.Copy).then_inc(self_hi.sem, 1)

            def k1(m, n):
                wait(act, k1_ps, m, 1)
                wait_last(act, k1_spread, m)
                for k in range(ND * DC):
                    last = nc.scalar.activation(
                        k1T[:, k // 2, k % 2, :, :].rearrange("p b k -> p (b k)"),
                        lin[1][:, k // 2, (k % 2) * P:(k % 2 + 1) * P], ACT.Identity, bias=bk[:, k:k + 1])
                last.then_inc(k1_kept.sem, 1)

            def q1(m, n):
                wait_last(act, scores1, m)
                wait(act, edge_value, m, 1)
                for direction in range(ND):
                    wait(act, q1_ps, m, direction + 1)
                    for o in range(DC):
                        k = direction * DC + o
                        last = nc.scalar.activation(q1T[:, direction, o, :], lin[direction][:, o, :], ACT.Identity,
                                                    bias=bq4[:, k:k + 1], scale=DH ** -0.5)
                    last.then_inc(q1_kept.sem, 1)

            def v1(m, n):
                wait(act, v1_ps, m, 1)
                wait_last(act, mixed1, m)
                v = ao1_ps[:, :, :].rearrange("p a (j h f) -> p a j h f", h=2, f=DH)
                for b in range(MB):
                    for r in range(4):
                        last = nc.scalar.activation(vb1[r * NKP:(r + 1) * NKP, b, :, r % 2, :],
                                                    v[b * NKP:(b + 1) * NKP, r // 2, :, r % 2, :], ACT.Copy)
                last.then_inc(v1_kept.sem, 1)

            def score1(m, t):
                wait(act, shifted1, m, t + 1)
                nc.scalar.activation(e1[:, :, :, :], e1[:, :, :, :], ACT.Exp).then_inc(exps1.sem, 1)

            def probs_t1(m, t):
                wait(act, pT1_ps, m, 2 * t + 1)
                wait(act, mixed1, m, t)
                nc.scalar.activation(pT1[:, 0:4, :], tr1[0], ACT.Copy).then_inc(pT1_a.sem, 1)

            run_streams(act, {
                (0, "norm"): norm(0), (1, "norm"): norm(1), (0, "qkv"): qkv, (0, "rope_scale"): rope_scale,
                (0, "heads"): heads, (0, "score"): score, (0, "probsT"): probs_t, (0, "mix"): mix,
                (1, "mlp_up"): mlp_up, (1, "self"): self_feat, (1, "k1"): k1, (1, "q1"): q1, (1, "v1"): v1,
                (1, "score1"): score1, (1, "probsT1"): probs_t1,
            })

        @block.vector
        def _(dve):
            nc.vector.memset(eps[:, :], EPS).then_inc(zeros_set.sem, 1)
            nc.vector.memset(ones_r[:, :].bitcast(F32), 1.0).then_inc(zeros_set.sem, 1)
            nc.vector.memset(ones_f[:, :], 1.0).then_inc(zeros_set.sem, 1)
            nc.vector.memset(vb[:, :, :, :, :, :].rearrange("p t j s h f -> p (t j s h f)"), 0.0).then_inc(zeros_set.sem, 1)
            nc.vector.memset(vb1[:, :, :, :, :].rearrange("p b j h f -> p (b j h f)"), 0.0).then_inc(zeros_set.sem, 1)
            nc.vector.memset(p1[:, :, :, :, :].rearrange("p j a h k -> p (j a h k)"), 0.0).then_inc(zeros_set.sem, 1)
            dve.wait_ge(consts_in.sem, 16 * len(small))
            dve.wait_ge(cond_tanh.sem, 1)
            nc.vector.scalar_tensor_tensor(cond_t[:, :, :], cond_t[:, :, :], 1.0, cond[:, :, :], ALU.add, ALU.mult)\
                .then_inc(table_step.sem, 1)
            dve.wait_ge(table_step.sem, 1)
            nc.vector.tensor_scalar(cond_s[:, :, :], cond_t[:, :, :], 0.5, None, ALU.mult).then_inc(cond_ready.sem, 1)
            nc.vector.tensor_copy(pos_f[:, :], pos_i[:, :]).then_inc(table_step.sem, 1)
            dve.wait_ge(table_step.sem, 2)
            nc.vector.tensor_scalar(ang[:, 0, :], freq[:, :], pos_f[:, :], None, ALU.mult)
            nc.vector.tensor_scalar(ang[:, 1, :], freq[:, :], pos_f[:, :], 1.5707963267948966, ALU.mult, ALU.add)\
                .then_inc(table_step.sem, 1)
            dve.wait_ge(table_step.sem, 3)
            nc.vector.tensor_scalar(turns_i[:, :, :], ang[:, :, :], 0.15915494309189535, None, ALU.mult)\
                .then_inc(table_step.sem, 1)
            dve.wait_ge(table_step.sem, 4)
            nc.vector.tensor_copy(turns[:, :, :], turns_i[:, :, :]).then_inc(table_step.sem, 1)
            for i, part in enumerate(TWO_PI_PARTS):
                dve.wait_ge(table_step.sem, 5 + i)
                last = nc.vector.scalar_tensor_tensor(ang[:, :, :], turns[:, :, :], -part, ang[:, :, :], ALU.mult, ALU.add)
                if i < 2:
                    last.then_inc(table_step.sem, 1)
                else:
                    last.then_inc(biases_set.sem, 1)
            dve.wait_ge(biases_set.sem, 1)
            nc.vector.tensor_scalar(ang[:, :, :], ang[:, :, :], 3.1415925, -3.1415925, ALU.min, ALU.max)\
                .then_inc(table_step.sem, 1)
            nc.vector.tensor_scalar(bq4[:, :], bq, DH ** -0.5, None, ALU.mult)
            nc.vector.tensor_tensor(bout[:, :], bo[:, 0:DC], bo[:, DC:2 * DC], ALU.add).then_inc(biases_set.sem, 1)
            for k, name in enumerate(names):
                dve.wait_ge(weight_hi.sem, k + 1)
                nc.vector.scalar_tensor_tensor(wl[name][:, :, :], stage_view(k), WEIGHT_SCALE.get(name, 1.0),
                                               wh[name][:, :, :].bitcast(F32), ALU.mult, ALU.subtract)\
                    .then_inc(weight_lo.sem, 1)
            dve.wait_ge(sines.sem, 1)
            half = DH // 2
            for i in range(2):
                for a in range(2):
                    nc.vector.tensor_tensor(cosw[:, i, a * half:(a + 1) * half], lnw[:, i, a * half:(a + 1) * half],
                                            ang[:, 1, :], ALU.mult)
                    last = nc.vector.scalar_tensor_tensor(sinw[:, i, a * half:(a + 1) * half], ang[:, 0, :],
                                                          (1.0, -1.0)[a], lnw[:, i, a * half:(a + 1) * half],
                                                          ALU.mult, ALU.mult)
            last.then_inc(table_step.sem, 1)
            ps = [lin[0], lin[1], tr[0]]
            for j in range(NMOD):
                dve.wait_ge(mods_ps.sem, 4 * (j // 4 + 1))
                one = 1.0 if j // DC in (SCALE_A // DC, SCALE_M // DC) else 0.0
                nc.vector.tensor_scalar(mods[:, j, :], ps[j // 4][:, :, :].rearrange("p a b -> p (a b)")[:, (j % 4) * P:(j % 4 + 1) * P],
                                        adaln_b[:, j:j + 1], one, ALU.add, ALU.add).then_inc(mods_set.sem, 1)
            for o in range(DC):
                dve.wait_ge(mods_ps.sem, NMOD + DC)
                nc.vector.tensor_copy(mods[:, COND + o, :], ao_ps[:, 0, o * P:(o + 1) * P]).then_inc(mods_set.sem, 1)
            dve.wait_ge(mods_set.sem, NMOD + DC)
            dve.wait_ge(table_step.sem, 9)
            dve.wait_ge(zeros_set.sem, 6)
            dve.wait_ge(biases_set.sem, 2)

            def per_seq(ap):
                return ap.unsqueeze(3).to_broadcast([P, ap.shape[1], MB, S])

            def by_seq(ap):
                return ap.rearrange("p c (b s) -> p c b s", s=S)

            def norm(stream):
                x = (x_in, x1)[stream]
                shift, scale = ((SHIFT_A, SCALE_A), (SHIFT_M, SCALE_M))[stream]

                def step(m, n):
                    wait_last(dve, (proj_gated, cond_part)[stream], m)
                    nc.vector.tensor_tensor(mod[stream][:, :, :], mods[:, :, bass.ds(m * MB, MB)],
                                            ones_f[:, :].rearrange("p (c b) -> p c b", b=MB), ALU.mult)\
                        .then_inc(mod_set[stream].sem, 1)
                    wait(dve, roots[stream], m, 1)
                    nc.vector.reciprocal(rms_inv[stream][:, :], rms_root[stream][:, :]).then_inc(inverses[stream].sem, 1)
                    wait(dve, spread[stream], m, 1)
                    nc.vector.tensor_tensor(xn[stream][:, :, :], x[:, :, :],
                                            spread_ps[stream].unsqueeze(1).to_broadcast([P, DC, MT]), ALU.mult)\
                        .then_inc(normed[stream].sem, 1)
                    wait(dve, normed[stream], m, 1)
                    wait(dve, mod_set[stream], m, 1)
                    nc.vector.tensor_tensor(by_seq(xn[stream][:, :, :]), by_seq(xn[stream][:, :, :]),
                                            per_seq(mod[stream][:, scale:scale + DC, :]), ALU.mult)\
                        .then_inc(scaled[stream].sem, 1)
                    wait(dve, scaled[stream], m, 1)
                    nc.vector.tensor_tensor(by_seq(xn[stream][:, :, :]), by_seq(xn[stream][:, :, :]),
                                            per_seq(mod[stream][:, shift:shift + DC, :]), ALU.add)\
                        .then_inc(shifted[stream].sem, 1)
                return step

            def qkv(m, t):
                wait(dve, qk_squares, m, t + 1)
                if t == 0:
                    wait_last(dve, qk_roots, m)
                nc.vector.tensor_reduce(qk_ss[:, t, :], qk_sq[:, :, :, :].rearrange("p a h f -> p (a h) f"), AX.X, ALU.add)\
                    .then_inc(qk_sums.sem, 1)

            def rope_scale(m, n):
                wait(dve, qk_roots, m, 1)
                nc.vector.reciprocal(qk_inv[:, :, :], qk_root[:, :, :]).then_inc(qk_inverses.sem, 1)
                wait(dve, qk_inverses, m, 1)
                for s in range(2):
                    nc.vector.tensor_scalar(q_inv[:, s, :, :], qk_inv[:, :, 0:H], seq_ind[:, s:s + 1], None, ALU.mult)\
                        .then_inc(q_inverses.sem, 1)

            def rope(m, t):
                wait(dve, qk_kept, m, t + 1)
                nc.vector.tensor_tensor(qs[:, :, :, :], qk[:, t, :, :, :],
                                        sinw[:, :, :].unsqueeze(2).to_broadcast([P, 2, H, DH]), ALU.mult)\
                    .then_inc(sin_part.sem, 1)
                wait(dve, sin_part, m, t + 1)
                wait(dve, cos_part, m, t + 1)
                half = DH // 2
                for a in range(2):
                    nc.vector.tensor_tensor(qr[:, :, :, a * half:(a + 1) * half], qc[:, :, :, a * half:(a + 1) * half],
                                            qs[:, :, :, (1 - a) * half:(2 - a) * half], ALU.add).then_inc(rotated.sem, 1)
                wait(dve, rotated, m, 2 * t + 2)
                wait(dve, q_inverses, m, 2)
                wait(dve, kT_ps, m, t)
                qr_v = qr[:, :, :, :].rearrange("p a (g h) f -> p a g h f", g=NG)
                qd_v = qd[:, :, :, :].rearrange("p g s (h f) -> p g s h f", f=DH)
                for s in range(2):
                    nc.vector.tensor_tensor(qd_v[:, :, s, :, :], qr_v[:, 0, :, :, :],
                                            q_inv[:, s, t, :].rearrange("p (g h) -> p g h", g=NG).unsqueeze(3)
                                            .to_broadcast([P, NG, 4, DH]), ALU.mult)
                kd_v = kd[:, :, :, :].rearrange("p g s (h f) -> p g s h f", f=DH)
                for s in range(2):
                    last = nc.vector.tensor_tensor(kd_v[:, :, s, :, :], qr_v[:, 1, :, :, :],
                                                   qk_inv[:, t, H:2 * H].rearrange("p (g h) -> p g h", g=NG).unsqueeze(3)
                                                   .to_broadcast([P, NG, 4, DH]), ALU.mult)
                last.then_inc(heads_split.sem, 1)

            def score(m, t):
                wait(dve, scores, m, t + 1)
                s_v = s0_ps[:, :, :].rearrange("p a (h s) -> p (a h) s", s=S)
                nc.vector.tensor_reduce(mx0[:, :], s_v, AX.X, ALU.max).then_inc(maxima.sem, 1)
                wait(dve, maxima, m, t + 1)
                wait(dve, pT_ps, m, 2 * (t + 1 - TILES))
                nc.vector.tensor_tensor(e0[t][:, :, :], s_v, mx0[:, :].unsqueeze(2).to_broadcast([P, H, S]),
                                        ALU.subtract).then_inc(shifted_s.sem, 1)
                wait(dve, exps, m, t + 1)
                nc.vector.tensor_reduce(sum0[:, :], e0[t][:, :, :], AX.X, ALU.add).then_inc(exp_sums.sem, 1)
                wait(dve, exp_sums, m, t + 1)
                nc.vector.reciprocal(inv0[t][:, :], sum0[:, :]).then_inc(inv_sums.sem, 1)

            def probs_t(m, t):
                wait(dve, pT_ps, m, 2 * t + 2)
                wait(dve, mixed, m, t)
                nc.vector.tensor_copy(pT0[:, 4:8, :], tr[1][:, :, :]).then_inc(pT_b.sem, 1)

            def mix(m, t):
                wait(dve, mixed_hi, m, t + 1)
                wait_last(dve, proj_done, m)
                nc.vector.tensor_tensor(aol[:, :, t * P:(t + 1) * P], ao_ps[:, 0, :].rearrange("p (c t) -> p c t", c=DC),
                                        aoh[:, :, t * P:(t + 1) * P].bitcast(F32), ALU.subtract)\
                    .then_inc(mixed_lo.sem, 1)

            def proj(m, n):
                wait(dve, proj_done, m, 1)
                wait_last(dve, x2_done, m)
                for o in range(DC):
                    nc.vector.scalar_tensor_tensor(
                        by_seq(x1[:, o:o + 1, :])[:, 0], by_seq(s0_ps[:, 0:1, o * MT:(o + 1) * MT])[:, 0], proj_b[:, o:o + 1],
                        mod[0][:, GATE_A + o, :].unsqueeze(2).to_broadcast([P, MB, S]), ALU.add, ALU.mult)\
                        .then_inc(proj_gated.sem, 1)
                wait(dve, proj_gated, m, DC)
                wait(dve, x_res_s, m, 16)
                nc.vector.tensor_tensor(x1[:, :, :], x1[:, :, :], x_res[:, :, :], ALU.add).then_inc(x1_done.sem, 1)

            def mlp_up(m, n):
                wait(dve, z_tanh, m, n + 1)
                wait(dve, g_lo, m, n)
                wait(dve, g_hi, m, n)
                nc.vector.scalar_tensor_tensor(gf[:, :, :], th[:, :, :], 1.0, lin[0][:, :, :], ALU.add, ALU.mult)\
                    .then_inc(z_silu.sem, 1)
                wait(dve, z_silu, m, n + 1)
                wait(dve, z_done, m, 2 * n + 2)
                nc.vector.tensor_tensor(gf[:, :, :], gf[:, :, :], lin[1][:, :, :], ALU.mult).then_inc(g_done.sem, 1)

            def mlp_down(m, n):
                wait(dve, down_done, m, 1)
                wait_last(dve, relu_done, m)
                nc.vector.tensor_tensor(by_seq(x2[:, :, :]), by_seq(lin[0][:, :, :]),
                                        per_seq(mod[1][:, GATE_M:GATE_M + DC, :]), ALU.mult).then_inc(down_gated.sem, 1)
                wait(dve, down_gated, m, 1)
                nc.vector.tensor_tensor(x2[:, :, :], x2[:, :, :], x1[:, :, :], ALU.add).then_inc(x2_done.sem, 1)

            def self_feat(m, n):
                wait(dve, rowsum, m, 1)
                nc.vector.tensor_scalar(gate[:, :], lin[1][:, 0, :], 0.0, None, ALU.not_equal).then_inc(row_gate.sem, 1)
                wait(dve, row_gate, m, 1)
                wait_last(dve, Signal(out_s.sem, 16), m)
                nc.vector.tensor_tensor(by_seq(sf[:, :, :]),
                                        gate[:, :].rearrange("p (b s) -> p b s", s=S).unsqueeze(1).to_broadcast([P, DC, MB, S]),
                                        per_seq(mod[1][:, COND:COND + DC, :]), ALU.mult).then_inc(cond_part.sem, 1)
                wait(dve, cond_part, m, 1)
                wait(dve, self_ps, m, 1)
                for o in range(DC):
                    nc.vector.scalar_tensor_tensor(sf[:, o, :], lin[0][:, o, :], self_b[:, o:o + 1], sf[:, o, :],
                                                   ALU.add, ALU.add).then_inc(self_done.sem, 1)

            def edges(m, n):
                wait(dve, adj_s, m, 16)
                a = adj[:, :, :, :].rearrange("p t e l -> p (t e) l")
                w = adw
                wait_last(dve, scores1, m)
                flat = [v[:, :, :].rearrange("p t e -> p (t e)") for v in (edge_n, edge_v, edge_bias)]
                nc.vector.tensor_reduce(flat[0], a, AX.X, ALU.add).then_inc(edge_count.sem, 1)
                nc.vector.tensor_tensor(w, a, edge_w[:, :].unsqueeze(1).to_broadcast([P, TILES * NE, NL]), ALU.mult)\
                    .then_inc(edge_weighted.sem, 1)
                wait(dve, edge_weighted, m, 1)
                wait(dve, edge_count, m, 1)
                nc.vector.tensor_reduce(flat[1], w, AX.X, ALU.add).then_inc(edge_value.sem, 1)
                nc.vector.tensor_scalar(flat[0], flat[0], 0.0, NEG, ALU.is_le, ALU.mult).then_inc(edge_masked.sem, 1)
                wait(dve, edge_masked, m, 1)
                nc.vector.scalar_tensor_tensor(flat[2], flat[1], edge_b[:, :], flat[0], ALU.add, ALU.add)\
                    .then_inc(edge_ready.sem, 1)

            def k1(m, n):
                wait(dve, k1_kept, m, 1)
                wait_last(dve, scores1, m)
                for k in range(ND * DC):
                    nc.vector.tensor_tensor(kbd1[:, k, :, :, :],
                                            k1T[:, k // 2, k % 2, :, 0:NKV].unsqueeze(2).to_broadcast([P, MB, 8, NKV]),
                                            hmask8[:, :].unsqueeze(1).unsqueeze(3).to_broadcast([P, MB, 8, NKV]),
                                            ALU.mult).then_inc(k1_spread.sem, 1)

            def score1(m, t):
                wait(dve, scores1, m, t + 1)
                wait(dve, edge_ready, m, 1)
                wait(dve, probs1, m, t)
                for direction in range(ND):
                    last = nc.vector.tensor_tensor(
                        e1[:, direction, :, :], s1_ps[direction][:, 0:H * NKV].rearrange("p (h k) -> p h k", k=NKV),
                        edge_bias[:, t, direction * NKV:(direction + 1) * NKV].unsqueeze(1).to_broadcast([P, H, NKV]),
                        ALU.add)
                last.then_inc(biased1.sem, 1)
                wait(dve, biased1, m, t + 1)
                e_v = e1[:, :, :, :].rearrange("p a h k -> p (a h) k")
                mx_v, sum_v, inv_v = (v[:, :, :].rearrange("p a h -> p (a h)") for v in (mx1, sum1, inv1))
                nc.vector.tensor_reduce(mx_v, e_v, AX.X, ALU.max).then_inc(maxima1.sem, 1)
                wait(dve, maxima1, m, t + 1)
                nc.vector.tensor_tensor(e_v, e_v, mx_v.unsqueeze(2).to_broadcast([P, ND * H, NKV]), ALU.subtract)\
                    .then_inc(shifted1.sem, 1)
                wait(dve, exps1, m, t + 1)
                nc.vector.tensor_reduce(sum_v, e_v, AX.X, ALU.add).then_inc(sums1.sem, 1)
                wait(dve, sums1, m, t + 1)
                nc.vector.reciprocal(inv_v, sum_v).then_inc(inverses1.sem, 1)

            def probs_t1(m, t):
                wait(dve, pT1_ps, m, 2 * t + 2)
                wait(dve, mixed1, m, t)
                nc.vector.tensor_copy(pT1[:, 4:8, :], tr1[1]).then_inc(pT1_b.sem, 1)

            def mix1(m, t):
                wait(dve, mixed1, m, t + 1)
                for c in range(DC):
                    last = nc.vector.scalar_tensor_tensor(sf[:, c, t * P:(t + 1) * P], ao1_ps[:, 0, c * P:(c + 1) * P],
                                                          bout[:, c:c + 1], sf[:, c, t * P:(t + 1) * P], ALU.add, ALU.add)
                last.then_inc(summed1.sem, 1)

            def out(m, n):
                wait(dve, summed1, m, TILES)
                nc.vector.scalar_tensor_tensor(sf[:, :, :], sf[:, :, :], 0.0, x2[:, :, :], ALU.max, ALU.add)\
                    .then_inc(relu_done.sem, 1)

            run_streams(dve, {
                (0, "norm"): norm(0), (1, "norm"): norm(1), (0, "qkv"): qkv, (0, "rope_scale"): rope_scale,
                (0, "rope"): rope, (0, "score"): score, (0, "probsT"): probs_t, (0, "mix"): mix, (0, "proj"): proj,
                (1, "mlp_up"): mlp_up, (1, "mlp_down"): mlp_down, (1, "self"): self_feat, (1, "edges"): edges,
                (1, "k1"): k1, (1, "score1"): score1, (1, "probsT1"): probs_t1, (1, "mix1"): mix1, (1, "out"): out,
            })

        @block.gpsimd
        def _(pool):
            pool.wait_ge(zeros_set.sem, 6)
            pool.wait_ge(table_step.sem, 9)
            pool.wait_ge(mods_set.sem, NMOD + DC)

            def low_part(out, full, hi):
                return nc.gpsimd.tensor_tensor(out, full, hi.bitcast(F32), ALU.subtract)

            def norm(stream):
                def step(m, n):
                    wait(pool, normed_hi[stream], m, 1)
                    low_part(nl[stream][:, :, :], xn[stream][:, :, :], nh[stream][:, :, :])\
                        .then_inc(normed_lo[stream].sem, 1)
                return step

            def rope(m, t):
                wait(pool, qk_kept, m, t + 1)
                wait(pool, rotated, m, 2 * t)
                nc.gpsimd.tensor_tensor(qc[:, :, :, :], qk[:, t, :, :, :],
                                        cosw[:, :, :].unsqueeze(2).to_broadcast([P, 2, H, DH]), ALU.mult)\
                    .then_inc(cos_part.sem, 1)

            def heads(m, t):
                wait(pool, kT_kept, m, t + 1)
                wait(pool, scores, m, t + 1 - TILES)
                nc.gpsimd.tensor_tensor(kbd[:, t, :, :, :], kT[:, :, :].unsqueeze(2).to_broadcast([P, NG, 4, S]),
                                        hmask4[:, :].unsqueeze(1).unsqueeze(3).to_broadcast([P, NG, 4, S]), ALU.mult)\
                    .then_inc(k_spread.sem, 1)

            def score(m, t):
                wait(pool, inv_sums, m, t + 1)
                nc.gpsimd.tensor_tensor(e0[t][:, :, :], e0[t][:, :, :],
                                        inv0[t][:, :].unsqueeze(2).to_broadcast([P, H, S]), ALU.mult)\
                    .then_inc(probs.sem, 1)

            def mlp_up(m, n):
                wait(pool, g_hi, m, n + 1)
                low_part(gl[:, 2 * n:2 * n + 2, :], gf[:, :, :], gh[:, 2 * n:2 * n + 2, :]).then_inc(g_lo.sem, 1)

            def self_feat(m, n):
                wait(pool, x2_hi, m, 1)
                low_part(nl[1][:, :, :], x2[:, :, :], nh[1][:, :, :]).then_inc(x2_lo.sem, 1)
                wait(pool, self_hi, m, 1)
                low_part(nl[1][:, :, :], sf[:, :, :], nh[1][:, :, :]).then_inc(self_lo.sem, 1)

            def score1(m, t):
                wait(pool, inverses1, m, t + 1)
                wait(pool, pT1_ps, m, 2 * t)
                for direction in range(ND):
                    last = nc.gpsimd.tensor_tensor(
                        p1[:, :, direction, :, 0:NKV], e1[:, direction, :, :].rearrange("p (j h) k -> p j h k", h=2),
                        inv1[:, direction, :].rearrange("p (j h) -> p j h", h=2).unsqueeze(3).to_broadcast([P, NJ, 2, NKV]),
                        ALU.mult)
                last.then_inc(probs1.sem, 1)

            run_streams(pool, {
                (0, "norm"): norm(0), (1, "norm"): norm(1), (0, "rope"): rope, (0, "heads"): heads,
                (0, "score"): score, (1, "mlp_up"): mlp_up, (1, "self"): self_feat, (1, "score1"): score1,
            })


def kernel(**inputs):
    import numpy as np

    from concourse import bacc
    from concourse.bass_utils import run_bass_kernel_spmd

    a = {k: np.asarray(v) for k, v in inputs.items()}

    def col(v):
        return v.reshape(-1, P).T

    def padded(v, axis):
        pad = [(0, 0), (0, 0)]
        pad[axis] = (0, MC * P - HM)
        return np.pad(v, pad)

    def rows(v):
        return np.broadcast_to(v, (P, *v.shape))

    adj = a["mask_BxSxSx11_ik0"]
    part = np.arange(P)
    arrays = {
        "xT": a["x"].reshape(B * S, D).T,
        "condT": a["cond_1024"].T,
        "pos": np.tile(a["pos_S"], 2).reshape(P, 1),
        "adj": np.stack([adj[:, :, :NKV], adj[:, :NKV].transpose(0, 2, 1, 3)], 2).reshape(B * S, NE * NL),
        "adaln": a["L0_cond_adaln_w"], "qkv": a["L0_cond_qkv_w"], "proj": a["L0_cond_proj_w"],
        "w1": padded(a["L0_cond_w1_w"], 1), "w3": padded(a["L0_cond_w3_w"], 1), "w2": padded(a["L0_cond_w2_w"], 0),
        "self": a["L1_cond_W_self"].T[:D], "self_cond": a["L1_cond_W_self"].T[D:],
        "q1": np.concatenate([w.T for w in a["L1_cond_Wq"]], 1),
        "k1": np.concatenate([w.T for w in a["L1_cond_Wk"]], 1),
        "out1": np.concatenate([w.reshape(D, D).T for w in a["L1_cond_Wout"]], 1),
        "colb": np.concatenate([col(a[k]) for k in ("L0_cond_adaln_b", "L0_cond_proj_b", "L1_cond_b_self",
                                                    "L1_cond_bq", "L1_cond_bk", "L1_cond_bout")], 1),
        "lnw": rows(np.stack([a["L0_cond_lnq_w"], a["L0_cond_lnk_w"]])),
        "edge_w": rows(a["L1_cond_w_bias"]), "edge_b": rows(a["L1_cond_b_bias"].reshape(1)),
        "ident": np.eye(P, dtype=np.float32),
        "mean_col": np.full((P, 1), 1.0 / D, np.float32),
        "hmask4": (part[:, None] % 64 // DH == np.arange(4)).astype(np.float32),
        "hmask8": (part[:, None] // DH == np.arange(8)).astype(np.float32),
        "seq_ind": (part[:, None] // S == np.arange(2)).astype(np.float32),
        "freq": np.broadcast_to((1.0 / 10000.0 ** (np.arange(DH // 2, dtype=np.float32) / (DH // 2)))
                                .astype(np.float32), (P, DH // 2)),
    }
    arrays = {k: np.ascontiguousarray(v) for k, v in arrays.items()}
    nc = bacc.Bacc("TRN2", target_bir_lowering=False, num_devices=1)
    d = {k: nc.dram_tensor(f"in_{k}", v.shape, mybir.dt.from_np(v.dtype), kind="ExternalInput").ap()
         for k, v in arrays.items()}
    d["outT"] = nc.dram_tensor("out_T", (D, B * S), F32, kind="ExternalOutput").ap()
    build_program(nc, d)
    r = run_bass_kernel_spmd(nc, [{f"in_{k}": v for k, v in arrays.items()}], core_ids=[0])
    return r.results[0]["out_T"].T.reshape(B, S, D)
```

```python
from contextlib import ExitStack

import concourse.bass as bass
from concourse import mybir

F32 = mybir.dt.float32
F32R = mybir.dt.float32r
I32 = mybir.dt.int32
ALU = mybir.AluOpType
ACT = mybir.ActivationFunctionType
AX = mybir.AxisListType

P = 128
B, S, D = 128, 64, 256
H, DH = 16, 16
HM = 704
NKV = 20
NKP = 32
NL = 11
EPS = 1e-6
NEG = -9000000000000000.0
DC = D // P
MC = -(-HM // P)
MB = 4
MT = MB * S
TILES = MT // P
NM = B // MB
NJ = H // 2
NG = H // 4
ND = 2
NE = ND * NKV
NMOD = 6 * DC
SHIFT_A, SCALE_A, GATE_A, SHIFT_M, SCALE_M, GATE_M = range(0, NMOD, DC)
COND = NMOD
TWO_PI_PARTS = (6.28125, 0.0019350051879882812, 3.019916e-7)
WEIGHTS = {"qkv": (DC, 3 * D), "proj": (DC, D), "w1": (DC, MC * P), "w3": (DC, MC * P), "w2": (MC, D),
           "self": (DC, D), "q1": (DC, ND * D)}
WEIGHT_SCALE = {"w2": 0.5}

ORDER = {
    "PE": [
        (0, "mlp_up", 0), (1, "heads", 0), (0, "mlp_up", 1), (0, "mlp_up", 2), (1, "score", 0), (1, "heads", 1),
        (0, "mlp_down", 0), (1, "score", 1), (0, "self", 0), (1, "probsT", 0), (0, "k1", 0), (0, "q1", 0),
        (1, "mix", 0), (1, "probsT", 1), (0, "score1", 0), (1, "mix", 1), (0, "v1", 0), (1, "proj", 0),
        (2, "norm0_mean", 0), (2, "norm0_apply", 0), (0, "probsT1", 0), (1, "norm1_mean", 0), (0, "score1", 1),
        (1, "norm1_apply", 0), (2, "qkv", 0), (2, "qkv", 1), (0, "mix1", 0), (0, "probsT1", 1), (0, "mix1", 1),
    ],
    "DVE": [
        (0, "mlp_up", 0), (1, "rope", 1), (0, "mlp_up", 1), (0, "mlp_up", 2), (1, "score", 0), (0, "edges", 0),
        (0, "mlp_down", 0), (1, "soft", 0), (0, "self", 0), (1, "score", 1), (1, "probsT", 0), (1, "soft", 1),
        (0, "k1", 0), (1, "mix", 0), (1, "probsT", 1), (0, "score1", 0), (1, "mix", 1), (0, "soft1", 0),
        (2, "norm0_mean", 0), (1, "proj", 0), (2, "norm0_apply", 0), (0, "probsT1", 0), (1, "norm1_mean", 0),
        (0, "score1", 1), (0, "soft1", 1), (2, "qkv", 0), (1, "norm1_apply", 0), (2, "qkv", 1), (0, "mix1", 0),
        (0, "probsT1", 1), (2, "rope_scale", 0), (2, "rope", 0), (0, "mix1", 1), (0, "out", 0),
    ],
    "Activation": [
        (0, "mlp_up", 0), (1, "heads", 0), (0, "mlp_up", 1), (0, "mlp_up", 2), (1, "heads", 1), (1, "score", 0),
        (0, "x2_split", 0), (0, "self_split", 0), (1, "score", 1), (1, "probsT", 0), (0, "k1", 0), (0, "q1", 0),
        (1, "mix", 0), (1, "probsT", 1), (1, "mix", 1), (0, "score1", 0), (2, "norm0_mean", 0), (0, "v1", 0),
        (0, "probsT1", 0), (1, "norm1_mean", 0), (2, "norm0_apply", 0), (0, "score1", 1), (2, "qkv", 0),
        (2, "qkv", 1), (2, "rope_scale", 0), (1, "norm1_apply", 0), (0, "probsT1", 1),
    ],
    "Pool": [
        (1, "rope", 1), (0, "mlp_up", 0), (1, "heads", 0), (0, "mlp_up", 1), (0, "mlp_up", 2), (1, "heads", 1),
        (0, "x2_split", 0), (1, "soft", 0), (0, "self_split", 0), (1, "soft", 1), (0, "soft1", 0),
        (2, "norm0_apply", 0), (0, "soft1", 1), (2, "rope", 0), (1, "norm1_apply", 0),
    ],
    "SP": [
        (2, "norm0_mean", 0), (2, "mlp_up", 0), (2, "norm0_apply", 0), (0, "out", 0),
    ],
}


class Signal:

    def __init__(self, sem, per):
        self.sem, self.per = sem, per


def wait(engine, signal, m, n):
    value = m * signal.per + n
    if not isinstance(value, int) or value > 0:
        engine.wait_ge(signal.sem, value)


def wait_last(engine, signal, m):
    wait(engine, signal, m, 0)


def run_steps(engine, name, steps):
    ahead = max(a for order in ORDER.values() for a, _, _ in order)

    def take(m):
        for a, step, n in ORDER[name]:
            if step in steps and (not isinstance(m, int) or 0 <= m + a < NM):
                steps[step](m + a, n)

    for m in range(-ahead, 1):
        take(m)
    with engine.Fori(1, NM - ahead) as m:
        take(m)
    for m in range(NM - ahead, NM):
        take(m)


def build_program(nc, d):
    with ExitStack() as ctx:
        def sb(name, shape, dt=F32):
            return ctx.enter_context(nc.sbuf_tensor(name, shape, dt))

        def signal(name, per=1):
            return Signal(ctx.enter_context(nc.semaphore(name)), per)

        ident = sb("ident", [P, P])
        mean_col = sb("mean_col", [P, 1])
        ones_r = sb("ones_r", [P, P], F32R)
        ones_f = sb("ones_f", [P, 56])
        hmask4 = sb("hmask4", [P, 4])
        hmask8 = sb("hmask8", [P, 8])
        seq_ind = sb("seq_ind", [P, 2])
        eps = sb("eps", [P, 1])
        wh = {k: sb(f"{k}_hi", [P, *s], F32R) for k, s in WEIGHTS.items()}
        wl = {k: sb(f"{k}_lo", [P, *s], F32R) for k, s in WEIGHTS.items()}
        wk1 = sb("wk1", [P, DC, ND * D])
        wo1 = sb("wo1", [P, DC, ND * D])
        mods = sb("mods", [P, NMOD + DC, B])
        colb = sb("colb", [P, NMOD + 2 * DC + 3 * ND * DC])
        adaln_b, proj_b = colb[:, 0:NMOD], colb[:, NMOD:NMOD + DC]
        self_b = colb[:, NMOD + DC:NMOD + 2 * DC]
        bq, bk, bo = (colb[:, NMOD + 2 * DC + i * ND * DC:NMOD + 2 * DC + (i + 1) * ND * DC] for i in range(3))
        bq4 = sb("bq4", [P, ND * DC])
        bout = sb("bout", [P, DC])
        lnw = sb("lnw", [P, 2, DH])
        edge_w = sb("edge_w", [P, NL])
        edge_b = sb("edge_b", [P, 1])
        pos_i = sb("pos_i", [P, 1], I32)
        pos_f = sb("pos_f", [P, 1])
        freq = sb("freq", [P, DH // 2])
        ang = sb("ang", [P, 2, DH // 2])
        turns_i = sb("turns_i", [P, 2, DH // 2], I32)
        turns = sb("turns", [P, 2, DH // 2])
        cosw = sb("cosw", [P, 2, DH])
        sinw = sb("sinw", [P, 2, DH])

        xn = [sb(f"xn{i}", [P, DC, MT]) for i in range(2)]
        rms_root = [sb(f"rms_root{i}", [P, TILES]) for i in range(2)]
        rms_inv = [sb(f"rms_inv{i}", [P, TILES]) for i in range(2)]
        mod = [sb(f"mod{i}", [P, NMOD + DC, MB]) for i in range(2)]
        nh = [sb(f"nh{i}", [P, DC, MT], F32R) for i in range(2)]
        nl = [sb(f"nl{i}", [P, DC, MT], F32R) for i in range(2)]

        x_in = sb("x_in", [P, DC, MT])
        x_res = sb("x_res", [P, DC, MT])
        x1 = sb("x1", [P, DC, MT])
        qk = sb("qk", [P, TILES, 2, H, DH])
        qk_sq = sb("qk_sq", [P, 2, H, DH])
        qk_ss = sb("qk_ss", [P, TILES, 2 * H])
        qk_root = sb("qk_root", [P, TILES, 2 * H])
        qk_inv = sb("qk_inv", [P, TILES, 2 * H])
        q_inv = sb("q_inv", [P, 2, TILES, H])
        qc = sb("qc", [P, 2, H, DH])
        qs = sb("qs", [P, 2, H, DH])
        qr = qk_sq
        qd = sb("qd", [P, NG, 2, 4 * DH])
        kd = sb("kd", [P, NG, 2, 4 * DH])
        vb = sb("vb", [P, TILES, NJ, 2, 2, DH])
        qT = [sb(f"qT{i}", [P, NG, P]) for i in range(TILES)]
        kT = sb("kT", [P, NG, S])
        kbd = sb("kbd", [P, TILES, NG, 4, S])
        mx0 = sb("mx0", [P, H])
        e0 = [sb(f"e0_{i}", [P, H, S]) for i in range(TILES)]
        sum0 = sb("sum0", [P, H])
        inv0 = [sb(f"inv0_{i}", [P, H]) for i in range(TILES)]
        pT0 = sb("pT0", [P, NJ, P])
        aoh = sb("aoh", [P, DC, MT], F32R)
        aol = sb("aol", [P, DC, MT], F32R)

        th = sb("th", [P, 2, MT])
        gf = sb("gf", [P, 2, MT])
        gh = sb("gh", [P, MC, MT], F32R)
        gl = sb("gl", [P, MC, MT], F32R)
        x2 = sb("x2", [P, DC, MT])
        sf = sb("sf", [P, DC, MT])
        gate = sb("gate", [P, MT])
        kv = sb("kv", [P, DC, MB, NKP])
        q1T = sb("q1T", [P, ND, DC, MT])
        k1T = sb("k1T", [P, ND, DC, MB, NKP])
        kbd1 = sb("kbd1", [P, ND * DC, MB, 8, NKV])
        vb1 = sb("vb1", [P, MB, NJ, 2, DH])
        adj = sb("adj", [P, TILES, NE, NL], I32)
        adw = q1T[:, :, :, :].rearrange("p a c t -> p (a c t)")[:, 0:TILES * NE * NL].rearrange("p (e l) -> p e l", l=NL)
        edge_n = sb("edge_n", [P, TILES, NE])
        edge_v = sb("edge_v", [P, TILES, NE])
        edge_bias = sb("edge_bias", [P, TILES, NE])
        e1 = sb("e1", [P, ND, H, NKV])
        mx1 = sb("mx1", [P, ND, H])
        sum1 = sb("sum1", [P, ND, H])
        inv1 = sb("inv1", [P, ND, H])
        p1 = sb("p1", [P, NJ, ND, 2, NKP])
        pT1 = sb("pT1", [P, NJ, P])
        stage = [kbd1[:, :, :, :, :].rearrange("p a b c d -> p (a b c d)")[:, 0:DC * 3 * D],
                 kbd[:, :, :, :, :].rearrange("p a b c d -> p (a b c d)")[:, 0:DC * 3 * D]]

        cond, cond_t = (v.rearrange("p (c b) -> p c b", b=B) for v in (th[:, 0, :], th[:, 1, :]))
        cond_s = gf[:, 0, :].rearrange("p (c b) -> p c b", b=B)

        lin = [ctx.enter_context(nc.psum_tensor(f"lin{i}", [P, 2, MT], F32)) for i in range(2)]
        s0_ps = ctx.enter_context(nc.psum_tensor("s0_ps", [P, 2, 2 * MT], F32))
        tr = [ctx.enter_context(nc.psum_tensor(f"tr{i}", [P, 4, P], F32)) for i in range(2)]
        ao_ps = ctx.enter_context(nc.psum_tensor("ao_ps", [P, 2, MT], F32))
        ao1_ps = ctx.enter_context(nc.psum_tensor("ao1_ps", [P, 2, MT], F32))
        s1_ps = [lin[i][:, :, :].rearrange("p a b -> p (a b)") for i in range(2)]
        tr1 = [s.rearrange("p (a b) -> p a b", b=P) for s in s1_ps]
        qkv_ps = [(s0_ps[:, 0, :], s0_ps[:, 1, 0:D]),
                  (tr[0][:, :, :].rearrange("p a b -> p (a b)"),
                   tr[1][:, :, :].rearrange("p a b -> p (a b)")[:, 0:D])]
        ms_ps, spread_ps = ao_ps[:, 1, 0:TILES], ao_ps[:, 0, :]

        consts_in = signal("consts_in")
        stage_in = [signal("stage0_in"), signal("stage1_in")]
        zeros_set = signal("zeros_set")
        weight_hi = signal("weight_hi")
        weight_lo = signal("weight_lo")
        table_step = signal("table_step")
        sines = signal("sines")
        cond_tanh = signal("cond_tanh")
        cond_ready = signal("cond_ready")
        mods_ps = signal("mods_ps")
        mods_set = signal("mods_set")
        biases_set = signal("biases_set")

        x_in_s, x_res_s, adj_s = signal("x_in_s", 16), signal("x_res_s", 16), signal("adj_s", 16)
        out_s = signal("out_s", 16)
        mod_set = [signal("mod_set_L0"), signal("mod_set_L1")]
        squares = [signal("squares_L0"), signal("squares_L1")]
        means = [signal("means_L0"), signal("means_L1")]
        roots = [signal("roots_L0"), signal("roots_L1")]
        inverses = [signal("inverses_L0"), signal("inverses_L1")]
        spread = [signal("spread_L0"), signal("spread_L1")]
        normed = [signal("normed_L0"), signal("normed_L1")]
        scaled = [signal("scaled_L0"), signal("scaled_L1")]
        shifted = [signal("shifted_L0"), signal("shifted_L1")]
        normed_hi = [signal("normed_hi_L0"), signal("normed_hi_L1")]
        normed_lo = [signal("normed_lo_L0"), signal("normed_lo_L1")]
        qkv_done = signal("qkv_done", TILES)
        qk_squares, qk_kept, v_kept = signal("qk_squares", TILES), signal("qk_kept", TILES), signal("v_kept", TILES)
        qk_sums, qk_roots, qk_inverses = signal("qk_sums", TILES), signal("qk_roots"), signal("qk_inverses")
        q_inverses = signal("q_inverses", 2)
        cos_part, sin_part = signal("cos_part", TILES), signal("sin_part", TILES)
        rotated = signal("rotated", 2 * TILES)
        heads_split = signal("heads_split", TILES)
        qT_ps, kT_ps = signal("qT_ps", TILES), signal("kT_ps", TILES)
        qT_kept, kT_kept = signal("qT_kept", TILES), signal("kT_kept", TILES)
        k_spread = signal("k_spread", TILES)
        scores, maxima, shifted_s = signal("scores", TILES), signal("maxima", TILES), signal("shifted_s", TILES)
        exps, exp_sums, inv_sums = signal("exps", TILES), signal("exp_sums", TILES), signal("inv_sums", TILES)
        probs = signal("probs", TILES)
        pT_ps = signal("pT_ps", 2 * TILES)
        pT_a, pT_b = signal("pT_a", TILES), signal("pT_b", TILES)
        mixed, mixed_hi, mixed_lo = signal("mixed", TILES), signal("mixed_hi", TILES), signal("mixed_lo", TILES)
        proj_done, proj_gated, x1_done = signal("proj_done"), signal("proj_gated", DC), signal("x1_done")

        z_done, z_tanh, z_silu = signal("z_done", MC), signal("z_tanh", MC // 2), signal("z_silu", MC // 2)
        g_done, g_hi, g_lo = signal("g_done", MC // 2), signal("g_hi", MC // 2), signal("g_lo", MC // 2)
        down_done, down_gated = signal("down_done"), signal("down_gated")
        x2_done, x2_hi, x2_lo = signal("x2_done"), signal("x2_hi"), signal("x2_lo")
        rowsum, row_gate, cond_part = signal("rowsum"), signal("row_gate"), signal("cond_part")
        self_ps, self_done = signal("self_ps"), signal("self_done", DC)
        self_hi, self_lo = signal("self_hi"), signal("self_lo")
        q1_ps, q1_kept = signal("q1_ps", ND), signal("q1_kept", ND)
        kv_kept = signal("kv_kept")
        k1_ps, k1_kept, k1_spread = signal("k1_ps"), signal("k1_kept"), signal("k1_spread", ND * DC)
        v1_ps, v1_kept = signal("v1_ps"), signal("v1_kept")
        edge_count, edge_weighted, edge_value = signal("edge_count"), signal("edge_weighted"), signal("edge_value")
        edge_masked, edge_ready = signal("edge_masked"), signal("edge_ready")
        scores1, biased1 = signal("scores1", TILES), signal("biased1", TILES)
        maxima1, shifted1, exps1 = signal("maxima1", TILES), signal("shifted1", TILES), signal("exps1", TILES)
        sums1, inverses1, probs1 = signal("sums1", TILES), signal("inverses1", TILES), signal("probs1", TILES)
        pT1_ps, pT1_a, pT1_b = signal("pT1_ps", 2 * TILES), signal("pT1_a", TILES), signal("pT1_b", TILES)
        mixed1, summed1 = signal("mixed1", TILES), signal("summed1", TILES)
        relu_done = signal("relu_done")

        small = [(ident[:, :], d["ident"]), (mean_col[:, :], d["mean_col"]), (hmask4[:, :], d["hmask4"]),
                 (hmask8[:, :], d["hmask8"]), (seq_ind[:, :], d["seq_ind"]), (colb[:, :], d["colb"]),
                 (lnw[:, :, :], d["lnw"]), (edge_w[:, :], d["edge_w"]), (edge_b[:, :], d["edge_b"]),
                 (pos_i[:, :], d["pos"]), (freq[:, :], d["freq"]),
                 (cond[:, :, :], d["condT"].rearrange("(c p) b -> p c b", p=P)),
                 (wk1[:, :, :], d["k1"].rearrange("(c p) n -> p c n", p=P)),
                 (wo1[:, :, :], d["out1"].rearrange("(c p) n -> p c n", p=P))]
        staged = [(d[k].rearrange("(c p) n -> p c n", p=P), c * n) for k, (c, n) in WEIGHTS.items()]
        staged += [(d["adaln"][c * P:(c + 1) * P, :], NMOD * P) for c in range(DC)]
        NW = len(WEIGHTS)
        x_v = d["xT"].rearrange("(c p) t -> p c t", p=P)
        out_v = d["outT"].rearrange("(c p) t -> p c t", p=P)
        adj_v = d["adj"].rearrange("(n p) e -> p n e", p=P)
        names = list(WEIGHTS)

        def stage_view(k):
            shape = WEIGHTS[names[k]]
            return stage[k % 2][:, 0:shape[0] * shape[1]].rearrange("p (c n) -> p c n", n=shape[1])

        block = ctx.enter_context(nc.Block())

        @block.sync
        def _(sp):
            for dst, src in small:
                sp.dma_start(dst, src).then_inc(consts_in.sem, 16)
            for k, (src, n) in enumerate(staged):
                if k >= 2:
                    sp.wait_ge(weight_lo.sem, k - 1)
                if k < NW:
                    sp.dma_start(stage_view(k), src).then_inc(stage_in[k % 2].sem, 16)
                else:
                    sp.dma_start(stage[k % 2][:, 0:n], src).then_inc(stage_in[k % 2].sem, 16)
            sp.wait_ge(mods_ps.sem, NMOD)
            sp.dma_start(stage[0][:, 0:DC * D].rearrange("p (c n) -> p c n", n=D),
                         d["self_cond"].rearrange("(c p) n -> p c n", p=P)).then_inc(stage_in[0].sem, 16)

            def load_x(m, n):
                wait_last(sp, normed[0], m)
                sp.dma_start(x_in[:, :, :], x_v[:, :, bass.ds(m * MT, MT)]).then_inc(x_in_s.sem, 16)

            def load_residual(m, n):
                wait_last(sp, x1_done, m)
                sp.dma_start(x_res[:, :, :], x_v[:, :, bass.ds(m * MT, MT)]).then_inc(x_res_s.sem, 16)

            def load_edges(m, n):
                if n > 0:
                    return
                wait_last(sp, edge_weighted, m)
                sp.dma_start(adj[:, :, :, :].rearrange("p n e l -> p n (e l)"),
                             adj_v[:, bass.ds(m * TILES, TILES), :]).then_inc(adj_s.sem, 16)

            def store(m, n):
                wait(sp, relu_done, m, 1)
                sp.dma_start(out_v[:, :, bass.ds(m * MT, MT)], sf[:, :, :]).then_inc(out_s.sem, 16)

            run_steps(sp, "SP", {"norm0_mean": load_x, "norm0_apply": load_residual, "mlp_up": load_edges, "out": store})
            wait(sp, out_s, NM, 0)

        @block.tensor
        def _(pe):
            def linear(out, terms):
                for i, (lhsT, rhs) in enumerate(terms):
                    last = nc.tensor.matmul(out, lhsT, rhs, start=i == 0, stop=i == len(terms) - 1)
                return last

            def fm_terms(k, cols, hi, lo, chunks):
                return [(w[:, c, cols], a[:, c, :]) for c in range(chunks)
                        for w, a in ((wl[k], hi), (wh[k], lo), (wh[k], hi))]

            pe.wait_ge(consts_in.sem, 16 * len(small))
            pe.wait_ge(cond_ready.sem, 1)
            for c in range(DC):
                pe.wait_ge(stage_in[(NW + c) % 2].sem, 16 * ((NW + c) // 2 + 1))
            ps = [lin[0][:, :, :], lin[1][:, :, :], tr[0][:, :, :]]
            for j in range(NMOD):
                out = ps[j // 4].rearrange("p a b -> p (a b)")[:, (j % 4) * P:(j % 4 + 1) * P]
                for c in range(DC):
                    last = nc.tensor.matmul(out, stage[(NW + c) % 2][:, j * P:(j + 1) * P], cond_s[:, c, :],
                                            start=c == 0, stop=c == DC - 1)
                last.then_inc(mods_ps.sem, 1)
            pe.wait_ge(stage_in[0].sem, 16 * ((NW + DC + 1) // 2 + 1))
            w_cond = stage[0][:, 0:DC * D].rearrange("p (c n) -> p c n", n=D)
            for o in range(DC):
                for c in range(DC):
                    last = nc.tensor.matmul(ao_ps[:, 0, o * P:(o + 1) * P], w_cond[:, c, o * P:(o + 1) * P],
                                            cond[:, c, :], start=c == 0, stop=c == DC - 1)
                last.then_inc(mods_ps.sem, 1)
            pe.wait_ge(weight_hi.sem, NW)
            pe.wait_ge(weight_lo.sem, NW)
            pe.wait_ge(zeros_set.sem, 5)
            pe.wait_ge(mods_set.sem, NMOD + DC)

            def norm_mean(norm):
                def step(m, n):
                    wait(pe, squares[norm], m, 1)
                    if norm == 0:
                        wait_last(pe, mixed_lo, m)
                        wait(pe, normed[1], m - 1, 0)
                    elif not isinstance(m, int) or m < NM - 1:
                        wait(pe, normed[0], m + 1, 1)
                    else:
                        wait(pe, mixed_lo, m, TILES)
                    for t in range(TILES):
                        for c in range(DC):
                            last = nc.tensor.matmul(ms_ps[:, t:t + 1], xn[norm][:, c, t * P:(t + 1) * P],
                                                    mean_col[:, :], start=c == 0, stop=c == DC - 1)
                    last.then_inc(means[norm].sem, 1)
                return step

            def norm_apply(norm):
                def step(m, n):
                    wait(pe, inverses[norm], m, 1)
                    for t in range(TILES):
                        last = nc.tensor.matmul(spread_ps[:, t * P:(t + 1) * P],
                                                rms_inv[norm][:, t:t + 1].to_broadcast([P, P]), ident[:, :],
                                                start=True, stop=True)
                    last.then_inc(spread[norm].sem, 1)
                return step

            def qkv(m, t):
                if t == 0:
                    wait(pe, normed_hi[0], m, 1)
                    wait(pe, normed_lo[0], m, 1)
                    wait_last(pe, proj_gated, m)
                else:
                    wait_last(pe, pT_a, m)
                    wait_last(pe, pT_b, m)
                qk_ps, v_ps = qkv_ps[t]
                rows = slice(t * P, (t + 1) * P)
                terms = [(a[:, c, rows], w[:, c, :]) for c in range(DC)
                         for a, w in ((nh[0], wl["qkv"]), (nl[0], wh["qkv"]), (nh[0], wh["qkv"]))]
                linear(qk_ps, [(a, w[:, 0:2 * D]) for a, w in terms])
                linear(v_ps, [(a, w[:, 2 * D:3 * D]) for a, w in terms]).then_inc(qkv_done.sem, 1)

            def heads(m, t):
                wait(pe, heads_split, m, t + 1)
                if t == 0:
                    wait(pe, v_kept, m, TILES)
                    wait(pe, qk_kept, m, TILES)
                else:
                    wait(pe, kT_kept, m, t)
                    wait(pe, qT_kept, m, t)
                for g in range(NG):
                    last = nc.tensor.transpose(tr[0][:, g, :], qd[:, g, :, :].rearrange("p s f -> p (s f)"), ident[:, :])
                last.then_inc(qT_ps.sem, 1)
                for g in range(NG):
                    last = nc.tensor.transpose(tr[1][:, g, :], kd[:, g, :, :].rearrange("p s f -> p (s f)"), ident[:, :])
                last.then_inc(kT_ps.sem, 1)

            def score(m, t):
                wait(pe, qT_kept, m, t + 1)
                wait(pe, k_spread, m, t + 1)
                if t == 0:
                    wait(pe, qk_kept, m, 1)
                    wait(pe, v_kept, m, 1)
                else:
                    wait(pe, shifted_s, m, t)
                for g in range(NG):
                    last = nc.tensor.matmul(s0_ps[:, g // 2, (g % 2) * 4 * S:(g % 2 + 1) * 4 * S], qT[t][:, g, :],
                                            kbd[:, t, g, :, :].rearrange("p h s -> p (h s)"), start=True, stop=True)
                last.then_inc(scores.sem, 1)

            def probs_t(m, t):
                wait(pe, probs, m, t + 1)
                wait(pe, qT_kept, m, TILES)
                wait(pe, kT_kept, m, TILES)
                if t > 0:
                    wait(pe, pT_a, m, t)
                    wait(pe, pT_b, m, t)
                for j in range(NJ):
                    last = nc.tensor.transpose(tr[j // 4][:, j % 4, :],
                                               e0[t][:, 2 * j:2 * j + 2, :].rearrange("p h s -> p (h s)"), ident[:, :])
                    if j % 4 == 3:
                        last.then_inc(pT_ps.sem, 1)

            def mix(m, t):
                wait(pe, pT_a, m, t + 1)
                wait(pe, pT_b, m, t + 1)
                wait(pe, v_kept, m, t + 1)
                if t > 0:
                    wait(pe, mixed_lo, m, t)
                else:
                    wait(pe, normed[0], m, 1)
                    wait_last(pe, normed[1], m)
                for j in range(NJ):
                    for s in range(2):
                        f = 32 * (j % 4)
                        last = nc.tensor.matmul(ao_ps[f:f + 32, 0, (j // 4) * P + s * S:(j // 4) * P + (s + 1) * S],
                                                vb[:, t, j, s, :, :].rearrange("p h f -> p (h f)"),
                                                pT0[:, j, s * S:(s + 1) * S], start=True, stop=True,
                                                tile_position=(0, f))
                last.then_inc(mixed.sem, 1)

            def proj(m, n):
                wait(pe, mixed_hi, m, TILES)
                wait(pe, mixed_lo, m, TILES)
                wait(pe, shifted_s, m, TILES)
                for o in range(DC):
                    last = linear(s0_ps[:, 0, o * MT:(o + 1) * MT],
                                  fm_terms("proj", slice(o * P, (o + 1) * P), aoh, aol, DC))
                last.then_inc(proj_done.sem, 1)

            def mlp_up(m, n):
                if n == 0:
                    wait(pe, normed_hi[1], m, 1)
                    wait(pe, normed_lo[1], m, 1)
                    wait_last(pe, pT1_a, m)
                    wait_last(pe, pT1_b, m)
                else:
                    wait(pe, z_silu, m, n)
                for k, name in enumerate(("w1", "w3")):
                    if k == 1 and n > 0:
                        wait(pe, g_done, m, n)
                    for c in range(2):
                        j = 2 * n + c
                        last = linear(lin[k][:, c, :], fm_terms(name, slice(j * P, (j + 1) * P), nh[1], nl[1], DC))
                    last.then_inc(z_done.sem, 1)

            def mlp_down(m, n):
                wait(pe, g_hi, m, MC // 2)
                wait(pe, g_lo, m, MC // 2)
                for o in range(DC):
                    last = linear(lin[0][:, o, :], fm_terms("w2", slice(o * P, (o + 1) * P), gh, gl, MC))
                last.then_inc(down_done.sem, 1)

            def self_feat(m, n):
                wait(pe, x2_hi, m, 1)
                wait(pe, x2_lo, m, 1)
                linear(lin[1][:, 0, :], [(ones_r[:, :], a[:, c, :]) for c in range(DC) for a in (nl[1], nh[1])])\
                    .then_inc(rowsum.sem, 1)
                for o in range(DC):
                    last = linear(lin[0][:, o, :], fm_terms("self", slice(o * P, (o + 1) * P), nh[1], nl[1], DC))
                last.then_inc(self_ps.sem, 1)

            def k1(m, n):
                wait(pe, kv_kept, m, 1)
                wait(pe, row_gate, m, 1)
                for k in range(ND * DC):
                    for c in range(DC):
                        last = nc.tensor.matmul(lin[1][:, k // 2, (k % 2) * P:(k % 2 + 1) * P],
                                                wk1[:, c, k * P:(k + 1) * P],
                                                kv[:, c, :, :].rearrange("p b k -> p (b k)"),
                                                start=c == 0, stop=c == DC - 1)
                last.then_inc(k1_ps.sem, 1)

            def q1(m, n):
                wait(pe, self_hi, m, 1)
                wait(pe, self_lo, m, 1)
                for direction in range(ND):
                    if direction == 1:
                        wait(pe, k1_kept, m, 1)
                    for o in range(DC):
                        k = direction * DC + o
                        last = linear(lin[direction][:, o, :],
                                      fm_terms("q1", slice(k * P, (k + 1) * P), nh[1], nl[1], DC))
                    last.then_inc(q1_ps.sem, 1)

            def v1(m, n):
                wait_last(pe, summed1, m)
                wait(pe, kv_kept, m, 1)
                linear(ao1_ps[:, :, :].rearrange("p a b -> p (a b)"),
                       [(kv[:, c, :, :].rearrange("p b k -> p (b k)"), wo1[:, c, :]) for c in range(DC)])\
                    .then_inc(v1_ps.sem, 1)

            def score1(m, t):
                if t == 0:
                    wait(pe, q1_kept, m, ND)
                    wait(pe, k1_spread, m, ND * DC)
                else:
                    wait(pe, pT1_a, m, t)
                    wait(pe, pT1_b, m, t)
                for direction in range(ND):
                    for c in range(DC):
                        for s in range(2):
                            b = 2 * t + s
                            last = nc.tensor.matmul(
                                s1_ps[direction][s * S:(s + 1) * S, c * 8 * NKV:(c + 1) * 8 * NKV],
                                q1T[:, direction, c, b * S:(b + 1) * S],
                                kbd1[:, direction * DC + c, b, :, :].rearrange("p h k -> p (h k)"),
                                start=True, stop=True)
                last.then_inc(scores1.sem, 1)

            def probs_t1(m, t):
                wait(pe, probs1, m, t + 1)
                for j in range(NJ):
                    last = nc.tensor.transpose(tr1[j // 4][:, j % 4, :],
                                               p1[:, j, :, :, :].rearrange("p a h k -> p (a h k)"), ident[:, :])
                    if j % 4 == 3:
                        last.then_inc(pT1_ps.sem, 1)

            def mix1(m, t):
                wait(pe, pT1_a, m, t + 1)
                wait(pe, pT1_b, m, t + 1)
                wait(pe, v1_kept, m, 1)
                if t > 0:
                    wait(pe, summed1, m, t)
                for j in range(NJ):
                    for s in range(2):
                        f = 32 * (j % 4)
                        last = nc.tensor.matmul(ao1_ps[f:f + 32, 0, (j // 4) * P + s * S:(j // 4) * P + (s + 1) * S],
                                                vb1[:, 2 * t + s, j, :, :].rearrange("p h f -> p (h f)"),
                                                pT1[:, j, s * S:(s + 1) * S], start=True, stop=True,
                                                tile_position=(0, f))
                last.then_inc(mixed1.sem, 1)

            run_steps(pe, "PE", {
                "norm0_mean": norm_mean(0), "norm1_mean": norm_mean(1), "norm0_apply": norm_apply(0),
                "norm1_apply": norm_apply(1), "qkv": qkv, "heads": heads, "score": score, "probsT": probs_t, "mix": mix, "proj": proj,
                "mlp_up": mlp_up, "mlp_down": mlp_down, "self": self_feat, "k1": k1,
                "q1": q1, "v1": v1, "score1": score1, "probsT1": probs_t1, "mix1": mix1,
            })

        @block.scalar
        def _(act):
            act.wait_ge(consts_in.sem, 16 * len(small))
            nc.scalar.activation(cond_t[:, :, :], cond[:, :, :], ACT.Tanh, scale=0.5).then_inc(cond_tanh.sem, 1)
            for k, name in enumerate(names):
                act.wait_ge(stage_in[k % 2].sem, 16 * (k // 2 + 1))
                nc.scalar.activation(wh[name][:, :, :], stage_view(k), ACT.Copy,
                                     scale=WEIGHT_SCALE.get(name, 1.0)).then_inc(weight_hi.sem, 1)
            act.wait_ge(table_step.sem, 8)
            nc.scalar.activation(ang[:, :, :], ang[:, :, :], ACT.Sin).then_inc(sines.sem, 1)
            act.wait_ge(biases_set.sem, 2)
            act.wait_ge(zeros_set.sem, 5)

            def norm_mean(norm):
                x = (x_in, x1)[norm]

                def step(m, n):
                    if norm == 0:
                        wait(act, x_in_s, m, 16)
                    else:
                        wait(act, x1_done, m, 1)
                    wait_last(act, normed_lo[norm], m)
                    wait_last(act, normed_hi[norm], m)
                    nc.scalar.activation(xn[norm][:, :, :], x[:, :, :], ACT.Square).then_inc(squares[norm].sem, 1)
                    wait(act, means[norm], m, 1)
                    nc.scalar.activation(rms_root[norm][:, :], ms_ps, ACT.Sqrt, bias=eps[:, :])\
                        .then_inc(roots[norm].sem, 1)
                return step

            def norm_apply(norm):
                def step(m, n):
                    wait(act, shifted[norm], m, 1)
                    wait_last(act, (qkv_done, q1_ps)[norm], m)
                    nc.scalar.activation(nh[norm][:, :, :], xn[norm][:, :, :], ACT.Copy).then_inc(normed_hi[norm].sem, 1)
                return step

            def qkv(m, t):
                wait(act, qkv_done, m, t + 1)
                qk_ps, v_ps = qkv_ps[t]
                wait(act, qk_sums, m, t)
                if t == 0:
                    wait_last(act, heads_split, m)
                nc.scalar.activation(qk_sq[:, :, :, :].rearrange("p a h f -> p (a h f)"), qk_ps, ACT.Square)\
                    .then_inc(qk_squares.sem, 1)
                if t == 0:
                    wait_last(act, cos_part, m)
                    wait_last(act, sin_part, m)
                    wait_last(act, mixed, m)
                nc.scalar.activation(qk[:, t, :, :, :].rearrange("p a h f -> p (a h f)"), qk_ps, ACT.Copy)\
                    .then_inc(qk_kept.sem, 1)
                v = v_ps.rearrange("p (j h f) -> p j h f", h=2, f=DH)
                for s in range(2):
                    for h in range(2):
                        last = nc.scalar.activation(vb[h * S:(h + 1) * S, t, :, s, h, :], v[s * S:(s + 1) * S, :, h, :],
                                                    ACT.Copy)
                last.then_inc(v_kept.sem, 1)

            def rope_scale(m, n):
                wait(act, qk_sums, m, TILES)
                wait_last(act, qk_inverses, m)
                nc.scalar.activation(qk_root[:, :, :], qk_ss[:, :, :], ACT.Sqrt, bias=eps[:, :], scale=1.0 / DH)\
                    .then_inc(qk_roots.sem, 1)

            def heads(m, t):
                wait(act, qT_ps, m, t + 1)
                wait(act, scores, m, t - TILES + 1)
                nc.scalar.activation(qT[t][:, :, :], tr[0][:, :, :], ACT.Copy).then_inc(qT_kept.sem, 1)
                wait(act, kT_ps, m, t + 1)
                wait(act, k_spread, m, t)
                for s in range(2):
                    last = nc.scalar.activation(kT[s * S:(s + 1) * S, :, :], tr[1][s * S:(s + 1) * S, :, s * S:(s + 1) * S],
                                                ACT.Copy)
                last.then_inc(kT_kept.sem, 1)

            def score(m, t):
                wait(act, shifted_s, m, t + 1)
                nc.scalar.activation(e0[t][:, :, :], e0[t][:, :, :], ACT.Exp, scale=DH ** -0.5).then_inc(exps.sem, 1)

            def probs_t(m, t):
                wait(act, pT_ps, m, 2 * t + 1)
                wait(act, mixed, m, t)
                nc.scalar.activation(pT0[:, 0:4, :], tr[0][:, :, :], ACT.Copy).then_inc(pT_a.sem, 1)

            def mix(m, t):
                wait(act, mixed, m, t + 1)
                wait_last(act, proj_done, m)
                nc.scalar.activation(aoh[:, :, t * P:(t + 1) * P],
                                     ao_ps[:, 0, :].rearrange("p (c t) -> p c t", c=DC), ACT.Copy)\
                    .then_inc(mixed_hi.sem, 1)

            def mlp_up(m, n):
                wait(act, z_done, m, 2 * n + 1)
                wait(act, z_silu, m, n)
                nc.scalar.activation(th[:, :, :], lin[0][:, :, :], ACT.Tanh, scale=0.5).then_inc(z_tanh.sem, 1)
                wait(act, g_done, m, n + 1)
                wait_last(act, down_done, m)
                nc.scalar.activation(gh[:, 2 * n:2 * n + 2, :], gf[:, :, :], ACT.Copy).then_inc(g_hi.sem, 1)

            def x2_split(m, n):
                wait(act, x2_done, m, 1)
                nc.scalar.activation(nh[1][:, :, :], x2[:, :, :], ACT.Copy).then_inc(x2_hi.sem, 1)

            def self_split(m, n):
                wait(act, self_done, m, DC)
                wait_last(act, v1_ps, m)
                nc.scalar.activation(kv[:, :, :, :], sf[:, :, :].rearrange("p c (b s) -> p c b s", s=S)[:, :, :, 0:NKP],
                                     ACT.Copy).then_inc(kv_kept.sem, 1)
                wait(act, x2_lo, m, 1)
                wait(act, self_ps, m, 1)
                nc.scalar.activation(nh[1][:, :, :], sf[:, :, :], ACT.Copy).then_inc(self_hi.sem, 1)

            def k1(m, n):
                wait(act, k1_ps, m, 1)
                wait_last(act, k1_spread, m)
                for k in range(ND * DC):
                    last = nc.scalar.activation(
                        k1T[:, k // 2, k % 2, :, :].rearrange("p b k -> p (b k)"),
                        lin[1][:, k // 2, (k % 2) * P:(k % 2 + 1) * P], ACT.Identity, bias=bk[:, k:k + 1])
                last.then_inc(k1_kept.sem, 1)

            def q1(m, n):
                wait_last(act, scores1, m)
                wait(act, edge_value, m, 1)
                for direction in range(ND):
                    wait(act, q1_ps, m, direction + 1)
                    for o in range(DC):
                        k = direction * DC + o
                        last = nc.scalar.activation(q1T[:, direction, o, :], lin[direction][:, o, :], ACT.Identity,
                                                    bias=bq4[:, k:k + 1], scale=DH ** -0.5)
                    last.then_inc(q1_kept.sem, 1)

            def v1(m, n):
                wait(act, v1_ps, m, 1)
                wait_last(act, mixed1, m)
                v = ao1_ps[:, :, :].rearrange("p a (j h f) -> p a j h f", h=2, f=DH)
                for b in range(MB):
                    for r in range(4):
                        last = nc.scalar.activation(vb1[r * NKP:(r + 1) * NKP, b, :, r % 2, :],
                                                    v[b * NKP:(b + 1) * NKP, r // 2, :, r % 2, :], ACT.Copy)
                last.then_inc(v1_kept.sem, 1)

            def score1(m, t):
                wait(act, shifted1, m, t + 1)
                nc.scalar.activation(e1[:, :, :, :], e1[:, :, :, :], ACT.Exp).then_inc(exps1.sem, 1)

            def probs_t1(m, t):
                wait(act, pT1_ps, m, 2 * t + 1)
                wait(act, mixed1, m, t)
                nc.scalar.activation(pT1[:, 0:4, :], tr1[0], ACT.Copy).then_inc(pT1_a.sem, 1)

            run_steps(act, "Activation", {
                "norm0_mean": norm_mean(0), "norm1_mean": norm_mean(1), "norm0_apply": norm_apply(0),
                "norm1_apply": norm_apply(1), "qkv": qkv, "rope_scale": rope_scale, "heads": heads, "score": score, "probsT": probs_t, "mix": mix,
                "mlp_up": mlp_up, "x2_split": x2_split, "self_split": self_split, "k1": k1, "q1": q1, "v1": v1,
                "score1": score1, "probsT1": probs_t1,
            })

        @block.vector
        def _(dve):
            nc.vector.memset(eps[:, :], EPS).then_inc(zeros_set.sem, 1)
            nc.vector.memset(ones_r[:, :].bitcast(F32), 1.0).then_inc(zeros_set.sem, 1)
            nc.vector.memset(ones_f[:, :], 1.0).then_inc(zeros_set.sem, 1)
            nc.vector.memset(vb[:, :, :, :, :, :].rearrange("p t j s h f -> p (t j s h f)"), 0.0).then_inc(zeros_set.sem, 1)
            nc.vector.memset(vb1[:, :, :, :, :].rearrange("p b j h f -> p (b j h f)"), 0.0).then_inc(zeros_set.sem, 1)
            nc.vector.memset(p1[:, :, :, :, :].rearrange("p j a h k -> p (j a h k)"), 0.0).then_inc(zeros_set.sem, 1)
            dve.wait_ge(consts_in.sem, 16 * len(small))
            dve.wait_ge(cond_tanh.sem, 1)
            nc.vector.scalar_tensor_tensor(cond_t[:, :, :], cond_t[:, :, :], 1.0, cond[:, :, :], ALU.add, ALU.mult)\
                .then_inc(table_step.sem, 1)
            dve.wait_ge(table_step.sem, 1)
            nc.vector.tensor_scalar(cond_s[:, :, :], cond_t[:, :, :], 0.5, None, ALU.mult).then_inc(cond_ready.sem, 1)
            nc.vector.tensor_copy(pos_f[:, :], pos_i[:, :]).then_inc(table_step.sem, 1)
            dve.wait_ge(table_step.sem, 2)
            nc.vector.tensor_scalar(ang[:, 0, :], freq[:, :], pos_f[:, :], None, ALU.mult)
            nc.vector.tensor_scalar(ang[:, 1, :], freq[:, :], pos_f[:, :], 1.5707963267948966, ALU.mult, ALU.add)\
                .then_inc(table_step.sem, 1)
            dve.wait_ge(table_step.sem, 3)
            nc.vector.tensor_scalar(turns_i[:, :, :], ang[:, :, :], 0.15915494309189535, None, ALU.mult)\
                .then_inc(table_step.sem, 1)
            dve.wait_ge(table_step.sem, 4)
            nc.vector.tensor_copy(turns[:, :, :], turns_i[:, :, :]).then_inc(table_step.sem, 1)
            for i, part in enumerate(TWO_PI_PARTS):
                dve.wait_ge(table_step.sem, 5 + i)
                last = nc.vector.scalar_tensor_tensor(ang[:, :, :], turns[:, :, :], -part, ang[:, :, :], ALU.mult, ALU.add)
                if i < 2:
                    last.then_inc(table_step.sem, 1)
                else:
                    last.then_inc(biases_set.sem, 1)
            dve.wait_ge(biases_set.sem, 1)
            nc.vector.tensor_scalar(ang[:, :, :], ang[:, :, :], 3.1415925, -3.1415925, ALU.min, ALU.max)\
                .then_inc(table_step.sem, 1)
            nc.vector.tensor_scalar(bq4[:, :], bq, DH ** -0.5, None, ALU.mult)
            nc.vector.tensor_tensor(bout[:, :], bo[:, 0:DC], bo[:, DC:2 * DC], ALU.add).then_inc(biases_set.sem, 1)
            for k, name in enumerate(names):
                dve.wait_ge(weight_hi.sem, k + 1)
                nc.vector.scalar_tensor_tensor(wl[name][:, :, :], stage_view(k), WEIGHT_SCALE.get(name, 1.0),
                                               wh[name][:, :, :].bitcast(F32), ALU.mult, ALU.subtract)\
                    .then_inc(weight_lo.sem, 1)
            dve.wait_ge(sines.sem, 1)
            half = DH // 2
            for i in range(2):
                for a in range(2):
                    nc.vector.tensor_tensor(cosw[:, i, a * half:(a + 1) * half], lnw[:, i, a * half:(a + 1) * half],
                                            ang[:, 1, :], ALU.mult)
                    last = nc.vector.scalar_tensor_tensor(sinw[:, i, a * half:(a + 1) * half], ang[:, 0, :],
                                                          (1.0, -1.0)[a], lnw[:, i, a * half:(a + 1) * half],
                                                          ALU.mult, ALU.mult)
            last.then_inc(table_step.sem, 1)
            ps = [lin[0], lin[1], tr[0]]
            for j in range(NMOD):
                dve.wait_ge(mods_ps.sem, 4 * (j // 4 + 1))
                one = 1.0 if j // DC in (SCALE_A // DC, SCALE_M // DC) else 0.0
                nc.vector.tensor_scalar(mods[:, j, :], ps[j // 4][:, :, :].rearrange("p a b -> p (a b)")[:, (j % 4) * P:(j % 4 + 1) * P],
                                        adaln_b[:, j:j + 1], one, ALU.add, ALU.add).then_inc(mods_set.sem, 1)
            for o in range(DC):
                dve.wait_ge(mods_ps.sem, NMOD + DC)
                nc.vector.tensor_copy(mods[:, COND + o, :], ao_ps[:, 0, o * P:(o + 1) * P]).then_inc(mods_set.sem, 1)
            dve.wait_ge(mods_set.sem, NMOD + DC)
            dve.wait_ge(table_step.sem, 9)
            dve.wait_ge(zeros_set.sem, 6)
            dve.wait_ge(biases_set.sem, 2)

            def per_seq(ap):
                return ap.unsqueeze(3).to_broadcast([P, ap.shape[1], MB, S])

            def by_seq(ap):
                return ap.rearrange("p c (b s) -> p c b s", s=S)

            def norm_mean(norm):
                def step(m, n):
                    wait(dve, roots[norm], m, 1)
                    nc.vector.reciprocal(rms_inv[norm][:, :], rms_root[norm][:, :]).then_inc(inverses[norm].sem, 1)
                return step

            def norm_apply(norm):
                x = (x_in, x1)[norm]
                shift, scale = ((SHIFT_A, SCALE_A), (SHIFT_M, SCALE_M))[norm]

                def step(m, n):
                    wait_last(dve, (proj_gated, cond_part)[norm], m)
                    nc.vector.tensor_tensor(mod[norm][:, :, :], mods[:, :, bass.ds(m * MB, MB)],
                                            ones_f[:, :].rearrange("p (c b) -> p c b", b=MB), ALU.mult)\
                        .then_inc(mod_set[norm].sem, 1)
                    wait(dve, spread[norm], m, 1)
                    nc.vector.tensor_tensor(xn[norm][:, :, :], x[:, :, :],
                                            spread_ps.unsqueeze(1).to_broadcast([P, DC, MT]), ALU.mult)\
                        .then_inc(normed[norm].sem, 1)
                    wait(dve, normed[norm], m, 1)
                    wait(dve, mod_set[norm], m, 1)
                    nc.vector.tensor_tensor(by_seq(xn[norm][:, :, :]), by_seq(xn[norm][:, :, :]),
                                            per_seq(mod[norm][:, scale:scale + DC, :]), ALU.mult)\
                        .then_inc(scaled[norm].sem, 1)
                    wait(dve, scaled[norm], m, 1)
                    nc.vector.tensor_tensor(by_seq(xn[norm][:, :, :]), by_seq(xn[norm][:, :, :]),
                                            per_seq(mod[norm][:, shift:shift + DC, :]), ALU.add)\
                        .then_inc(shifted[norm].sem, 1)
                return step

            def qkv(m, t):
                wait(dve, qk_squares, m, t + 1)
                if t == 0:
                    wait_last(dve, qk_roots, m)
                nc.vector.tensor_reduce(qk_ss[:, t, :], qk_sq[:, :, :, :].rearrange("p a h f -> p (a h) f"), AX.X, ALU.add)\
                    .then_inc(qk_sums.sem, 1)

            def rope_scale(m, n):
                wait(dve, qk_roots, m, 1)
                nc.vector.reciprocal(qk_inv[:, :, :], qk_root[:, :, :]).then_inc(qk_inverses.sem, 1)
                wait(dve, qk_inverses, m, 1)
                for s in range(2):
                    nc.vector.tensor_scalar(q_inv[:, s, :, :], qk_inv[:, :, 0:H], seq_ind[:, s:s + 1], None, ALU.mult)\
                        .then_inc(q_inverses.sem, 1)

            def rope(m, t):
                wait(dve, qk_kept, m, t + 1)
                nc.vector.tensor_tensor(qs[:, :, :, :], qk[:, t, :, :, :],
                                        sinw[:, :, :].unsqueeze(2).to_broadcast([P, 2, H, DH]), ALU.mult)\
                    .then_inc(sin_part.sem, 1)
                wait(dve, sin_part, m, t + 1)
                wait(dve, cos_part, m, t + 1)
                half = DH // 2
                for a in range(2):
                    nc.vector.tensor_tensor(qr[:, :, :, a * half:(a + 1) * half], qc[:, :, :, a * half:(a + 1) * half],
                                            qs[:, :, :, (1 - a) * half:(2 - a) * half], ALU.add).then_inc(rotated.sem, 1)
                wait(dve, rotated, m, 2 * t + 2)
                wait(dve, q_inverses, m, 2)
                wait(dve, kT_ps, m, t)
                qr_v = qr[:, :, :, :].rearrange("p a (g h) f -> p a g h f", g=NG)
                qd_v = qd[:, :, :, :].rearrange("p g s (h f) -> p g s h f", f=DH)
                for s in range(2):
                    nc.vector.tensor_tensor(qd_v[:, :, s, :, :], qr_v[:, 0, :, :, :],
                                            q_inv[:, s, t, :].rearrange("p (g h) -> p g h", g=NG).unsqueeze(3)
                                            .to_broadcast([P, NG, 4, DH]), ALU.mult)
                kd_v = kd[:, :, :, :].rearrange("p g s (h f) -> p g s h f", f=DH)
                for s in range(2):
                    last = nc.vector.tensor_tensor(kd_v[:, :, s, :, :], qr_v[:, 1, :, :, :],
                                                   qk_inv[:, t, H:2 * H].rearrange("p (g h) -> p g h", g=NG).unsqueeze(3)
                                                   .to_broadcast([P, NG, 4, DH]), ALU.mult)
                last.then_inc(heads_split.sem, 1)

            def score(m, t):
                wait(dve, scores, m, t + 1)
                s_v = s0_ps[:, :, :].rearrange("p a (h s) -> p (a h) s", s=S)
                nc.vector.tensor_reduce(mx0[:, :], s_v, AX.X, ALU.max).then_inc(maxima.sem, 1)
                wait(dve, maxima, m, t + 1)
                wait(dve, pT_ps, m, 2 * (t + 1 - TILES))
                nc.vector.tensor_tensor(e0[t][:, :, :], s_v, mx0[:, :].unsqueeze(2).to_broadcast([P, H, S]),
                                        ALU.subtract).then_inc(shifted_s.sem, 1)

            def soft(m, t):
                wait(dve, exps, m, t + 1)
                nc.vector.tensor_reduce(sum0[:, :], e0[t][:, :, :], AX.X, ALU.add).then_inc(exp_sums.sem, 1)
                wait(dve, exp_sums, m, t + 1)
                nc.vector.reciprocal(inv0[t][:, :], sum0[:, :]).then_inc(inv_sums.sem, 1)

            def probs_t(m, t):
                wait(dve, pT_ps, m, 2 * t + 2)
                wait(dve, mixed, m, t)
                nc.vector.tensor_copy(pT0[:, 4:8, :], tr[1][:, :, :]).then_inc(pT_b.sem, 1)

            def mix(m, t):
                wait(dve, mixed_hi, m, t + 1)
                wait_last(dve, proj_done, m)
                nc.vector.tensor_tensor(aol[:, :, t * P:(t + 1) * P], ao_ps[:, 0, :].rearrange("p (c t) -> p c t", c=DC),
                                        aoh[:, :, t * P:(t + 1) * P].bitcast(F32), ALU.subtract)\
                    .then_inc(mixed_lo.sem, 1)

            def proj(m, n):
                wait(dve, proj_done, m, 1)
                wait_last(dve, x2_done, m)
                for o in range(DC):
                    nc.vector.scalar_tensor_tensor(
                        by_seq(x1[:, o:o + 1, :])[:, 0], by_seq(s0_ps[:, 0:1, o * MT:(o + 1) * MT])[:, 0], proj_b[:, o:o + 1],
                        mod[0][:, GATE_A + o, :].unsqueeze(2).to_broadcast([P, MB, S]), ALU.add, ALU.mult)\
                        .then_inc(proj_gated.sem, 1)
                wait(dve, proj_gated, m, DC)
                wait(dve, x_res_s, m, 16)
                nc.vector.tensor_tensor(x1[:, :, :], x1[:, :, :], x_res[:, :, :], ALU.add).then_inc(x1_done.sem, 1)

            def mlp_up(m, n):
                wait(dve, z_tanh, m, n + 1)
                wait(dve, g_lo, m, n)
                wait(dve, g_hi, m, n)
                nc.vector.scalar_tensor_tensor(gf[:, :, :], th[:, :, :], 1.0, lin[0][:, :, :], ALU.add, ALU.mult)\
                    .then_inc(z_silu.sem, 1)
                wait(dve, z_silu, m, n + 1)
                wait(dve, z_done, m, 2 * n + 2)
                nc.vector.tensor_tensor(gf[:, :, :], gf[:, :, :], lin[1][:, :, :], ALU.mult).then_inc(g_done.sem, 1)

            def mlp_down(m, n):
                wait(dve, down_done, m, 1)
                wait_last(dve, relu_done, m)
                nc.vector.tensor_tensor(by_seq(x2[:, :, :]), by_seq(lin[0][:, :, :]),
                                        per_seq(mod[1][:, GATE_M:GATE_M + DC, :]), ALU.mult).then_inc(down_gated.sem, 1)
                wait(dve, down_gated, m, 1)
                nc.vector.tensor_tensor(x2[:, :, :], x2[:, :, :], x1[:, :, :], ALU.add).then_inc(x2_done.sem, 1)

            def self_feat(m, n):
                wait(dve, rowsum, m, 1)
                nc.vector.tensor_scalar(gate[:, :], lin[1][:, 0, :], 0.0, None, ALU.not_equal).then_inc(row_gate.sem, 1)
                wait(dve, row_gate, m, 1)
                wait_last(dve, Signal(out_s.sem, 16), m)
                nc.vector.tensor_tensor(by_seq(sf[:, :, :]),
                                        gate[:, :].rearrange("p (b s) -> p b s", s=S).unsqueeze(1).to_broadcast([P, DC, MB, S]),
                                        per_seq(mod[1][:, COND:COND + DC, :]), ALU.mult).then_inc(cond_part.sem, 1)
                wait(dve, cond_part, m, 1)
                wait(dve, self_ps, m, 1)
                for o in range(DC):
                    nc.vector.scalar_tensor_tensor(sf[:, o, :], lin[0][:, o, :], self_b[:, o:o + 1], sf[:, o, :],
                                                   ALU.add, ALU.add).then_inc(self_done.sem, 1)

            def edges(m, n):
                wait(dve, adj_s, m, 16)
                a = adj[:, :, :, :].rearrange("p t e l -> p (t e) l")
                w = adw
                wait_last(dve, scores1, m)
                flat = [v[:, :, :].rearrange("p t e -> p (t e)") for v in (edge_n, edge_v, edge_bias)]
                nc.vector.tensor_reduce(flat[0], a, AX.X, ALU.add).then_inc(edge_count.sem, 1)
                nc.vector.tensor_tensor(w, a, edge_w[:, :].unsqueeze(1).to_broadcast([P, TILES * NE, NL]), ALU.mult)\
                    .then_inc(edge_weighted.sem, 1)
                wait(dve, edge_weighted, m, 1)
                wait(dve, edge_count, m, 1)
                nc.vector.tensor_reduce(flat[1], w, AX.X, ALU.add).then_inc(edge_value.sem, 1)
                nc.vector.tensor_scalar(flat[0], flat[0], 0.0, NEG, ALU.is_le, ALU.mult).then_inc(edge_masked.sem, 1)
                wait(dve, edge_masked, m, 1)
                nc.vector.scalar_tensor_tensor(flat[2], flat[1], edge_b[:, :], flat[0], ALU.add, ALU.add)\
                    .then_inc(edge_ready.sem, 1)

            def k1(m, n):
                wait(dve, k1_kept, m, 1)
                wait_last(dve, scores1, m)
                for k in range(ND * DC):
                    nc.vector.tensor_tensor(kbd1[:, k, :, :, :],
                                            k1T[:, k // 2, k % 2, :, 0:NKV].unsqueeze(2).to_broadcast([P, MB, 8, NKV]),
                                            hmask8[:, :].unsqueeze(1).unsqueeze(3).to_broadcast([P, MB, 8, NKV]),
                                            ALU.mult).then_inc(k1_spread.sem, 1)

            def score1(m, t):
                wait(dve, scores1, m, t + 1)
                wait(dve, edge_ready, m, 1)
                wait(dve, probs1, m, t)
                for direction in range(ND):
                    last = nc.vector.tensor_tensor(
                        e1[:, direction, :, :], s1_ps[direction][:, 0:H * NKV].rearrange("p (h k) -> p h k", k=NKV),
                        edge_bias[:, t, direction * NKV:(direction + 1) * NKV].unsqueeze(1).to_broadcast([P, H, NKV]),
                        ALU.add)
                last.then_inc(biased1.sem, 1)
                wait(dve, biased1, m, t + 1)
                e_v = e1[:, :, :, :].rearrange("p a h k -> p (a h) k")
                mx_v = mx1[:, :, :].rearrange("p a h -> p (a h)")
                nc.vector.tensor_reduce(mx_v, e_v, AX.X, ALU.max).then_inc(maxima1.sem, 1)
                wait(dve, maxima1, m, t + 1)
                nc.vector.tensor_tensor(e_v, e_v, mx_v.unsqueeze(2).to_broadcast([P, ND * H, NKV]), ALU.subtract)\
                    .then_inc(shifted1.sem, 1)

            def soft1(m, t):
                wait(dve, exps1, m, t + 1)
                sum_v, inv_v = (v[:, :, :].rearrange("p a h -> p (a h)") for v in (sum1, inv1))
                nc.vector.tensor_reduce(sum_v, e1[:, :, :, :].rearrange("p a h k -> p (a h) k"), AX.X, ALU.add).then_inc(sums1.sem, 1)
                wait(dve, sums1, m, t + 1)
                nc.vector.reciprocal(inv_v, sum_v).then_inc(inverses1.sem, 1)

            def probs_t1(m, t):
                wait(dve, pT1_ps, m, 2 * t + 2)
                wait(dve, mixed1, m, t)
                nc.vector.tensor_copy(pT1[:, 4:8, :], tr1[1]).then_inc(pT1_b.sem, 1)

            def mix1(m, t):
                wait(dve, mixed1, m, t + 1)
                for c in range(DC):
                    last = nc.vector.scalar_tensor_tensor(sf[:, c, t * P:(t + 1) * P], ao1_ps[:, 0, c * P:(c + 1) * P],
                                                          bout[:, c:c + 1], sf[:, c, t * P:(t + 1) * P], ALU.add, ALU.add)
                last.then_inc(summed1.sem, 1)

            def out(m, n):
                wait(dve, summed1, m, TILES)
                nc.vector.scalar_tensor_tensor(sf[:, :, :], sf[:, :, :], 0.0, x2[:, :, :], ALU.max, ALU.add)\
                    .then_inc(relu_done.sem, 1)

            run_steps(dve, "DVE", {
                "norm0_mean": norm_mean(0), "norm1_mean": norm_mean(1), "norm0_apply": norm_apply(0),
                "norm1_apply": norm_apply(1), "qkv": qkv, "rope_scale": rope_scale,
                "rope": rope, "score": score, "soft": soft, "probsT": probs_t, "mix": mix, "proj": proj,
                "mlp_up": mlp_up, "mlp_down": mlp_down, "self": self_feat, "edges": edges,
                "k1": k1, "score1": score1, "soft1": soft1, "probsT1": probs_t1, "mix1": mix1, "out": out,
            })

        @block.gpsimd
        def _(pool):
            pool.wait_ge(zeros_set.sem, 6)
            pool.wait_ge(table_step.sem, 9)
            pool.wait_ge(mods_set.sem, NMOD + DC)

            def low_part(out, full, hi):
                return nc.gpsimd.tensor_tensor(out, full, hi.bitcast(F32), ALU.subtract)

            def norm_apply(norm):
                def step(m, n):
                    wait(pool, normed_hi[norm], m, 1)
                    low_part(nl[norm][:, :, :], xn[norm][:, :, :], nh[norm][:, :, :])\
                        .then_inc(normed_lo[norm].sem, 1)
                return step

            def rope(m, t):
                wait(pool, qk_kept, m, t + 1)
                wait(pool, rotated, m, 2 * t)
                nc.gpsimd.tensor_tensor(qc[:, :, :, :], qk[:, t, :, :, :],
                                        cosw[:, :, :].unsqueeze(2).to_broadcast([P, 2, H, DH]), ALU.mult)\
                    .then_inc(cos_part.sem, 1)

            def heads(m, t):
                wait(pool, kT_kept, m, t + 1)
                wait(pool, scores, m, t + 1 - TILES)
                nc.gpsimd.tensor_tensor(kbd[:, t, :, :, :], kT[:, :, :].unsqueeze(2).to_broadcast([P, NG, 4, S]),
                                        hmask4[:, :].unsqueeze(1).unsqueeze(3).to_broadcast([P, NG, 4, S]), ALU.mult)\
                    .then_inc(k_spread.sem, 1)

            def soft(m, t):
                wait(pool, inv_sums, m, t + 1)
                nc.gpsimd.tensor_tensor(e0[t][:, :, :], e0[t][:, :, :],
                                        inv0[t][:, :].unsqueeze(2).to_broadcast([P, H, S]), ALU.mult)\
                    .then_inc(probs.sem, 1)

            def mlp_up(m, n):
                wait(pool, g_hi, m, n + 1)
                low_part(gl[:, 2 * n:2 * n + 2, :], gf[:, :, :], gh[:, 2 * n:2 * n + 2, :]).then_inc(g_lo.sem, 1)

            def x2_split(m, n):
                wait(pool, x2_hi, m, 1)
                low_part(nl[1][:, :, :], x2[:, :, :], nh[1][:, :, :]).then_inc(x2_lo.sem, 1)

            def self_split(m, n):
                wait(pool, self_hi, m, 1)
                low_part(nl[1][:, :, :], sf[:, :, :], nh[1][:, :, :]).then_inc(self_lo.sem, 1)

            def soft1(m, t):
                wait(pool, inverses1, m, t + 1)
                wait(pool, pT1_ps, m, 2 * t)
                for direction in range(ND):
                    last = nc.gpsimd.tensor_tensor(
                        p1[:, :, direction, :, 0:NKV], e1[:, direction, :, :].rearrange("p (j h) k -> p j h k", h=2),
                        inv1[:, direction, :].rearrange("p (j h) -> p j h", h=2).unsqueeze(3).to_broadcast([P, NJ, 2, NKV]),
                        ALU.mult)
                last.then_inc(probs1.sem, 1)

            run_steps(pool, "Pool", {
                "norm0_apply": norm_apply(0), "norm1_apply": norm_apply(1), "rope": rope, "heads": heads,
                "soft": soft, "mlp_up": mlp_up, "x2_split": x2_split, "self_split": self_split, "soft1": soft1,
            })


def kernel(**inputs):
    import numpy as np

    from concourse import bacc
    from concourse.bass_utils import run_bass_kernel_spmd

    a = {k: np.asarray(v) for k, v in inputs.items()}

    def col(v):
        return v.reshape(-1, P).T

    def padded(v, axis):
        pad = [(0, 0), (0, 0)]
        pad[axis] = (0, MC * P - HM)
        return np.pad(v, pad)

    def rows(v):
        return np.broadcast_to(v, (P, *v.shape))

    adj = a["mask_BxSxSx11_ik0"]
    part = np.arange(P)
    arrays = {
        "xT": a["x"].reshape(B * S, D).T,
        "condT": a["cond_1024"].T,
        "pos": np.tile(a["pos_S"], 2).reshape(P, 1),
        "adj": np.stack([adj[:, :, :NKV], adj[:, :NKV].transpose(0, 2, 1, 3)], 2).reshape(B * S, NE * NL),
        "adaln": a["L0_cond_adaln_w"], "qkv": a["L0_cond_qkv_w"], "proj": a["L0_cond_proj_w"],
        "w1": padded(a["L0_cond_w1_w"], 1), "w3": padded(a["L0_cond_w3_w"], 1), "w2": padded(a["L0_cond_w2_w"], 0),
        "self": a["L1_cond_W_self"].T[:D], "self_cond": a["L1_cond_W_self"].T[D:],
        "q1": np.concatenate([w.T for w in a["L1_cond_Wq"]], 1),
        "k1": np.concatenate([w.T for w in a["L1_cond_Wk"]], 1),
        "out1": np.concatenate([w.reshape(D, D).T for w in a["L1_cond_Wout"]], 1),
        "colb": np.concatenate([col(a[k]) for k in ("L0_cond_adaln_b", "L0_cond_proj_b", "L1_cond_b_self",
                                                    "L1_cond_bq", "L1_cond_bk", "L1_cond_bout")], 1),
        "lnw": rows(np.stack([a["L0_cond_lnq_w"], a["L0_cond_lnk_w"]])),
        "edge_w": rows(a["L1_cond_w_bias"]), "edge_b": rows(a["L1_cond_b_bias"].reshape(1)),
        "ident": np.eye(P, dtype=np.float32),
        "mean_col": np.full((P, 1), 1.0 / D, np.float32),
        "hmask4": (part[:, None] % 64 // DH == np.arange(4)).astype(np.float32),
        "hmask8": (part[:, None] // DH == np.arange(8)).astype(np.float32),
        "seq_ind": (part[:, None] // S == np.arange(2)).astype(np.float32),
        "freq": np.broadcast_to((1.0 / 10000.0 ** (np.arange(DH // 2, dtype=np.float32) / (DH // 2)))
                                .astype(np.float32), (P, DH // 2)),
    }
    arrays = {k: np.ascontiguousarray(v) for k, v in arrays.items()}
    nc = bacc.Bacc("TRN2", target_bir_lowering=False, num_devices=1)
    d = {k: nc.dram_tensor(f"in_{k}", v.shape, mybir.dt.from_np(v.dtype), kind="ExternalInput").ap()
         for k, v in arrays.items()}
    d["outT"] = nc.dram_tensor("out_T", (D, B * S), F32, kind="ExternalOutput").ap()
    build_program(nc, d)
    r = run_bass_kernel_spmd(nc, [{f"in_{k}": v for k, v in arrays.items()}], core_ids=[0])
    return r.results[0]["out_T"].T.reshape(B, S, D)
```

```python
from contextlib import ExitStack

import concourse.bass as bass
from concourse import mybir

F32 = mybir.dt.float32
F32R = mybir.dt.float32r
I32 = mybir.dt.int32
ALU = mybir.AluOpType
ACT = mybir.ActivationFunctionType
AX = mybir.AxisListType

P = 128
B, S, D = 128, 64, 256
H, DH = 16, 16
HM = 704
NKV = 20
NKP = 32
NL = 11
EPS = 1e-6
NEG = -9000000000000000.0
DC = D // P
MC = -(-HM // P)
MB = 4
MT = MB * S
TILES = MT // P
NM = B // MB
NJ = H // 2
NG = H // 4
ND = 2
NE = ND * NKV
NMOD = 6 * DC
SHIFT_A, SCALE_A, GATE_A, SHIFT_M, SCALE_M, GATE_M = range(0, NMOD, DC)
K1_ON_POOL = 2
COND = NMOD
TWO_PI_PARTS = (6.28125, 0.0019350051879882812, 3.019916e-7)
WEIGHTS = {"qkv": (DC, 3 * D), "proj": (DC, D), "w1": (DC, MC * P), "w3": (DC, MC * P), "w2": (MC, D),
           "self": (DC, D), "q1": (DC, ND * D)}
WEIGHT_SCALE = {"w2": 0.5}

ORDER = {
    "PE": [
        (0, "mlp_up", 0), (1, "heads", 0), (0, "mlp_up", 1), (1, "score", 0), (1, "heads", 1), (0, "mlp_up", 2),
        (1, "score", 1), (0, "mlp_down", 0), (1, "probsT", 0), (1, "mix", 0), (2, "norm0_mean", 0), (0, "self", 0),
        (1, "probsT", 1), (2, "norm0_apply", 0), (1, "mix", 1), (0, "k1", 0), (1, "proj", 0), (0, "q1", 0),
        (0, "v1", 0), (0, "score1", 0), (1, "norm1_mean", 0), (0, "score1", 1), (2, "qkv", 0),
        (1, "norm1_apply", 0), (2, "qkv", 1), (0, "probsT1", 0), (0, "mix1", 0), (0, "probsT1", 1), (0, "mix1", 1),
    ],
    "DVE": [
        (0, "mlp_up", 0), (1, "rope", 1), (0, "mlp_up", 1), (1, "score_max", 0), (1, "score", 0), (0, "mlp_up", 2),
        (1, "soft", 0), (1, "soft_inverse", 0), (1, "score_max", 1), (1, "score", 1), (0, "mlp_down", 0),
        (1, "soft", 1), (1, "soft_inverse", 1), (0, "edges", 0), (0, "row_mask", 0), (1, "mix", 0),
        (2, "norm0_mean", 0), (0, "self", 0), (1, "mix", 1), (0, "edge_masks", 0), (1, "proj", 0),
        (2, "norm0_apply", 0), (2, "norm0_scale", 0), (0, "k1", 0), (2, "norm0_shift", 0), (0, "score1_bias", 0),
        (0, "score1_max", 0), (0, "score1", 0), (0, "score1_bias", 1), (1, "norm1_mean", 0), (0, "score1_max", 1),
        (0, "soft1", 0), (0, "score1", 1), (0, "soft1_inverse", 0), (2, "qkv", 0), (1, "norm1_apply", 0),
        (0, "soft1", 1), (1, "norm1_scale", 0), (0, "soft1_inverse", 1), (2, "qkv", 1), (1, "norm1_shift", 0),
        (2, "rope_scale", 0), (0, "mix1", 0), (2, "rope", 0), (0, "mix1", 1), (0, "out", 0),
    ],
    "Activation": [
        (0, "mlp_up", 0), (1, "heads", 0), (0, "mlp_split", 0), (0, "mlp_up", 1), (0, "mlp_split", 1),
        (1, "heads", 1), (0, "mlp_up", 2), (0, "mlp_split", 2), (1, "score", 0), (1, "score", 1), (1, "probsT", 0),
        (2, "norm0_mean", 0), (0, "x2_split", 0), (2, "norm0_root", 0), (1, "mix", 0), (1, "probsT", 1),
        (0, "self_split", 0), (1, "mix", 1), (0, "k1", 0), (0, "q1", 0), (1, "norm1_mean", 0),
        (2, "norm0_apply", 0), (0, "v1", 0), (1, "norm1_root", 0), (0, "score1", 0), (2, "qkv", 0),
        (0, "score1", 1), (2, "qkv", 1), (0, "probsT1", 0), (2, "rope_scale", 0), (1, "norm1_apply", 0),
        (0, "probsT1", 1),
    ],
    "Pool": [
        (1, "rope", 1), (1, "heads", 0), (0, "mlp_up", 0), (0, "mlp_up", 1), (1, "heads", 1), (0, "mlp_up", 2),
        (1, "soft", 0), (0, "mlp_down", 0), (0, "x2_split", 0), (1, "soft", 1), (0, "self", 0),
        (0, "self_split", 0), (0, "k1", 0), (1, "proj", 0), (2, "norm0_apply", 0), (0, "soft1", 0), (0, "soft1", 1),
        (2, "rope", 0), (1, "norm1_apply", 0),
    ],
    "SP": [
        (2, "norm0_mean", 0), (1, "mlp_up", 0), (0, "out", 0), (2, "norm0_apply", 0),
    ],
}


class Signal:

    def __init__(self, sem, per):
        self.sem, self.per = sem, per


def wait(engine, signal, m, n):
    value = m * signal.per + n
    if not isinstance(value, int) or value > 0:
        engine.wait_ge(signal.sem, value)


def wait_last(engine, signal, m):
    wait(engine, signal, m, 0)


def run_steps(engine, name, steps):
    ahead = max(a for order in ORDER.values() for a, _, _ in order)

    def take(m):
        for a, step, n in ORDER[name]:
            if step in steps and (not isinstance(m, int) or 0 <= m + a < NM):
                steps[step](m + a, n)

    for m in range(-ahead, 1):
        take(m)
    with engine.Fori(1, NM - ahead) as m:
        take(m)
    for m in range(NM - ahead, NM):
        take(m)


def build_program(nc, d):
    with ExitStack() as ctx:
        def sb(name, shape, dt=F32):
            return ctx.enter_context(nc.sbuf_tensor(name, shape, dt))

        def signal(name, per=1):
            return Signal(ctx.enter_context(nc.semaphore(name)), per)

        ident = sb("ident", [P, P])
        mean_col = sb("mean_col", [P, 1])
        ones_r = sb("ones_r", [P, P], F32R)
        ones_f = sb("ones_f", [P, 56])
        hmask4 = sb("hmask4", [P, 4])
        hmask8 = sb("hmask8", [P, 8])
        seq_ind = sb("seq_ind", [P, 2])
        eps = sb("eps", [P, 1])
        wh = {k: sb(f"{k}_hi", [P, *s], F32R) for k, s in WEIGHTS.items()}
        wl = {k: sb(f"{k}_lo", [P, *s], F32R) for k, s in WEIGHTS.items()}
        wk1 = sb("wk1", [P, DC, ND * D])
        wo1 = sb("wo1", [P, DC, ND * D])
        mods = sb("mods", [P, NMOD + DC, B])
        colb = sb("colb", [P, NMOD + 2 * DC + 3 * ND * DC])
        adaln_b, proj_b = colb[:, 0:NMOD], colb[:, NMOD:NMOD + DC]
        self_b = colb[:, NMOD + DC:NMOD + 2 * DC]
        bq, bk, bo = (colb[:, NMOD + 2 * DC + i * ND * DC:NMOD + 2 * DC + (i + 1) * ND * DC] for i in range(3))
        bq4 = sb("bq4", [P, ND * DC])
        bout = sb("bout", [P, DC])
        lnw = sb("lnw", [P, 2, DH])
        edge_w = sb("edge_w", [P, NL])
        edge_b = sb("edge_b", [P, 1])
        pos_i = sb("pos_i", [P, 1], I32)
        pos_f = sb("pos_f", [P, 1])
        freq = sb("freq", [P, DH // 2])
        ang = sb("ang", [P, 2, DH // 2])
        turns_i = sb("turns_i", [P, 2, DH // 2], I32)
        turns = sb("turns", [P, 2, DH // 2])
        cosw = sb("cosw", [P, 2, DH])
        sinw = sb("sinw", [P, 2, DH])

        xn = [sb(f"xn{i}", [P, DC, MT]) for i in range(2)]
        rms_root = [sb(f"rms_root{i}", [P, TILES]) for i in range(2)]
        rms_inv = [sb(f"rms_inv{i}", [P, TILES]) for i in range(2)]
        mod = [sb(f"mod{i}", [P, NMOD + DC, MB]) for i in range(2)]
        nh = [sb(f"nh{i}", [P, DC, MT], F32R) for i in range(2)]
        nl = [sb(f"nl{i}", [P, DC, MT], F32R) for i in range(2)]

        x_in = sb("x_in", [P, DC, MT])
        x_res = sb("x_res", [P, DC, MT])
        x1 = sb("x1", [P, DC, MT])
        qk = sb("qk", [P, TILES, 2, H, DH])
        qk_sq = sb("qk_sq", [P, 2, H, DH])
        qk_ss = sb("qk_ss", [P, TILES, 2 * H])
        qk_root = sb("qk_root", [P, TILES, 2 * H])
        qk_inv = sb("qk_inv", [P, TILES, 2 * H])
        q_inv = sb("q_inv", [P, 2, TILES, H])
        qc = sb("qc", [P, 2, H, DH])
        qs = sb("qs", [P, 2, H, DH])
        qr = qk_sq
        qd = sb("qd", [P, NG, 2, 4 * DH])
        kd = sb("kd", [P, NG, 2, 4 * DH])
        vb = sb("vb", [P, TILES, NJ, 2, 2, DH])
        qT = [sb(f"qT{i}", [P, NG, P]) for i in range(TILES)]
        kT = sb("kT", [P, NG, S])
        kbd = sb("kbd", [P, TILES, NG, 4, S])
        mx0 = sb("mx0", [P, H])
        e0 = [sb(f"e0_{i}", [P, H, S]) for i in range(TILES)]
        sum0 = sb("sum0", [P, H])
        inv0 = [sb(f"inv0_{i}", [P, H]) for i in range(TILES)]
        pT0 = sb("pT0", [P, NJ, P])
        aoh = sb("aoh", [P, DC, MT], F32R)
        aol = sb("aol", [P, DC, MT], F32R)

        th = sb("th", [P, 2, MT])
        gf = sb("gf", [P, 2, MT])
        gh = sb("gh", [P, MC, MT], F32R)
        gl = sb("gl", [P, MC, MT], F32R)
        x2 = sb("x2", [P, DC, MT])
        sf = sb("sf", [P, DC, MT])
        gate = sb("gate", [P, MT])
        kv = sb("kv", [P, DC, MB, NKP])
        q1T = sb("q1T", [P, ND, DC, MT])
        k1T = sb("k1T", [P, ND, DC, MB, NKP])
        kbd1 = sb("kbd1", [P, ND * DC, MB, 8, NKV])
        vb1 = sb("vb1", [P, MB, NJ, 2, DH])
        adj = sb("adj", [P, TILES, NE, NL], I32)
        adw = q1T[:, :, :, :].rearrange("p a c t -> p (a c t)")[:, 0:TILES * NE * NL].rearrange("p (e l) -> p e l", l=NL)
        edge_n = sb("edge_n", [P, TILES, NE])
        edge_v = sb("edge_v", [P, TILES, NE])
        edge_bias = sb("edge_bias", [P, TILES, NE])
        e1 = [sb("e1", [P, ND, H, NKV])[:, :, :, :],
              adj[:, :, :, :].bitcast(F32).rearrange("p t e l -> p (t e l)")[:, 0:ND * H * NKV]
              .rearrange("p (a h k) -> p a h k", a=ND, h=H)]
        mx1 = sb("mx1", [P, ND, H])
        sum1 = sb("sum1", [P, ND, H])
        inv1 = [sb(f"inv1_{i}", [P, ND, H]) for i in range(TILES)]
        p1 = sb("p1", [P, NJ, ND, 2, NKP])
        pT1 = sb("pT1", [P, NJ, P])
        stage = [kbd1[:, :, :, :, :].rearrange("p a b c d -> p (a b c d)")[:, 0:DC * 3 * D],
                 kbd[:, :, :, :, :].rearrange("p a b c d -> p (a b c d)")[:, 0:DC * 3 * D]]

        cond, cond_t = (v.rearrange("p (c b) -> p c b", b=B) for v in (th[:, 0, :], th[:, 1, :]))
        cond_s = gf[:, 0, :].rearrange("p (c b) -> p c b", b=B)

        lin = [ctx.enter_context(nc.psum_tensor(f"lin{i}", [P, 2, MT], F32)) for i in range(2)]
        s0_ps = ctx.enter_context(nc.psum_tensor("s0_ps", [P, 2, 2 * MT], F32))
        tr = [ctx.enter_context(nc.psum_tensor(f"tr{i}", [P, 4, P], F32)) for i in range(2)]
        ao_ps = ctx.enter_context(nc.psum_tensor("ao_ps", [P, 2, MT], F32))
        ao1_ps = ctx.enter_context(nc.psum_tensor("ao1_ps", [P, 2, MT], F32))
        s1_ps = [lin[i][:, :, :].rearrange("p a b -> p (a b)") for i in range(2)]
        tr1 = [s.rearrange("p (a b) -> p a b", b=P) for s in s1_ps]
        qkv_ps = [(s0_ps[:, 0, :], s0_ps[:, 1, 0:D]),
                  (tr[0][:, :, :].rearrange("p a b -> p (a b)"),
                   tr[1][:, :, :].rearrange("p a b -> p (a b)")[:, 0:D])]
        ms_ps = [s0_ps[:, 1, 0:TILES], ao_ps[:, 1, 0:TILES]]
        spread_ps = [s0_ps[:, 0, 0:MT], ao_ps[:, 0, :]]

        consts_in = signal("consts_in")
        stage_in = [signal("stage0_in"), signal("stage1_in")]
        cond_weights_in, graph_weights_in = signal("cond_weights_in"), signal("graph_weights_in")
        zeros_set = signal("zeros_set")
        weight_hi = signal("weight_hi")
        weight_lo = signal("weight_lo")
        table_step = signal("table_step")
        sines = signal("sines")
        cond_tanh = signal("cond_tanh")
        cond_ready = signal("cond_ready")
        mods_ps = signal("mods_ps")
        mods_set = signal("mods_set")
        biases_set = signal("biases_set")

        x_in_s, x_res_s, adj_s = signal("x_in_s", 16), signal("x_res_s", 16), signal("adj_s", 16)
        out_s = signal("out_s", 16)
        mod_set = [signal("mod_set_L0"), signal("mod_set_L1")]
        squares = [signal("squares_L0"), signal("squares_L1")]
        means = [signal("means_L0"), signal("means_L1")]
        roots = [signal("roots_L0"), signal("roots_L1")]
        inverses = [signal("inverses_L0"), signal("inverses_L1")]
        spread = [signal("spread_L0"), signal("spread_L1")]
        normed = [signal("normed_L0"), signal("normed_L1")]
        scaled = [signal("scaled_L0"), signal("scaled_L1")]
        shifted = [signal("shifted_L0"), signal("shifted_L1")]
        normed_hi = [signal("normed_hi_L0"), signal("normed_hi_L1")]
        normed_lo = [signal("normed_lo_L0"), signal("normed_lo_L1")]
        qkv_done = signal("qkv_done", TILES)
        qk_squares, qk_kept, v_kept = signal("qk_squares", TILES), signal("qk_kept", TILES), signal("v_kept", TILES)
        qk_sums, qk_roots, qk_inverses = signal("qk_sums", TILES), signal("qk_roots"), signal("qk_inverses")
        q_inverses = signal("q_inverses", 2)
        cos_part, sin_part = signal("cos_part", TILES), signal("sin_part", TILES)
        rotated = signal("rotated", 2 * TILES)
        heads_split = signal("heads_split", TILES)
        qT_ps, kT_ps = signal("qT_ps", TILES), signal("kT_ps", TILES)
        qT_kept, kT_kept = signal("qT_kept", TILES), signal("kT_kept", TILES)
        k_spread = signal("k_spread", TILES)
        scores, maxima, shifted_s = signal("scores", TILES), signal("maxima", TILES), signal("shifted_s", TILES)
        exps, exp_sums, inv_sums = signal("exps", TILES), signal("exp_sums", TILES), signal("inv_sums", TILES)
        probs = signal("probs", TILES)
        pT_ps = signal("pT_ps", 2 * TILES)
        pT_a, pT_b = signal("pT_a", TILES), signal("pT_b", TILES)
        mixed, mixed_hi, mixed_lo = signal("mixed", TILES), signal("mixed_hi", TILES), signal("mixed_lo", TILES)
        proj_done, proj_gated, x1_done = signal("proj_done"), signal("proj_gated", DC), signal("x1_done")

        z_done, z_tanh, z_silu = signal("z_done", MC), signal("z_tanh", MC // 2), signal("z_silu", MC // 2)
        g_done, g_hi, g_lo = signal("g_done", MC // 2), signal("g_hi", MC // 2), signal("g_lo", MC // 2)
        down_done, down_gated = signal("down_done"), signal("down_gated")
        x2_done, x2_hi, x2_lo = signal("x2_done"), signal("x2_hi"), signal("x2_lo")
        rowsum, row_gate, cond_part = signal("rowsum"), signal("row_gate"), signal("cond_part")
        self_ps, self_done = signal("self_ps"), signal("self_done", DC)
        self_hi, self_lo = signal("self_hi"), signal("self_lo")
        q1_ps, q1_kept = signal("q1_ps", ND), signal("q1_kept", ND)
        kv_kept = signal("kv_kept")
        k1_ps, k1_kept = signal("k1_ps"), signal("k1_kept")
        k1_spread, k1_spread_pool = signal("k1_spread"), signal("k1_spread_pool")
        v1_ps, v1_kept = signal("v1_ps"), signal("v1_kept")
        edge_count, edge_weighted, edge_value = signal("edge_count"), signal("edge_weighted"), signal("edge_value")
        edge_masked, edge_ready = signal("edge_masked"), signal("edge_ready")
        scores1, biased1 = signal("scores1", TILES), signal("biased1", TILES)
        maxima1, shifted1, exps1 = signal("maxima1", TILES), signal("shifted1", TILES), signal("exps1", TILES)
        sums1, inverses1, probs1 = signal("sums1", TILES), signal("inverses1", TILES), signal("probs1", TILES)
        pT1_ps, pT1_a, pT1_b = signal("pT1_ps", 2 * TILES), signal("pT1_a", TILES), signal("pT1_b", TILES)
        mixed1, summed1 = signal("mixed1", TILES), signal("summed1", TILES)
        relu_done = signal("relu_done")

        small = [(ident[:, :], d["ident"]), (mean_col[:, :], d["mean_col"]), (hmask4[:, :], d["hmask4"]),
                 (hmask8[:, :], d["hmask8"]), (seq_ind[:, :], d["seq_ind"]), (colb[:, :], d["colb"]),
                 (lnw[:, :, :], d["lnw"]), (edge_w[:, :], d["edge_w"]), (edge_b[:, :], d["edge_b"]),
                 (pos_i[:, :], d["pos"]), (freq[:, :], d["freq"]),
                 (cond[:, :, :], d["condT"].rearrange("(c p) b -> p c b", p=P))]
        w_adaln = [(e[:, :, :].rearrange("p h s -> p (h s)"), x[:, :, :].rearrange("p c t -> p (c t)"))
                   for e, x in zip(e0, (x2, sf))]
        adaln_cut = H * S
        w_cond = x1[:, :, :]
        cond_weights = [(w_adaln[c][i], d["adaln"][c * P:(c + 1) * P, (0, adaln_cut)[i]:(adaln_cut, NMOD * P)[i]])
                        for c in range(DC) for i in range(2)]
        cond_weights.append((w_cond, d["self_cond"].rearrange("(c p) n -> p c n", p=P)))
        graph_weights = [(wk1[:, :, :], d["k1"].rearrange("(c p) n -> p c n", p=P)),
                         (wo1[:, :, :], d["out1"].rearrange("(c p) n -> p c n", p=P))]
        NW = len(WEIGHTS)
        x_v = d["xT"].rearrange("(c p) t -> p c t", p=P)
        out_v = d["outT"].rearrange("(c p) t -> p c t", p=P)
        adj_v = d["adj"].rearrange("(n p) e -> p n e", p=P)
        names = list(WEIGHTS)

        def stage_view(k):
            shape = WEIGHTS[names[k]]
            return stage[k % 2][:, 0:shape[0] * shape[1]].rearrange("p (c n) -> p c n", n=shape[1])

        block = ctx.enter_context(nc.Block())

        @block.sync
        def _(sp):
            for dst, src in small:
                sp.dma_start(dst, src).then_inc(consts_in.sem, 16)
            for dst, src in cond_weights:
                sp.dma_start(dst, src).then_inc(cond_weights_in.sem, 16)
            for k, name in enumerate(names):
                if k >= 2:
                    sp.wait_ge(weight_lo.sem, k - 1)
                sp.dma_start(stage_view(k), d[name].rearrange("(c p) n -> p c n", p=P)).then_inc(stage_in[k % 2].sem, 16)
            for dst, src in graph_weights:
                sp.dma_start(dst, src).then_inc(graph_weights_in.sem, 16)

            def load_x(m, n):
                wait_last(sp, normed[0], m)
                sp.dma_start(x_in[:, :, :], x_v[:, :, bass.ds(m * MT, MT)]).then_inc(x_in_s.sem, 16)

            def load_residual(m, n):
                wait_last(sp, x1_done, m)
                sp.dma_start(x_res[:, :, :], x_v[:, :, bass.ds(m * MT, MT)]).then_inc(x_res_s.sem, 16)

            def load_edges(m, n):
                if n > 0:
                    return
                wait_last(sp, probs1, m)
                sp.dma_start(adj[:, :, :, :].rearrange("p n e l -> p n (e l)"),
                             adj_v[:, bass.ds(m * TILES, TILES), :]).then_inc(adj_s.sem, 16)

            def store(m, n):
                wait(sp, relu_done, m, 1)
                sp.dma_start(out_v[:, :, bass.ds(m * MT, MT)], sf[:, :, :]).then_inc(out_s.sem, 16)

            run_steps(sp, "SP", {"norm0_mean": load_x, "norm0_apply": load_residual, "mlp_up": load_edges, "out": store})
            wait(sp, out_s, NM, 0)

        @block.tensor
        def _(pe):
            def linear(out, terms):
                for i, (lhsT, rhs) in enumerate(terms):
                    last = nc.tensor.matmul(out, lhsT, rhs, start=i == 0, stop=i == len(terms) - 1)
                return last

            def fm_terms(k, cols, hi, lo, chunks):
                return [(w[:, c, cols], a[:, c, :]) for c in range(chunks)
                        for w, a in ((wl[k], hi), (wh[k], lo), (wh[k], hi))]

            pe.wait_ge(consts_in.sem, 16 * len(small))
            pe.wait_ge(cond_ready.sem, 1)
            pe.wait_ge(cond_weights_in.sem, 16 * len(cond_weights))
            ps = [lin[0][:, :, :], lin[1][:, :, :], tr[0][:, :, :]]
            for j in range(NMOD):
                out = ps[j // 4].rearrange("p a b -> p (a b)")[:, (j % 4) * P:(j % 4 + 1) * P]
                part, col0 = (0, j * P) if j * P < adaln_cut else (1, j * P - adaln_cut)
                for c in range(DC):
                    last = nc.tensor.matmul(out, w_adaln[c][part][:, col0:col0 + P], cond_s[:, c, :],
                                            start=c == 0, stop=c == DC - 1)
                last.then_inc(mods_ps.sem, 1)
            for o in range(DC):
                for c in range(DC):
                    last = nc.tensor.matmul(ao_ps[:, 0, o * P:(o + 1) * P], w_cond[:, c, o * P:(o + 1) * P],
                                            cond[:, c, :], start=c == 0, stop=c == DC - 1)
                last.then_inc(mods_ps.sem, 1)
            pe.wait_ge(graph_weights_in.sem, 16 * len(graph_weights))
            pe.wait_ge(weight_hi.sem, NW)
            pe.wait_ge(weight_lo.sem, NW)
            pe.wait_ge(zeros_set.sem, 5)
            pe.wait_ge(mods_set.sem, NMOD + DC)

            def norm_mean(norm):
                def step(m, n):
                    wait(pe, squares[norm], m, 1)
                    if norm == 0:
                        wait_last(pe, shifted_s, m)
                    for t in range(TILES):
                        for c in range(DC):
                            last = nc.tensor.matmul(ms_ps[norm][:, t:t + 1], xn[norm][:, c, t * P:(t + 1) * P],
                                                    mean_col[:, :], start=c == 0, stop=c == DC - 1)
                    last.then_inc(means[norm].sem, 1)
                return step

            def norm_apply(norm):
                def step(m, n):
                    wait(pe, inverses[norm], m, 1)
                    for t in range(TILES):
                        last = nc.tensor.matmul(spread_ps[norm][:, t * P:(t + 1) * P],
                                                rms_inv[norm][:, t:t + 1].to_broadcast([P, P]), ident[:, :],
                                                start=True, stop=True)
                    last.then_inc(spread[norm].sem, 1)
                return step

            def qkv(m, t):
                if t == 0:
                    wait(pe, normed_hi[0], m, 1)
                    wait(pe, normed_lo[0], m, 1)
                else:
                    wait_last(pe, pT_a, m)
                    wait_last(pe, pT_b, m)
                qk_ps, v_ps = qkv_ps[t]
                rows = slice(t * P, (t + 1) * P)
                terms = [(a[:, c, rows], w[:, c, :]) for c in range(DC)
                         for a, w in ((nh[0], wl["qkv"]), (nl[0], wh["qkv"]), (nh[0], wh["qkv"]))]
                linear(qk_ps, [(a, w[:, 0:2 * D]) for a, w in terms])
                linear(v_ps, [(a, w[:, 2 * D:3 * D]) for a, w in terms]).then_inc(qkv_done.sem, 1)

            def heads(m, t):
                wait(pe, heads_split, m, t + 1)
                if t == 0:
                    wait(pe, v_kept, m, TILES)
                    wait(pe, qk_kept, m, TILES)
                else:
                    wait(pe, kT_kept, m, t)
                    wait(pe, qT_kept, m, t)
                for g in range(NG):
                    last = nc.tensor.transpose(tr[0][:, g, :], qd[:, g, :, :].rearrange("p s f -> p (s f)"), ident[:, :])
                last.then_inc(qT_ps.sem, 1)
                for g in range(NG):
                    last = nc.tensor.transpose(tr[1][:, g, :], kd[:, g, :, :].rearrange("p s f -> p (s f)"), ident[:, :])
                last.then_inc(kT_ps.sem, 1)

            def score(m, t):
                wait(pe, qT_kept, m, t + 1)
                wait(pe, k_spread, m, t + 1)
                if t == 0:
                    wait(pe, qk_kept, m, 1)
                    wait(pe, v_kept, m, 1)
                else:
                    wait(pe, shifted_s, m, t)
                for g in range(NG):
                    last = nc.tensor.matmul(s0_ps[:, g // 2, (g % 2) * 4 * S:(g % 2 + 1) * 4 * S], qT[t][:, g, :],
                                            kbd[:, t, g, :, :].rearrange("p h s -> p (h s)"), start=True, stop=True)
                last.then_inc(scores.sem, 1)

            def probs_t(m, t):
                wait(pe, probs, m, t + 1)
                wait(pe, qT_kept, m, TILES)
                wait(pe, kT_kept, m, TILES)
                if t > 0:
                    wait(pe, pT_a, m, t)
                    wait(pe, pT_b, m, t)
                for j in range(NJ):
                    last = nc.tensor.transpose(tr[j // 4][:, j % 4, :],
                                               e0[t][:, 2 * j:2 * j + 2, :].rearrange("p h s -> p (h s)"), ident[:, :])
                    if j % 4 == 3:
                        last.then_inc(pT_ps.sem, 1)

            def mix(m, t):
                wait(pe, pT_a, m, t + 1)
                wait(pe, pT_b, m, t + 1)
                wait(pe, v_kept, m, t + 1)
                if t > 0:
                    wait(pe, mixed_lo, m, t)
                else:
                    wait_last(pe, normed[1], m)
                for j in range(NJ):
                    for s in range(2):
                        f = 32 * (j % 4)
                        last = nc.tensor.matmul(ao_ps[f:f + 32, 0, (j // 4) * P + s * S:(j // 4) * P + (s + 1) * S],
                                                vb[:, t, j, s, :, :].rearrange("p h f -> p (h f)"),
                                                pT0[:, j, s * S:(s + 1) * S], start=True, stop=True,
                                                tile_position=(0, f))
                last.then_inc(mixed.sem, 1)

            def proj(m, n):
                wait(pe, mixed_hi, m, TILES)
                wait(pe, mixed_lo, m, TILES)
                for o in range(DC):
                    last = linear(ao_ps[:, o, :],
                                  fm_terms("proj", slice(o * P, (o + 1) * P), aoh, aol, DC))
                last.then_inc(proj_done.sem, 1)

            def mlp_up(m, n):
                if n == 0:
                    wait(pe, normed_hi[1], m, 1)
                    wait(pe, normed_lo[1], m, 1)
                    wait_last(pe, pT1_a, m)
                    wait_last(pe, pT1_b, m)
                else:
                    wait(pe, z_silu, m, n)
                for k, name in enumerate(("w1", "w3")):
                    if k == 1 and n > 0:
                        wait(pe, g_done, m, n)
                    for c in range(2):
                        j = 2 * n + c
                        last = linear(lin[k][:, c, :], fm_terms(name, slice(j * P, (j + 1) * P), nh[1], nl[1], DC))
                    last.then_inc(z_done.sem, 1)

            def mlp_down(m, n):
                wait(pe, g_hi, m, MC // 2)
                wait(pe, g_lo, m, MC // 2)
                for o in range(DC):
                    last = linear(lin[0][:, o, :], fm_terms("w2", slice(o * P, (o + 1) * P), gh, gl, MC))
                last.then_inc(down_done.sem, 1)

            def self_feat(m, n):
                wait(pe, x2_hi, m, 1)
                wait(pe, x2_lo, m, 1)
                linear(lin[1][:, 0, :], [(ones_r[:, :], a[:, c, :]) for c in range(DC) for a in (nl[1], nh[1])])\
                    .then_inc(rowsum.sem, 1)
                for o in range(DC):
                    last = linear(lin[0][:, o, :], fm_terms("self", slice(o * P, (o + 1) * P), nh[1], nl[1], DC))
                last.then_inc(self_ps.sem, 1)

            def k1(m, n):
                wait(pe, kv_kept, m, 1)
                wait(pe, row_gate, m, 1)
                for k in range(ND * DC):
                    for c in range(DC):
                        last = nc.tensor.matmul(lin[1][:, k // 2, (k % 2) * P:(k % 2 + 1) * P],
                                                wk1[:, c, k * P:(k + 1) * P],
                                                kv[:, c, :, :].rearrange("p b k -> p (b k)"),
                                                start=c == 0, stop=c == DC - 1)
                last.then_inc(k1_ps.sem, 1)

            def q1(m, n):
                wait(pe, self_hi, m, 1)
                wait(pe, self_lo, m, 1)
                for direction in range(ND):
                    if direction == 1:
                        wait(pe, k1_kept, m, 1)
                    for o in range(DC):
                        k = direction * DC + o
                        last = linear(lin[direction][:, o, :],
                                      fm_terms("q1", slice(k * P, (k + 1) * P), nh[1], nl[1], DC))
                    last.then_inc(q1_ps.sem, 1)

            def v1(m, n):
                wait_last(pe, summed1, m)
                wait(pe, kv_kept, m, 1)
                linear(ao1_ps[:, :, :].rearrange("p a b -> p (a b)"),
                       [(kv[:, c, :, :].rearrange("p b k -> p (b k)"), wo1[:, c, :]) for c in range(DC)])\
                    .then_inc(v1_ps.sem, 1)

            def score1(m, t):
                if t == 0:
                    wait(pe, q1_kept, m, ND)
                    wait(pe, k1_spread, m, 1)
                    wait(pe, k1_spread_pool, m, 1)
                else:
                    wait(pe, biased1, m, t)
                for direction in range(ND):
                    for c in range(DC):
                        for s in range(2):
                            b = 2 * t + s
                            last = nc.tensor.matmul(
                                s1_ps[direction][s * S:(s + 1) * S, c * 8 * NKV:(c + 1) * 8 * NKV],
                                q1T[:, direction, c, b * S:(b + 1) * S],
                                kbd1[:, direction * DC + c, b, :, :].rearrange("p h k -> p (h k)"),
                                start=True, stop=True)
                last.then_inc(scores1.sem, 1)

            def probs_t1(m, t):
                wait(pe, probs1, m, t + 1)
                if t == 0:
                    wait(pe, biased1, m, TILES)
                else:
                    wait(pe, pT1_a, m, t)
                    wait(pe, pT1_b, m, t)
                for j in range(NJ):
                    last = nc.tensor.transpose(tr1[j // 4][:, j % 4, :],
                                               p1[:, j, :, :, :].rearrange("p a h k -> p (a h k)"), ident[:, :])
                    if j % 4 == 3:
                        last.then_inc(pT1_ps.sem, 1)

            def mix1(m, t):
                wait(pe, pT1_a, m, t + 1)
                wait(pe, pT1_b, m, t + 1)
                wait(pe, v1_kept, m, 1)
                if t > 0:
                    wait(pe, summed1, m, t)
                for j in range(NJ):
                    for s in range(2):
                        f = 32 * (j % 4)
                        last = nc.tensor.matmul(ao1_ps[f:f + 32, 0, (j // 4) * P + s * S:(j // 4) * P + (s + 1) * S],
                                                vb1[:, 2 * t + s, j, :, :].rearrange("p h f -> p (h f)"),
                                                pT1[:, j, s * S:(s + 1) * S], start=True, stop=True,
                                                tile_position=(0, f))
                last.then_inc(mixed1.sem, 1)

            run_steps(pe, "PE", {
                "norm0_mean": norm_mean(0), "norm1_mean": norm_mean(1), "norm0_apply": norm_apply(0),
                "norm1_apply": norm_apply(1), "qkv": qkv, "heads": heads, "score": score, "probsT": probs_t, "mix": mix, "proj": proj,
                "mlp_up": mlp_up, "mlp_down": mlp_down, "self": self_feat, "k1": k1,
                "q1": q1, "v1": v1, "score1": score1, "probsT1": probs_t1, "mix1": mix1,
            })

        @block.scalar
        def _(act):
            act.wait_ge(consts_in.sem, 16 * len(small))
            nc.scalar.activation(cond_t[:, :, :], cond[:, :, :], ACT.Tanh, scale=0.5).then_inc(cond_tanh.sem, 1)
            for k, name in enumerate(names):
                act.wait_ge(stage_in[k % 2].sem, 16 * (k // 2 + 1))
                nc.scalar.activation(wh[name][:, :, :], stage_view(k), ACT.Copy,
                                     scale=WEIGHT_SCALE.get(name, 1.0)).then_inc(weight_hi.sem, 1)
            act.wait_ge(table_step.sem, 8)
            nc.scalar.activation(ang[:, :, :], ang[:, :, :], ACT.Sin).then_inc(sines.sem, 1)
            act.wait_ge(biases_set.sem, 2)
            act.wait_ge(zeros_set.sem, 5)

            def norm_mean(norm):
                x = (x_in, x1)[norm]

                def step(m, n):
                    if norm == 0:
                        wait(act, x_in_s, m, 16)
                    else:
                        wait(act, x1_done, m, 1)
                    wait_last(act, normed_lo[norm], m)
                    wait_last(act, normed_hi[norm], m)
                    nc.scalar.activation(xn[norm][:, :, :], x[:, :, :], ACT.Square).then_inc(squares[norm].sem, 1)
                return step

            def norm_root(norm):
                def step(m, n):
                    wait(act, means[norm], m, 1)
                    nc.scalar.activation(rms_root[norm][:, :], ms_ps[norm], ACT.Sqrt, bias=eps[:, :])\
                        .then_inc(roots[norm].sem, 1)
                return step

            def norm_apply(norm):
                def step(m, n):
                    wait(act, shifted[norm], m, 1)
                    wait_last(act, (qkv_done, q1_ps)[norm], m)
                    nc.scalar.activation(nh[norm][:, :, :], xn[norm][:, :, :], ACT.Copy).then_inc(normed_hi[norm].sem, 1)
                return step

            def qkv(m, t):
                wait(act, qkv_done, m, t + 1)
                qk_ps, v_ps = qkv_ps[t]
                wait(act, qk_sums, m, t)
                if t == 0:
                    wait_last(act, heads_split, m)
                nc.scalar.activation(qk_sq[:, :, :, :].rearrange("p a h f -> p (a h f)"), qk_ps, ACT.Square)\
                    .then_inc(qk_squares.sem, 1)
                if t == 0:
                    wait_last(act, cos_part, m)
                    wait_last(act, sin_part, m)
                    wait_last(act, mixed, m)
                nc.scalar.activation(qk[:, t, :, :, :].rearrange("p a h f -> p (a h f)"), qk_ps, ACT.Copy)\
                    .then_inc(qk_kept.sem, 1)
                v = v_ps.rearrange("p (j h f) -> p j h f", h=2, f=DH)
                for s in range(2):
                    for h in range(2):
                        last = nc.scalar.activation(vb[h * S:(h + 1) * S, t, :, s, h, :], v[s * S:(s + 1) * S, :, h, :],
                                                    ACT.Copy)
                last.then_inc(v_kept.sem, 1)

            def rope_scale(m, n):
                wait(act, qk_sums, m, TILES)
                wait_last(act, qk_inverses, m)
                nc.scalar.activation(qk_root[:, :, :], qk_ss[:, :, :], ACT.Sqrt, bias=eps[:, :], scale=1.0 / DH)\
                    .then_inc(qk_roots.sem, 1)

            def heads(m, t):
                wait(act, qT_ps, m, t + 1)
                wait(act, scores, m, t - TILES + 1)
                nc.scalar.activation(qT[t][:, :, :], tr[0][:, :, :], ACT.Copy).then_inc(qT_kept.sem, 1)
                wait(act, kT_ps, m, t + 1)
                wait(act, k_spread, m, t)
                for s in range(2):
                    last = nc.scalar.activation(kT[s * S:(s + 1) * S, :, :], tr[1][s * S:(s + 1) * S, :, s * S:(s + 1) * S],
                                                ACT.Copy)
                last.then_inc(kT_kept.sem, 1)

            def score(m, t):
                wait(act, shifted_s, m, t + 1)
                nc.scalar.activation(e0[t][:, :, :], e0[t][:, :, :], ACT.Exp, scale=DH ** -0.5).then_inc(exps.sem, 1)

            def probs_t(m, t):
                wait(act, pT_ps, m, 2 * t + 1)
                wait(act, mixed, m, t)
                nc.scalar.activation(pT0[:, 0:4, :], tr[0][:, :, :], ACT.Copy).then_inc(pT_a.sem, 1)
                wait(act, pT_ps, m, 2 * t + 2)
                nc.scalar.activation(pT0[:, 4:8, :], tr[1][:, :, :], ACT.Copy).then_inc(pT_b.sem, 1)

            def mix(m, t):
                wait(act, mixed, m, t + 1)
                wait_last(act, proj_done, m)
                nc.scalar.activation(aoh[:, :, t * P:(t + 1) * P],
                                     ao_ps[:, 0, :].rearrange("p (c t) -> p c t", c=DC), ACT.Copy)\
                    .then_inc(mixed_hi.sem, 1)

            def mlp_up(m, n):
                wait(act, z_done, m, 2 * n + 1)
                wait(act, z_silu, m, n)
                nc.scalar.activation(th[:, :, :], lin[0][:, :, :], ACT.Tanh, scale=0.5).then_inc(z_tanh.sem, 1)

            def mlp_split(m, n):
                wait(act, g_done, m, n + 1)
                wait_last(act, down_done, m)
                nc.scalar.activation(gh[:, 2 * n:2 * n + 2, :], gf[:, :, :], ACT.Copy).then_inc(g_hi.sem, 1)

            def x2_split(m, n):
                wait(act, x2_done, m, 1)
                nc.scalar.activation(nh[1][:, :, :], x2[:, :, :], ACT.Copy).then_inc(x2_hi.sem, 1)

            def self_split(m, n):
                wait(act, self_done, m, DC)
                wait_last(act, v1_ps, m)
                nc.scalar.activation(kv[:, :, :, :], sf[:, :, :].rearrange("p c (b s) -> p c b s", s=S)[:, :, :, 0:NKP],
                                     ACT.Copy).then_inc(kv_kept.sem, 1)
                wait(act, x2_lo, m, 1)
                wait(act, self_ps, m, 1)
                nc.scalar.activation(nh[1][:, :, :], sf[:, :, :], ACT.Copy).then_inc(self_hi.sem, 1)

            def k1(m, n):
                wait(act, k1_ps, m, 1)
                wait_last(act, k1_spread, m)
                wait_last(act, k1_spread_pool, m)
                for k in range(ND * DC):
                    last = nc.scalar.activation(
                        k1T[:, k // 2, k % 2, :, :].rearrange("p b k -> p (b k)"),
                        lin[1][:, k // 2, (k % 2) * P:(k % 2 + 1) * P], ACT.Identity, bias=bk[:, k:k + 1])
                last.then_inc(k1_kept.sem, 1)

            def q1(m, n):
                wait_last(act, scores1, m)
                wait(act, edge_value, m, 1)
                for direction in range(ND):
                    wait(act, q1_ps, m, direction + 1)
                    for o in range(DC):
                        k = direction * DC + o
                        last = nc.scalar.activation(q1T[:, direction, o, :], lin[direction][:, o, :], ACT.Identity,
                                                    bias=bq4[:, k:k + 1], scale=DH ** -0.5)
                    last.then_inc(q1_kept.sem, 1)

            def v1(m, n):
                wait(act, v1_ps, m, 1)
                wait_last(act, mixed1, m)
                v = ao1_ps[:, :, :].rearrange("p a (j h f) -> p a j h f", h=2, f=DH)
                for b in range(MB):
                    for r in range(4):
                        last = nc.scalar.activation(vb1[r * NKP:(r + 1) * NKP, b, :, r % 2, :],
                                                    v[b * NKP:(b + 1) * NKP, r // 2, :, r % 2, :], ACT.Copy)
                last.then_inc(v1_kept.sem, 1)

            def score1(m, t):
                wait(act, shifted1, m, t + 1)
                nc.scalar.activation(e1[t], e1[t], ACT.Exp).then_inc(exps1.sem, 1)

            def probs_t1(m, t):
                wait(act, pT1_ps, m, 2 * t + 1)
                wait(act, mixed1, m, t)
                nc.scalar.activation(pT1[:, 0:4, :], tr1[0], ACT.Copy).then_inc(pT1_a.sem, 1)
                wait(act, pT1_ps, m, 2 * t + 2)
                nc.scalar.activation(pT1[:, 4:8, :], tr1[1], ACT.Copy).then_inc(pT1_b.sem, 1)

            run_steps(act, "Activation", {
                "norm0_mean": norm_mean(0), "norm0_root": norm_root(0), "norm1_root": norm_root(1), "norm1_mean": norm_mean(1), "norm0_apply": norm_apply(0),
                "norm1_apply": norm_apply(1), "qkv": qkv, "rope_scale": rope_scale, "heads": heads, "score": score, "probsT": probs_t, "mix": mix,
                "mlp_up": mlp_up, "mlp_split": mlp_split, "x2_split": x2_split, "self_split": self_split, "k1": k1, "q1": q1, "v1": v1,
                "score1": score1, "probsT1": probs_t1,
            })

        def per_seq(ap):
            return ap.unsqueeze(3).to_broadcast([P, ap.shape[1], MB, S])

        def by_seq(ap):
            return ap.rearrange("p c (b s) -> p c b s", s=S)

        def spread_k1(queue, engine, m, chunks):
            wait(queue, k1_kept, m, 1)
            wait_last(queue, scores1, m)
            for k in chunks:
                last = engine.tensor_tensor(kbd1[:, k, :, :, :],
                                            k1T[:, k // 2, k % 2, :, 0:NKV].unsqueeze(2).to_broadcast([P, MB, 8, NKV]),
                                            hmask8[:, :].unsqueeze(1).unsqueeze(3).to_broadcast([P, MB, 8, NKV]),
                                            ALU.mult)
            return last

        @block.vector
        def _(dve):
            nc.vector.memset(eps[:, :], EPS).then_inc(zeros_set.sem, 1)
            nc.vector.memset(ones_r[:, :].bitcast(F32), 1.0).then_inc(zeros_set.sem, 1)
            nc.vector.memset(ones_f[:, :], 1.0).then_inc(zeros_set.sem, 1)
            nc.vector.memset(vb[:, :, :, :, :, :].rearrange("p t j s h f -> p (t j s h f)"), 0.0).then_inc(zeros_set.sem, 1)
            nc.vector.memset(vb1[:, :, :, :, :].rearrange("p b j h f -> p (b j h f)"), 0.0).then_inc(zeros_set.sem, 1)
            nc.vector.memset(p1[:, :, :, :, :].rearrange("p j a h k -> p (j a h k)"), 0.0).then_inc(zeros_set.sem, 1)
            dve.wait_ge(consts_in.sem, 16 * len(small))
            dve.wait_ge(cond_tanh.sem, 1)
            nc.vector.scalar_tensor_tensor(cond_t[:, :, :], cond_t[:, :, :], 1.0, cond[:, :, :], ALU.add, ALU.mult)\
                .then_inc(table_step.sem, 1)
            dve.wait_ge(table_step.sem, 1)
            nc.vector.tensor_scalar(cond_s[:, :, :], cond_t[:, :, :], 0.5, None, ALU.mult).then_inc(cond_ready.sem, 1)
            nc.vector.tensor_copy(pos_f[:, :], pos_i[:, :]).then_inc(table_step.sem, 1)
            dve.wait_ge(table_step.sem, 2)
            nc.vector.tensor_scalar(ang[:, 0, :], freq[:, :], pos_f[:, :], None, ALU.mult)
            nc.vector.tensor_scalar(ang[:, 1, :], freq[:, :], pos_f[:, :], 1.5707963267948966, ALU.mult, ALU.add)\
                .then_inc(table_step.sem, 1)
            dve.wait_ge(table_step.sem, 3)
            nc.vector.tensor_scalar(turns_i[:, :, :], ang[:, :, :], 0.15915494309189535, None, ALU.mult)\
                .then_inc(table_step.sem, 1)
            dve.wait_ge(table_step.sem, 4)
            nc.vector.tensor_copy(turns[:, :, :], turns_i[:, :, :]).then_inc(table_step.sem, 1)
            for i, part in enumerate(TWO_PI_PARTS):
                dve.wait_ge(table_step.sem, 5 + i)
                last = nc.vector.scalar_tensor_tensor(ang[:, :, :], turns[:, :, :], -part, ang[:, :, :], ALU.mult, ALU.add)
                if i < 2:
                    last.then_inc(table_step.sem, 1)
                else:
                    last.then_inc(biases_set.sem, 1)
            dve.wait_ge(biases_set.sem, 1)
            nc.vector.tensor_scalar(ang[:, :, :], ang[:, :, :], 3.1415925, -3.1415925, ALU.min, ALU.max)\
                .then_inc(table_step.sem, 1)
            nc.vector.tensor_scalar(bq4[:, :], bq, DH ** -0.5, None, ALU.mult)
            nc.vector.tensor_tensor(bout[:, :], bo[:, 0:DC], bo[:, DC:2 * DC], ALU.add).then_inc(biases_set.sem, 1)
            for k, name in enumerate(names):
                dve.wait_ge(weight_hi.sem, k + 1)
                nc.vector.scalar_tensor_tensor(wl[name][:, :, :], stage_view(k), WEIGHT_SCALE.get(name, 1.0),
                                               wh[name][:, :, :].bitcast(F32), ALU.mult, ALU.subtract)\
                    .then_inc(weight_lo.sem, 1)
            dve.wait_ge(sines.sem, 1)
            half = DH // 2
            for i in range(2):
                for a in range(2):
                    nc.vector.tensor_tensor(cosw[:, i, a * half:(a + 1) * half], lnw[:, i, a * half:(a + 1) * half],
                                            ang[:, 1, :], ALU.mult)
                    last = nc.vector.scalar_tensor_tensor(sinw[:, i, a * half:(a + 1) * half], ang[:, 0, :],
                                                          (1.0, -1.0)[a], lnw[:, i, a * half:(a + 1) * half],
                                                          ALU.mult, ALU.mult)
            last.then_inc(table_step.sem, 1)
            ps = [lin[0], lin[1], tr[0]]
            for j in range(NMOD):
                dve.wait_ge(mods_ps.sem, 4 * (j // 4 + 1))
                one = 1.0 if j // DC in (SCALE_A // DC, SCALE_M // DC) else 0.0
                nc.vector.tensor_scalar(mods[:, j, :], ps[j // 4][:, :, :].rearrange("p a b -> p (a b)")[:, (j % 4) * P:(j % 4 + 1) * P],
                                        adaln_b[:, j:j + 1], one, ALU.add, ALU.add).then_inc(mods_set.sem, 1)
            for o in range(DC):
                dve.wait_ge(mods_ps.sem, NMOD + DC)
                nc.vector.tensor_copy(mods[:, COND + o, :], ao_ps[:, 0, o * P:(o + 1) * P]).then_inc(mods_set.sem, 1)
            dve.wait_ge(mods_set.sem, NMOD + DC)
            dve.wait_ge(table_step.sem, 9)
            dve.wait_ge(zeros_set.sem, 6)
            dve.wait_ge(biases_set.sem, 2)

            def norm_mean(norm):
                def step(m, n):
                    wait(dve, roots[norm], m, 1)
                    nc.vector.reciprocal(rms_inv[norm][:, :], rms_root[norm][:, :]).then_inc(inverses[norm].sem, 1)
                return step

            def norm_apply(norm):
                x = (x_in, x1)[norm]

                def step(m, n):
                    wait_last(dve, (proj_gated, cond_part)[norm], m)
                    nc.vector.tensor_tensor(mod[norm][:, :, :], mods[:, :, bass.ds(m * MB, MB)],
                                            ones_f[:, :].rearrange("p (c b) -> p c b", b=MB), ALU.mult)\
                        .then_inc(mod_set[norm].sem, 1)
                    wait(dve, spread[norm], m, 1)
                    nc.vector.tensor_tensor(xn[norm][:, :, :], x[:, :, :],
                                            spread_ps[norm].unsqueeze(1).to_broadcast([P, DC, MT]), ALU.mult)\
                        .then_inc(normed[norm].sem, 1)
                return step

            def norm_scale(norm):
                scale = (SCALE_A, SCALE_M)[norm]

                def step(m, n):
                    wait(dve, normed[norm], m, 1)
                    wait(dve, mod_set[norm], m, 1)
                    nc.vector.tensor_tensor(by_seq(xn[norm][:, :, :]), by_seq(xn[norm][:, :, :]),
                                            per_seq(mod[norm][:, scale:scale + DC, :]), ALU.mult)\
                        .then_inc(scaled[norm].sem, 1)
                return step

            def norm_shift(norm):
                shift = (SHIFT_A, SHIFT_M)[norm]

                def step(m, n):
                    wait(dve, scaled[norm], m, 1)
                    nc.vector.tensor_tensor(by_seq(xn[norm][:, :, :]), by_seq(xn[norm][:, :, :]),
                                            per_seq(mod[norm][:, shift:shift + DC, :]), ALU.add)\
                        .then_inc(shifted[norm].sem, 1)
                return step

            def qkv(m, t):
                wait(dve, qk_squares, m, t + 1)
                if t == 0:
                    wait_last(dve, qk_roots, m)
                nc.vector.tensor_reduce(qk_ss[:, t, :], qk_sq[:, :, :, :].rearrange("p a h f -> p (a h) f"), AX.X, ALU.add)\
                    .then_inc(qk_sums.sem, 1)

            def rope_scale(m, n):
                wait(dve, qk_roots, m, 1)
                nc.vector.reciprocal(qk_inv[:, :, :], qk_root[:, :, :]).then_inc(qk_inverses.sem, 1)
                wait(dve, qk_inverses, m, 1)
                for s in range(2):
                    nc.vector.tensor_scalar(q_inv[:, s, :, :], qk_inv[:, :, 0:H], seq_ind[:, s:s + 1], None, ALU.mult)\
                        .then_inc(q_inverses.sem, 1)

            def rope(m, t):
                wait(dve, qk_kept, m, t + 1)
                nc.vector.tensor_tensor(qs[:, :, :, :], qk[:, t, :, :, :],
                                        sinw[:, :, :].unsqueeze(2).to_broadcast([P, 2, H, DH]), ALU.mult)\
                    .then_inc(sin_part.sem, 1)
                wait(dve, sin_part, m, t + 1)
                wait(dve, cos_part, m, t + 1)
                half = DH // 2
                for a in range(2):
                    nc.vector.tensor_tensor(qr[:, :, :, a * half:(a + 1) * half], qc[:, :, :, a * half:(a + 1) * half],
                                            qs[:, :, :, (1 - a) * half:(2 - a) * half], ALU.add).then_inc(rotated.sem, 1)
                wait(dve, rotated, m, 2 * t + 2)
                wait(dve, q_inverses, m, 2)
                wait(dve, kT_ps, m, t)
                qr_v = qr[:, :, :, :].rearrange("p a (g h) f -> p a g h f", g=NG)
                qd_v = qd[:, :, :, :].rearrange("p g s (h f) -> p g s h f", f=DH)
                for s in range(2):
                    nc.vector.tensor_tensor(qd_v[:, :, s, :, :], qr_v[:, 0, :, :, :],
                                            q_inv[:, s, t, :].rearrange("p (g h) -> p g h", g=NG).unsqueeze(3)
                                            .to_broadcast([P, NG, 4, DH]), ALU.mult)
                kd_v = kd[:, :, :, :].rearrange("p g s (h f) -> p g s h f", f=DH)
                for s in range(2):
                    last = nc.vector.tensor_tensor(kd_v[:, :, s, :, :], qr_v[:, 1, :, :, :],
                                                   qk_inv[:, t, H:2 * H].rearrange("p (g h) -> p g h", g=NG).unsqueeze(3)
                                                   .to_broadcast([P, NG, 4, DH]), ALU.mult)
                last.then_inc(heads_split.sem, 1)

            s_v = s0_ps[:, :, :].rearrange("p a (h s) -> p (a h) s", s=S)

            def score_max(m, t):
                wait(dve, scores, m, t + 1)
                wait(dve, shifted_s, m, t)
                nc.vector.tensor_reduce(mx0[:, :], s_v, AX.X, ALU.max).then_inc(maxima.sem, 1)

            def score(m, t):
                wait(dve, maxima, m, t + 1)
                wait(dve, pT_ps, m, 2 * (t + 1 - TILES))
                nc.vector.tensor_tensor(e0[t][:, :, :], s_v, mx0[:, :].unsqueeze(2).to_broadcast([P, H, S]),
                                        ALU.subtract).then_inc(shifted_s.sem, 1)

            def soft(m, t):
                wait(dve, exps, m, t + 1)
                wait(dve, inv_sums, m, t)
                nc.vector.tensor_reduce(sum0[:, :], e0[t][:, :, :], AX.X, ALU.add).then_inc(exp_sums.sem, 1)

            def soft_inverse(m, t):
                wait(dve, exp_sums, m, t + 1)
                nc.vector.reciprocal(inv0[t][:, :], sum0[:, :]).then_inc(inv_sums.sem, 1)

            def mix(m, t):
                wait(dve, mixed_hi, m, t + 1)
                wait_last(dve, proj_done, m)
                nc.vector.tensor_tensor(aol[:, :, t * P:(t + 1) * P], ao_ps[:, 0, :].rearrange("p (c t) -> p c t", c=DC),
                                        aoh[:, :, t * P:(t + 1) * P].bitcast(F32), ALU.subtract)\
                    .then_inc(mixed_lo.sem, 1)

            def proj(m, n):
                wait(dve, proj_done, m, 1)
                wait_last(dve, x2_done, m)
                for o in range(DC):
                    nc.vector.scalar_tensor_tensor(
                        by_seq(x1[:, o:o + 1, :])[:, 0], by_seq(ao_ps[:, o:o + 1, :])[:, 0], proj_b[:, o:o + 1],
                        mod[0][:, GATE_A + o, :].unsqueeze(2).to_broadcast([P, MB, S]), ALU.add, ALU.mult)\
                        .then_inc(proj_gated.sem, 1)

            def mlp_up(m, n):
                wait(dve, z_tanh, m, n + 1)
                wait(dve, g_lo, m, n)
                wait(dve, g_hi, m, n)
                nc.vector.scalar_tensor_tensor(gf[:, :, :], th[:, :, :], 1.0, lin[0][:, :, :], ALU.add, ALU.mult)\
                    .then_inc(z_silu.sem, 1)
                wait(dve, z_silu, m, n + 1)
                wait(dve, z_done, m, 2 * n + 2)
                nc.vector.tensor_tensor(gf[:, :, :], gf[:, :, :], lin[1][:, :, :], ALU.mult).then_inc(g_done.sem, 1)

            def mlp_down(m, n):
                wait(dve, down_done, m, 1)
                wait_last(dve, relu_done, m)
                nc.vector.tensor_tensor(by_seq(x2[:, :, :]), by_seq(lin[0][:, :, :]),
                                        per_seq(mod[1][:, GATE_M:GATE_M + DC, :]), ALU.mult).then_inc(down_gated.sem, 1)

            def row_mask(m, n):
                wait(dve, rowsum, m, 1)
                wait_last(dve, cond_part, m)
                nc.vector.tensor_scalar(gate[:, :], lin[1][:, 0, :], 0.0, None, ALU.not_equal).then_inc(row_gate.sem, 1)

            def self_feat(m, n):
                wait(dve, cond_part, m, 1)
                wait(dve, self_ps, m, 1)
                for o in range(DC):
                    nc.vector.scalar_tensor_tensor(sf[:, o, :], lin[0][:, o, :], self_b[:, o:o + 1], sf[:, o, :],
                                                   ALU.add, ALU.add).then_inc(self_done.sem, 1)

            flat = [v[:, :, :].rearrange("p t e -> p (t e)") for v in (edge_n, edge_v, edge_bias)]

            def edges(m, n):
                wait(dve, adj_s, m, 16)
                a = adj[:, :, :, :].rearrange("p t e l -> p (t e) l")
                wait_last(dve, scores1, m)
                nc.vector.tensor_reduce(flat[0], a, AX.X, ALU.add).then_inc(edge_count.sem, 1)
                nc.vector.tensor_tensor(adw, a, edge_w[:, :].unsqueeze(1).to_broadcast([P, TILES * NE, NL]), ALU.mult)\
                    .then_inc(edge_weighted.sem, 1)

            def edge_masks(m, n):
                wait(dve, edge_weighted, m, 1)
                wait(dve, edge_count, m, 1)
                nc.vector.tensor_reduce(flat[1], adw, AX.X, ALU.add).then_inc(edge_value.sem, 1)
                nc.vector.tensor_scalar(flat[0], flat[0], 0.0, NEG, ALU.is_le, ALU.mult).then_inc(edge_masked.sem, 1)
                wait(dve, edge_masked, m, 1)
                nc.vector.scalar_tensor_tensor(flat[2], flat[1], edge_b[:, :], flat[0], ALU.add, ALU.add)\
                    .then_inc(edge_ready.sem, 1)

            def k1(m, n):
                spread_k1(dve, nc.vector, m, range(K1_ON_POOL, ND * DC)).then_inc(k1_spread.sem, 1)

            mx_v = mx1[:, :, :].rearrange("p a h -> p (a h)")
            sum_v = sum1[:, :, :].rearrange("p a h -> p (a h)")

            def score1_bias(m, t):
                wait(dve, scores1, m, t + 1)
                wait(dve, edge_ready, m, 1)
                wait(dve, probs1, m, t + 1 - TILES)
                for direction in range(ND):
                    last = nc.vector.tensor_tensor(
                        e1[t][:, direction, :, :], s1_ps[direction][:, 0:H * NKV].rearrange("p (h k) -> p h k", k=NKV),
                        edge_bias[:, t, direction * NKV:(direction + 1) * NKV].unsqueeze(1).to_broadcast([P, H, NKV]),
                        ALU.add)
                last.then_inc(biased1.sem, 1)

            def score1_max(m, t):
                wait(dve, biased1, m, t + 1)
                wait(dve, shifted1, m, t)
                nc.vector.tensor_reduce(mx_v, e1[t].rearrange("p a h k -> p (a h) k"), AX.X, ALU.max)\
                    .then_inc(maxima1.sem, 1)

            def score1(m, t):
                e_v = e1[t].rearrange("p a h k -> p (a h) k")
                wait(dve, maxima1, m, t + 1)
                nc.vector.tensor_tensor(e_v, e_v, mx_v.unsqueeze(2).to_broadcast([P, ND * H, NKV]), ALU.subtract)\
                    .then_inc(shifted1.sem, 1)

            def soft1(m, t):
                wait(dve, exps1, m, t + 1)
                wait(dve, inverses1, m, t)
                nc.vector.tensor_reduce(sum_v, e1[t].rearrange("p a h k -> p (a h) k"), AX.X, ALU.add).then_inc(sums1.sem, 1)

            def soft1_inverse(m, t):
                wait(dve, sums1, m, t + 1)
                nc.vector.reciprocal(inv1[t][:, :, :].rearrange("p a h -> p (a h)"), sum_v).then_inc(inverses1.sem, 1)

            def mix1(m, t):
                wait(dve, mixed1, m, t + 1)
                for c in range(DC):
                    last = nc.vector.scalar_tensor_tensor(sf[:, c, t * P:(t + 1) * P], ao1_ps[:, 0, c * P:(c + 1) * P],
                                                          bout[:, c:c + 1], sf[:, c, t * P:(t + 1) * P], ALU.add, ALU.add)
                last.then_inc(summed1.sem, 1)

            def out(m, n):
                wait(dve, summed1, m, TILES)
                nc.vector.scalar_tensor_tensor(sf[:, :, :], sf[:, :, :], 0.0, x2[:, :, :], ALU.max, ALU.add)\
                    .then_inc(relu_done.sem, 1)

            run_steps(dve, "DVE", {
                "norm0_mean": norm_mean(0), "norm1_mean": norm_mean(1), "norm0_apply": norm_apply(0),
                "norm1_apply": norm_apply(1), "qkv": qkv, "rope_scale": rope_scale,
                "rope": rope, "score_max": score_max, "score": score, "soft_inverse": soft_inverse, "norm0_scale": norm_scale(0),
                "norm1_scale": norm_scale(1), "norm0_shift": norm_shift(0), "norm1_shift": norm_shift(1), "soft": soft, "mix": mix, "proj": proj,
                "mlp_up": mlp_up, "mlp_down": mlp_down, "row_mask": row_mask, "self": self_feat, "edges": edges,
                "k1": k1, "score1_bias": score1_bias, "score1_max": score1_max, "score1": score1, "soft1_inverse": soft1_inverse,
                "edge_masks": edge_masks, "soft1": soft1, "mix1": mix1, "out": out,
            })

        @block.gpsimd
        def _(pool):
            pool.wait_ge(zeros_set.sem, 6)
            pool.wait_ge(table_step.sem, 9)
            pool.wait_ge(mods_set.sem, NMOD + DC)

            def low_part(out, full, hi):
                return nc.gpsimd.tensor_tensor(out, full, hi.bitcast(F32), ALU.subtract)

            def norm_apply(norm):
                def step(m, n):
                    wait(pool, normed_hi[norm], m, 1)
                    low_part(nl[norm][:, :, :], xn[norm][:, :, :], nh[norm][:, :, :])\
                        .then_inc(normed_lo[norm].sem, 1)
                return step

            def rope(m, t):
                wait(pool, qk_kept, m, t + 1)
                wait(pool, rotated, m, 2 * t)
                nc.gpsimd.tensor_tensor(qc[:, :, :, :], qk[:, t, :, :, :],
                                        cosw[:, :, :].unsqueeze(2).to_broadcast([P, 2, H, DH]), ALU.mult)\
                    .then_inc(cos_part.sem, 1)

            def heads(m, t):
                wait(pool, kT_kept, m, t + 1)
                wait(pool, scores, m, t + 1 - TILES)
                nc.gpsimd.tensor_tensor(kbd[:, t, :, :, :], kT[:, :, :].unsqueeze(2).to_broadcast([P, NG, 4, S]),
                                        hmask4[:, :].unsqueeze(1).unsqueeze(3).to_broadcast([P, NG, 4, S]), ALU.mult)\
                    .then_inc(k_spread.sem, 1)

            def soft(m, t):
                wait(pool, inv_sums, m, t + 1)
                nc.gpsimd.tensor_tensor(e0[t][:, :, :], e0[t][:, :, :],
                                        inv0[t][:, :].unsqueeze(2).to_broadcast([P, H, S]), ALU.mult)\
                    .then_inc(probs.sem, 1)

            def mlp_up(m, n):
                wait(pool, g_hi, m, n + 1)
                low_part(gl[:, 2 * n:2 * n + 2, :], gf[:, :, :], gh[:, 2 * n:2 * n + 2, :]).then_inc(g_lo.sem, 1)

            def proj(m, n):
                wait(pool, proj_gated, m, DC)
                wait(pool, x_res_s, m, 16)
                nc.gpsimd.tensor_tensor(x1[:, :, :], x1[:, :, :], x_res[:, :, :], ALU.add).then_inc(x1_done.sem, 1)

            def mlp_down(m, n):
                wait(pool, down_gated, m, 1)
                nc.gpsimd.tensor_tensor(x2[:, :, :], x2[:, :, :], x1[:, :, :], ALU.add).then_inc(x2_done.sem, 1)

            def self_feat(m, n):
                wait(pool, row_gate, m, 1)
                wait_last(pool, out_s, m)
                nc.gpsimd.tensor_tensor(by_seq(sf[:, :, :]),
                                        gate[:, :].rearrange("p (b s) -> p b s", s=S).unsqueeze(1).to_broadcast([P, DC, MB, S]),
                                        per_seq(mod[1][:, COND:COND + DC, :]), ALU.mult).then_inc(cond_part.sem, 1)

            def k1(m, n):
                spread_k1(pool, nc.gpsimd, m, range(K1_ON_POOL)).then_inc(k1_spread_pool.sem, 1)

            def x2_split(m, n):
                wait(pool, x2_hi, m, 1)
                low_part(nl[1][:, :, :], x2[:, :, :], nh[1][:, :, :]).then_inc(x2_lo.sem, 1)

            def self_split(m, n):
                wait(pool, self_hi, m, 1)
                low_part(nl[1][:, :, :], sf[:, :, :], nh[1][:, :, :]).then_inc(self_lo.sem, 1)

            def soft1(m, t):
                wait(pool, inverses1, m, t + 1)
                wait(pool, pT1_ps, m, 2 * t)
                for direction in range(ND):
                    last = nc.gpsimd.tensor_tensor(
                        p1[:, :, direction, :, 0:NKV], e1[t][:, direction, :, :].rearrange("p (j h) k -> p j h k", h=2),
                        inv1[t][:, direction, :].rearrange("p (j h) -> p j h", h=2).unsqueeze(3).to_broadcast([P, NJ, 2, NKV]),
                        ALU.mult)
                last.then_inc(probs1.sem, 1)

            run_steps(pool, "Pool", {
                "norm0_apply": norm_apply(0), "norm1_apply": norm_apply(1), "rope": rope, "heads": heads,
                "soft": soft, "proj": proj, "mlp_up": mlp_up, "mlp_down": mlp_down, "self": self_feat,
                "k1": k1, "x2_split": x2_split, "self_split": self_split, "soft1": soft1,
            })


def kernel(**inputs):
    import numpy as np

    from concourse import bacc
    from concourse.bass_utils import run_bass_kernel_spmd

    a = {k: np.asarray(v) for k, v in inputs.items()}

    def col(v):
        return v.reshape(-1, P).T

    def padded(v, axis):
        pad = [(0, 0), (0, 0)]
        pad[axis] = (0, MC * P - HM)
        return np.pad(v, pad)

    def rows(v):
        return np.broadcast_to(v, (P, *v.shape))

    adj = a["mask_BxSxSx11_ik0"]
    part = np.arange(P)
    arrays = {
        "xT": a["x"].reshape(B * S, D).T,
        "condT": a["cond_1024"].T,
        "pos": np.tile(a["pos_S"], 2).reshape(P, 1),
        "adj": np.stack([adj[:, :, :NKV], adj[:, :NKV].transpose(0, 2, 1, 3)], 2).reshape(B * S, NE * NL),
        "adaln": a["L0_cond_adaln_w"], "qkv": a["L0_cond_qkv_w"], "proj": a["L0_cond_proj_w"],
        "w1": padded(a["L0_cond_w1_w"], 1), "w3": padded(a["L0_cond_w3_w"], 1), "w2": padded(a["L0_cond_w2_w"], 0),
        "self": a["L1_cond_W_self"].T[:D], "self_cond": a["L1_cond_W_self"].T[D:],
        "q1": np.concatenate([w.T for w in a["L1_cond_Wq"]], 1),
        "k1": np.concatenate([w.T for w in a["L1_cond_Wk"]], 1),
        "out1": np.concatenate([w.reshape(D, D).T for w in a["L1_cond_Wout"]], 1),
        "colb": np.concatenate([col(a[k]) for k in ("L0_cond_adaln_b", "L0_cond_proj_b", "L1_cond_b_self",
                                                    "L1_cond_bq", "L1_cond_bk", "L1_cond_bout")], 1),
        "lnw": rows(np.stack([a["L0_cond_lnq_w"], a["L0_cond_lnk_w"]])),
        "edge_w": rows(a["L1_cond_w_bias"]), "edge_b": rows(a["L1_cond_b_bias"].reshape(1)),
        "ident": np.eye(P, dtype=np.float32),
        "mean_col": np.full((P, 1), 1.0 / D, np.float32),
        "hmask4": (part[:, None] % 64 // DH == np.arange(4)).astype(np.float32),
        "hmask8": (part[:, None] // DH == np.arange(8)).astype(np.float32),
        "seq_ind": (part[:, None] // S == np.arange(2)).astype(np.float32),
        "freq": np.broadcast_to((1.0 / 10000.0 ** (np.arange(DH // 2, dtype=np.float32) / (DH // 2)))
                                .astype(np.float32), (P, DH // 2)),
    }
    arrays = {k: np.ascontiguousarray(v) for k, v in arrays.items()}
    nc = bacc.Bacc("TRN2", target_bir_lowering=False, num_devices=1)
    d = {k: nc.dram_tensor(f"in_{k}", v.shape, mybir.dt.from_np(v.dtype), kind="ExternalInput").ap()
         for k, v in arrays.items()}
    d["outT"] = nc.dram_tensor("out_T", (D, B * S), F32, kind="ExternalOutput").ap()
    build_program(nc, d)
    r = run_bass_kernel_spmd(nc, [{f"in_{k}": v for k, v in arrays.items()}], core_ids=[0])
    return r.results[0]["out_T"].T.reshape(B, S, D)
```
